# Optimizing a Trainium2 kernel written in Bass

```python
import numpy as np
import jax
import jax.numpy as jnp

def _softmax(x, axis=-1):
    return jax.nn.softmax(x, axis=axis)

def _gelu(x):
    return jax.nn.gelu(x, approximate=True)

def _silu(x):
    return jax.nn.silu(x)

def _sigmoid(x):
    return jax.nn.sigmoid(x)

def _layernorm(x, axis=-1, eps=1e-05):
    m = jnp.mean(x, axis=axis, keepdims=True)
    v = jnp.var(x, axis=axis, keepdims=True)
    return (x - m) / jnp.sqrt(v + eps)

def _scatter_add(tgt, idx, src, axis=0):
    return tgt.at[idx].add(src)

def _segment_sum(src, seg, n):
    return jax.ops.segment_sum(src, seg, n)
kernel_name = 'mk_sandwich_d2_jaxref_r4_e142e5'

def setup_inputs(seed: int=0):
    np.random.seed(seed)
    _w = jnp.asarray

    def _L0_attn_setup():
        import jax, jax.numpy as jnp
        import numpy as np
        B, L, D, P = (4, 1024, 256, 64)
        EPS = 1e-08

        def _feature_map(x):
            return jax.nn.elu(x) + 1.0
        key = jax.random.key(seed)
        kx, kq, kk, kv, kp = jax.random.split(key, 5)
        x = jax.random.normal(kx, (B, L, D), dtype=jnp.float32)
        scale = 1.0 / np.sqrt(D)
        Wq = jax.random.uniform(kq, (D, D), jnp.float32, -scale, scale)
        Wk = jax.random.uniform(kk, (D, D), jnp.float32, -scale, scale)
        Wv = jax.random.uniform(kv, (D, D), jnp.float32, -scale, scale)
        g = jax.random.normal(kp, (D, P), dtype=jnp.float32)
        proj, _ = jnp.linalg.qr(g, mode='reduced')
        return {'x': x, 'Wq': Wq, 'Wk': Wk, 'Wv': Wv, 'proj': proj}
    _L0_attn_in = _L0_attn_setup()

    def _L0_ffn_setup():
        import jax, jax.numpy as jnp
        import numpy as np
        B, S, D = (1, 512, 256)
        E, K, F = (8, 2, 352)
        NS = 2
        SCALE = 2.5

        def _swiglu_mlp(x, wg, wu, wd):
            return jax.nn.silu(x @ wg) * (x @ wu) @ wd
        key = jax.random.key(seed)
        ks = jax.random.split(key, 8)
        s = 0.02
        return {'hidden_states': jax.random.normal(ks[0], (B, S, D), jnp.float32), 'gate_w': jax.random.normal(ks[1], (E, D), jnp.float32) * s, 'w_gate': jax.random.normal(ks[2], (E, D, F), jnp.float32) * s, 'w_up': jax.random.normal(ks[3], (E, D, F), jnp.float32) * s, 'w_down': jax.random.normal(ks[4], (E, F, D), jnp.float32) * s, 'sw_gate': jax.random.normal(ks[5], (D, F * NS), jnp.float32) * s, 'sw_up': jax.random.normal(ks[6], (D, F * NS), jnp.float32) * s, 'sw_down': jax.random.normal(ks[7], (F * NS, D), jnp.float32) * s}
    _L0_ffn_in = _L0_ffn_setup()

    def _L1_attn_setup():
        import jax, jax.numpy as jnp
        import numpy as np
        import math
        D_MODEL = 256
        D_K = 64
        D_V = 64
        N_HEADS = 16
        key = jax.random.key(seed)
        ks = jax.random.split(key, 5)
        std = 1.0 / math.sqrt(D_MODEL)
        x = jax.random.normal(ks[0], (2, 512, D_MODEL), dtype=jnp.float32)
        Wq = jax.random.normal(ks[1], (D_MODEL, N_HEADS * D_K), dtype=jnp.float32) * std
        Wk = jax.random.normal(ks[2], (D_MODEL, N_HEADS * D_K), dtype=jnp.float32) * std
        Wv = jax.random.normal(ks[3], (D_MODEL, N_HEADS * D_V), dtype=jnp.float32) * std
        Wo = jax.random.normal(ks[4], (N_HEADS * D_V, D_MODEL), dtype=jnp.float32) * std
        return {'x': x, 'Wq': Wq, 'Wk': Wk, 'Wv': Wv, 'Wo': Wo}
    _L1_attn_in = _L1_attn_setup()

    def _L1_ffn_setup():
        import jax, jax.numpy as jnp
        import numpy as np
        import math
        B, T, D, H, E, TOPK, CAPF = (4, 512, 256, 16, 8, 2, 2.0)
        HD = D // H

        def layernorm(x, g, b, eps=1e-05):
            m = jnp.mean(x, -1, keepdims=True)
            v = jnp.mean(jnp.square(x - m), -1, keepdims=True)
            return (x - m) * jax.lax.rsqrt(v + eps) * g + b

        def block_forward(x, ln1_g, ln1_b, Wqkv, Wproj, ln2_g, ln2_b, Wgate, W1, b1, W2, b2):
            Bb, Tt, d = x.shape
            hd = HD
            half = hd // 2
            h = layernorm(x, ln1_g, ln1_b)
            qkv = (h @ Wqkv).reshape(Bb, Tt, H, 3 * hd)
            q, k, v = (qkv[..., :hd], qkv[..., hd:2 * hd], qkv[..., 2 * hd:])
            inv_freq = 1.0 / 10000.0 ** (jnp.arange(0, hd, 2, dtype=jnp.float32) / hd)
            ang = jnp.arange(Tt, dtype=jnp.float32)[:, None] * inv_freq
            sin = jnp.sin(ang)[None, :, None, :].astype(x.dtype)
            cos = jnp.cos(ang)[None, :, None, :].astype(x.dtype)

            def rope(t):
                t1, t2 = (t[..., :half], t[..., half:])
                return jnp.concatenate([t1 * cos - t2 * sin, t1 * sin + t2 * cos], -1)
            q, k = (rope(q), rope(k))
            scores = jnp.einsum('bqhd,bkhd->bhqk', q, k) / math.sqrt(hd)
            causal = jnp.tril(jnp.ones((Tt, Tt), dtype=bool))
            scores = jnp.where(causal, scores, jnp.asarray(-1000000000.0, scores.dtype))
            probs = jax.nn.softmax(scores, axis=-1)
            attn = jnp.einsum('bhqk,bkhd->bqhd', probs, v).reshape(Bb, Tt, d) @ Wproj
            x = x + attn
            h2 = layernorm(x, ln2_g, ln2_b)
            flat = h2.reshape(-1, d)
            N = flat.shape[0]
            capacity = int(math.ceil(CAPF * N / E))
            gates = jax.nn.softmax((flat @ Wgate).astype(jnp.float32), -1).astype(flat.dtype)
            _, top_inds = jax.lax.top_k(gates, TOPK)
            mask = jnp.zeros((N, E), dtype=bool).at[jnp.arange(N)[:, None], top_inds].set(True)
            pos = jnp.cumsum(mask.astype(jnp.int32), axis=0) * mask - 1
            keep = (pos < capacity) & mask
            t_flat = jnp.repeat(jnp.arange(N), TOPK)
            e_flat = top_inds.reshape(-1)
            p = pos[t_flat, e_flat]
            kp = keep[t_flat, e_flat]
            p_eff = jnp.where(kp, p, capacity)
            exp_in = jnp.zeros((E, capacity, d), flat.dtype).at[e_flat, p_eff].set(flat[t_flat], mode='drop')
            hmid = jax.nn.gelu(jnp.einsum('ecd,edf->ecf', exp_in, W1) + b1[:, None, :], approximate=False)
            exp_out = jnp.einsum('ecf,efd->ecd', hmid, W2) + b2[:, None, :]
            gate = gates[t_flat, e_flat] * kp.astype(flat.dtype)
            p_g = jnp.minimum(p_eff, capacity - 1)
            moe = jnp.zeros((N, d), flat.dtype).at[t_flat].add(exp_out[e_flat, p_g] * gate[:, None])
            return x + moe.reshape(Bb, Tt, d)
        key = jax.random.key(seed)
        ks = jax.random.split(key, 8)
        s = 0.02
        return {'x': jax.random.normal(ks[0], (B, T, D), jnp.float32), 'ln1_g': jnp.ones((D,), jnp.float32), 'ln1_b': jnp.zeros((D,), jnp.float32), 'Wqkv': jax.random.normal(ks[1], (D, 3 * D), jnp.float32) * s, 'Wproj': jax.random.normal(ks[2], (D, D), jnp.float32) * s, 'ln2_g': jnp.ones((D,), jnp.float32), 'ln2_b': jnp.zeros((D,), jnp.float32), 'Wgate': jax.random.normal(ks[3], (D, E), jnp.float32) * s, 'W1': jax.random.normal(ks[4], (E, D, 4 * D), jnp.float32) * s, 'b1': jnp.zeros((E, 4 * D), jnp.float32), 'W2': jax.random.normal(ks[5], (E, 4 * D, D), jnp.float32) * s, 'b2': jnp.zeros((E, D), jnp.float32)}
    _L1_ffn_in = _L1_ffn_setup()
    _d = {'L0_attn_x': _L0_attn_in['x'], 'L0_attn_Wq': _L0_attn_in['Wq'], 'L0_attn_Wk': _L0_attn_in['Wk'], 'L0_attn_Wv': _L0_attn_in['Wv'], 'L0_attn_proj': _L0_attn_in['proj'], 'L0_ffn_gate_w': _L0_ffn_in['gate_w'], 'L0_ffn_w_gate': _L0_ffn_in['w_gate'], 'L0_ffn_w_up': _L0_ffn_in['w_up'], 'L0_ffn_w_down': _L0_ffn_in['w_down'], 'L0_ffn_sw_gate': _L0_ffn_in['sw_gate'], 'L0_ffn_sw_up': _L0_ffn_in['sw_up'], 'L0_ffn_sw_down': _L0_ffn_in['sw_down'], 'L1_attn_Wq': _L1_attn_in['Wq'], 'L1_attn_Wk': _L1_attn_in['Wk'], 'L1_attn_Wv': _L1_attn_in['Wv'], 'L1_attn_Wo': _L1_attn_in['Wo'], 'L1_ffn_ln1_g': _L1_ffn_in['ln1_g'], 'L1_ffn_ln1_b': _L1_ffn_in['ln1_b'], 'L1_ffn_Wqkv': _L1_ffn_in['Wqkv'], 'L1_ffn_Wproj': _L1_ffn_in['Wproj'], 'L1_ffn_ln2_g': _L1_ffn_in['ln2_g'], 'L1_ffn_ln2_b': _L1_ffn_in['ln2_b'], 'L1_ffn_Wgate': _L1_ffn_in['Wgate'], 'L1_ffn_W1': _L1_ffn_in['W1'], 'L1_ffn_b1': _L1_ffn_in['b1'], 'L1_ffn_W2': _L1_ffn_in['W2'], 'L1_ffn_b2': _L1_ffn_in['b2']}
    _x0 = _d['L0_attn_x']
    _d['L0_attn_x'] = jax.random.normal(jax.random.fold_in(jax.random.key(seed), 1), (4, 1024, 256), dtype=_x0.dtype)
    del _x0
    return _d

def reference(L0_attn_x, L0_attn_Wq, L0_attn_Wk, L0_attn_Wv, L0_attn_proj, L0_ffn_gate_w, L0_ffn_w_gate, L0_ffn_w_up, L0_ffn_w_down, L0_ffn_sw_gate, L0_ffn_sw_up, L0_ffn_sw_down, L1_attn_Wq, L1_attn_Wk, L1_attn_Wv, L1_attn_Wo, L1_ffn_ln1_g, L1_ffn_ln1_b, L1_ffn_Wqkv, L1_ffn_Wproj, L1_ffn_ln2_g, L1_ffn_ln2_b, L1_ffn_Wgate, L1_ffn_W1, L1_ffn_b1, L1_ffn_W2, L1_ffn_b2):

    def _L0_attn_ref(x, Wq, Wk, Wv, proj):
        import jax, jax.numpy as jnp
        import numpy as np
        B, L, D, P = (4, 1024, 256, 64)
        EPS = 1e-08

        def _feature_map(x):
            return jax.nn.elu(x) + 1.0
        q = jnp.einsum('bld,ed->ble', x, Wq)
        k = jnp.einsum('bld,ed->ble', x, Wk)
        v = jnp.einsum('bld,ed->ble', x, Wv)
        q_prime = _feature_map(q @ proj)
        k_prime = _feature_map(k @ proj)
        kv = jnp.einsum('blp,bld->bpd', k_prime, v)
        num = jnp.einsum('blp,bpd->bld', q_prime, kv)
        z = 1.0 / (jnp.sum(q_prime, axis=-1, keepdims=True) + EPS)
        return num * z

    def _L0_ffn_ref(hidden_states, gate_w, w_gate, w_up, w_down, sw_gate, sw_up, sw_down):
        import jax, jax.numpy as jnp
        import numpy as np
        B, S, D = (1, 512, 256)
        E, K, F = (8, 2, 352)
        NS = 2
        SCALE = 2.5

        def _swiglu_mlp(x, wg, wu, wd):
            return jax.nn.silu(x @ wg) * (x @ wu) @ wd
        identity = hidden_states
        x = hidden_states.reshape(-1, hidden_states.shape[-1])
        T = x.shape[0]
        logits = x.astype(jnp.float32) @ gate_w.astype(jnp.float32).T
        scores = jax.nn.softmax(logits, axis=-1)
        topk_w, topk_i = jax.lax.top_k(scores, K)
        topk_w = topk_w / (topk_w.sum(-1, keepdims=True) + 1e-20) * SCALE
        combine = jnp.zeros((T, E), jnp.float32).at[jnp.arange(T)[:, None], topk_i].set(topk_w)
        g = jax.nn.silu(jnp.einsum('td,edf->etf', x, w_gate)) * jnp.einsum('td,edf->etf', x, w_up)
        expert_out = jnp.einsum('etf,efd->etd', g, w_down)
        y = jnp.einsum('te,etd->td', combine, expert_out).astype(x.dtype)
        y = y.reshape(identity.shape)
        return y + _swiglu_mlp(identity, sw_gate, sw_up, sw_down)

    def _L1_attn_ref(x, Wq, Wk, Wv, Wo):
        import jax, jax.numpy as jnp
        import numpy as np
        import math
        D_MODEL = 256
        D_K = 64
        D_V = 64
        N_HEADS = 16
        B, S, D = x.shape
        H, dk, dv = (N_HEADS, D_K, D_V)
        q = (x @ Wq).reshape(B, S, H, dk)
        k = (x @ Wk).reshape(B, S, H, dk)
        v = (x @ Wv).reshape(B, S, H, dv)
        scores = jnp.einsum('bqhd,bkhd->bhqk', q / math.sqrt(dk), k)
        causal = jnp.tril(jnp.ones((S, S), dtype=bool))
        scores = scores + jnp.where(causal, 0.0, -jnp.inf).astype(scores.dtype)
        attn = jax.nn.softmax(scores, axis=-1)
        out = jnp.einsum('bhqk,bkhd->bqhd', attn, v).reshape(B, S, H * dv)
        return x + out @ Wo

    def _L1_ffn_ref(x, ln1_g, ln1_b, Wqkv, Wproj, ln2_g, ln2_b, Wgate, W1, b1, W2, b2):
        import jax, jax.numpy as jnp
        import numpy as np
        import math
        B, T, D, H, E, TOPK, CAPF = (4, 512, 256, 16, 8, 2, 2.0)
        HD = D // H

        def layernorm(x, g, b, eps=1e-05):
            m = jnp.mean(x, -1, keepdims=True)
            v = jnp.mean(jnp.square(x - m), -1, keepdims=True)
            return (x - m) * jax.lax.rsqrt(v + eps) * g + b

        def block_forward(x, ln1_g, ln1_b, Wqkv, Wproj, ln2_g, ln2_b, Wgate, W1, b1, W2, b2):
            Bb, Tt, d = x.shape
            hd = HD
            half = hd // 2
            h = layernorm(x, ln1_g, ln1_b)
            qkv = (h @ Wqkv).reshape(Bb, Tt, H, 3 * hd)
            q, k, v = (qkv[..., :hd], qkv[..., hd:2 * hd], qkv[..., 2 * hd:])
            inv_freq = 1.0 / 10000.0 ** (jnp.arange(0, hd, 2, dtype=jnp.float32) / hd)
            ang = jnp.arange(Tt, dtype=jnp.float32)[:, None] * inv_freq
            sin = jnp.sin(ang)[None, :, None, :].astype(x.dtype)
            cos = jnp.cos(ang)[None, :, None, :].astype(x.dtype)

            def rope(t):
                t1, t2 = (t[..., :half], t[..., half:])
                return jnp.concatenate([t1 * cos - t2 * sin, t1 * sin + t2 * cos], -1)
            q, k = (rope(q), rope(k))
            scores = jnp.einsum('bqhd,bkhd->bhqk', q, k) / math.sqrt(hd)
            causal = jnp.tril(jnp.ones((Tt, Tt), dtype=bool))
            scores = jnp.where(causal, scores, jnp.asarray(-1000000000.0, scores.dtype))
            probs = jax.nn.softmax(scores, axis=-1)
            attn = jnp.einsum('bhqk,bkhd->bqhd', probs, v).reshape(Bb, Tt, d) @ Wproj
            x = x + attn
            h2 = layernorm(x, ln2_g, ln2_b)
            flat = h2.reshape(-1, d)
            N = flat.shape[0]
            capacity = int(math.ceil(CAPF * N / E))
            gates = jax.nn.softmax((flat @ Wgate).astype(jnp.float32), -1).astype(flat.dtype)
            _, top_inds = jax.lax.top_k(gates, TOPK)
            mask = jnp.zeros((N, E), dtype=bool).at[jnp.arange(N)[:, None], top_inds].set(True)
            pos = jnp.cumsum(mask.astype(jnp.int32), axis=0) * mask - 1
            keep = (pos < capacity) & mask
            t_flat = jnp.repeat(jnp.arange(N), TOPK)
            e_flat = top_inds.reshape(-1)
            p = pos[t_flat, e_flat]
            kp = keep[t_flat, e_flat]
            p_eff = jnp.where(kp, p, capacity)
            exp_in = jnp.zeros((E, capacity, d), flat.dtype).at[e_flat, p_eff].set(flat[t_flat], mode='drop')
            hmid = jax.nn.gelu(jnp.einsum('ecd,edf->ecf', exp_in, W1) + b1[:, None, :], approximate=False)
            exp_out = jnp.einsum('ecf,efd->ecd', hmid, W2) + b2[:, None, :]
            gate = gates[t_flat, e_flat] * kp.astype(flat.dtype)
            p_g = jnp.minimum(p_eff, capacity - 1)
            moe = jnp.zeros((N, d), flat.dtype).at[t_flat].add(exp_out[e_flat, p_g] * gate[:, None])
            return x + moe.reshape(Bb, Tt, d)
        return block_forward(x, ln1_g, ln1_b, Wqkv, Wproj, ln2_g, ln2_b, Wgate, W1, b1, W2, b2)
    x = L0_attn_x
    x = x + _layernorm(_L0_attn_ref(_layernorm(x, axis=-1), L0_attn_Wq, L0_attn_Wk, L0_attn_Wv, L0_attn_proj), axis=-1)
    x = x + _layernorm(_L0_ffn_ref(_layernorm(x, axis=-1), L0_ffn_gate_w, L0_ffn_w_gate, L0_ffn_w_up, L0_ffn_w_down, L0_ffn_sw_gate, L0_ffn_sw_up, L0_ffn_sw_down), axis=-1)
    x = x + _layernorm(_L1_attn_ref(_layernorm(x, axis=-1), L1_attn_Wq, L1_attn_Wk, L1_attn_Wv, L1_attn_Wo), axis=-1)
    x = x + _layernorm(_L1_ffn_ref(_layernorm(x, axis=-1), L1_ffn_ln1_g, L1_ffn_ln1_b, L1_ffn_Wqkv, L1_ffn_Wproj, L1_ffn_ln2_g, L1_ffn_ln2_b, L1_ffn_Wgate, L1_ffn_W1, L1_ffn_b1, L1_ffn_W2, L1_ffn_b2), axis=-1)
    return x

_drawn_inputs = setup_inputs


def setup_inputs(seed=0):
    import zlib

    import numpy as np

    out = dict(_drawn_inputs(seed))
    spreads = {'L1_ffn_ln1_g': (1.0, 0.6),
     'L1_ffn_ln1_b': (0.0, 0.8),
     'L1_ffn_ln2_g': (1.0, 0.6),
     'L1_ffn_ln2_b': (0.0, 0.8),
     'L1_ffn_b1': (0.0, 0.8),
     'L1_ffn_b2': (0.0, 2.0)}
    factors = {'L1_ffn_Wqkv': 2.965,
     'L1_ffn_Wproj': 2.766,
     'L1_ffn_Wgate': 5.891,
     'L1_ffn_W1': 7.66,
     'L1_ffn_W2': 7.17}
    for name, (base, spread) in spreads.items():
        noise = np.random.default_rng([zlib.crc32(name.encode()), seed]).standard_normal(out[name].shape)
        drawn = base * np.exp(spread * noise) if base else spread * noise
        out[name] = jnp.asarray(drawn.astype(out[name].dtype))
    for name, factor in factors.items():
        out[name] = (out[name] * factor).astype(out[name].dtype)
    return out
```

```python
from contextlib import ExitStack

import numpy as np

import concourse.bass as bass
from concourse import mybir

F32 = mybir.dt.float32
F32R = mybir.dt.float32r
BF16 = mybir.dt.bfloat16
I32 = mybir.dt.int32
U32 = mybir.dt.uint32
ALU = mybir.AluOpType
ACT = mybir.ActivationFunctionType
AX = mybir.AxisListType

P = 128
B, L, D = 4, 1024, 256
N = B * L
T = N // P
TB = L // P
KD = D // P
LN_EPS = 1e-5

PROJ = 64
ATT_EPS = 1e-8

E = 8
F0, FS = 352, 704
ROUTE_SCALE = 2.5
BLK0 = (2 * N + E * (P - 1)) // P

HA, DK = 16, 64
H1, HD = 16, 16
F1 = 4 * D
CAP = 2 * N // E


def tiles_of(rows):
    return rows.rearrange("(t p) w -> p t w", p=P)


def spread(ap, n):
    return ap.unsqueeze(2).broadcast_to([ap.shape[0], ap.shape[1], n])


class Chain:

    def __init__(self, engine, sem):
        self.engine, self.sem, self.n = engine, sem, 0

    def step(self, instruction):
        self.n += 1
        instruction.then_inc(self.sem, 1)
        self.engine.wait_ge(self.sem, self.n)


def row_stats(dve, link, st, mean, var, tmp):
    link(dve.tensor_tensor(tmp, st[:, :, 1], st[:, :, 4], ALU.subtract))
    link(dve.tensor_tensor(tmp, tmp, tmp, ALU.mult))
    link(dve.tensor_tensor(mean, st[:, :, 1], st[:, :, 4], ALU.add))
    link(dve.tensor_scalar(mean, mean, 0.5, None, ALU.mult))
    link(dve.tensor_tensor(var, st[:, :, 2], st[:, :, 5], ALU.add))
    link(dve.tensor_scalar(var, var, 1.0 / D, None, ALU.mult))
    link(dve.scalar_tensor_tensor(out=var, in0=tmp, scalar=0.25, in1=var, op0=ALU.mult, op1=ALU.add))


def refine_rstd(dve, link, rstd, root, var_eps, tmp):
    link(dve.reciprocal(rstd, root))
    link(dve.tensor_tensor(tmp, rstd, rstd, ALU.mult))
    link(dve.tensor_tensor(tmp, tmp, var_eps, ALU.mult))
    link(dve.tensor_scalar(tmp, tmp, -0.5, 1.5, ALU.mult, ALU.add))
    link(dve.tensor_tensor(rstd, rstd, tmp, ALU.mult))


def norm_phase(nc, tag, x, ident, y=None, ysum=None, x_src=None, residual=True, xn=None, xT_sb=None,
               xT_dram=None, twice=False, gain=None, out_dst=None, x_save=None, x_load=None, zero=None):
    last = out_dst is not None
    first = y is not None and residual
    src = x if residual else y
    ZEROS = 8
    with ExitStack() as ctx:
        def sb(name, shape, dt=F32):
            return ctx.enter_context(nc.sbuf_tensor(f"{tag}_{name}", shape, dt))

        def sem(name):
            return ctx.enter_context(nc.semaphore(f"{tag}_{name}"))

        st = sb("st", [P, T, 6])
        mean, var, root, rstd, rstd2, tmp, z = (
            sb(n, [P, T]) for n in ("mean", "var", "root", "rstd", "rstd2", "tmp", "z"))
        ring = sb("ring", [P, 2, 2, D])
        ot = sb("ot", [P, 2, KD, 2 * P]) if xT_dram is not None else None
        tp = [ctx.enter_context(nc.psum_tensor(f"{tag}_tp{i}", [P, KD, 2 * P], F32)) for i in range(2)]
        x_in, chain, var_ok, root_ok, stats_ok, applied, added, tile_ok, turned, moved, saved, cleared, seen = (
            sem(n) for n in ("x_in", "chain", "var_ok", "root_ok", "stats_ok", "applied", "added", "tile_ok",
                             "turned", "moved", "saved", "cleared", "seen"))
        stored = [sem(f"stored{i}") for i in range(2)]
        block = ctx.enter_context(nc.Block())
        n_roots = int(first) + (0 if last else 1) + int(twice)

        @block.sync
        def _(sp):
            if x_src is not None:
                sp.dma_start(x[:, :, :], tiles_of(x_src)).then_inc(x_in, 16)
            if zero is not None:
                zeros, rows = zero
                n_rows = rows.shape[0] // P
                for c in range(ZEROS):
                    a, z_end = n_rows * c // ZEROS, n_rows * (c + 1) // ZEROS
                    sp.dma_start(tiles_of(rows)[:, a:z_end, :],
                                 zeros[:, :].unsqueeze(1).broadcast_to([P, z_end - a, D])).then_inc(cleared, 16)
            if x_load is not None:
                sp.dma_start(x[:, :, :], tiles_of(x_load)).then_inc(x_in, 16)
            if x_save is not None:
                sp.wait_ge(added, T)
                sp.dma_start(tiles_of(x_save), x[:, :, :]).then_inc(saved, 16)
                sp.wait_ge(saved, 16)
            if xT_dram is not None:
                for q in stored:
                    sp.sem_inc(q, 16)
                with sp.Fori(0, T // 4) as i:
                    for u in range(2):
                        s = i * 2 + u
                        sp.wait_ge(moved, s + 3)
                        sp.dma_start(xT_dram[:, :, bass.ds(s * 2 * P, 2 * P)], ot[:, u, :, :]).then_inc(stored[u], 16)
                for q in stored:
                    sp.wait_ge(q, 16 + 16 * (T // 4))
            if last:
                for c in range(4):
                    sp.wait_ge(added, T // 4 * (c + 1))
                    sp.dma_start(tiles_of(out_dst)[:, T // 4 * c:T // 4 * (c + 1), :],
                                 x[:, T // 4 * c:T // 4 * (c + 1), :]).then_inc(saved, 16)
                sp.wait_ge(saved, 64)
            if zero is not None:
                sp.wait_ge(cleared, 16 * ZEROS)

        @block.vector
        def _(dve):
            link = Chain(dve, chain).step
            rounds = [0, 0]

            def stats(rows):
                with dve.Fori(0, T // 4) as i:
                    for u in range(4):
                        dve.bn_stats(st[:, i * 4 + u, :], rows[:, i * 4 + u, 0:D]).then_inc(stats_ok, 1)
                rounds[0] += 1
                dve.wait_ge(stats_ok, T * rounds[0])
                row_stats(dve, link, st, mean[:, :], var[:, :], tmp[:, :])

            def inverse_root(v, r):
                dve.tensor_scalar(v, v, LN_EPS, None, ALU.add).then_inc(var_ok, 1)
                rounds[1] += 1
                dve.wait_ge(var_ok, rounds[1])
                dve.wait_ge(root_ok, rounds[1])
                refine_rstd(dve, link, r, root[:, :], v, tmp[:, :])

            if x_src is not None or x_load is not None:
                dve.wait_ge(x_in, 16)
            if first:
                stats(y)
                if ysum is not None:
                    link(dve.tensor_scalar(z[:, :], ysum, ATT_EPS, None, ALU.add))
                    link(dve.reciprocal(z[:, :], z[:, :]))
                    link(dve.tensor_tensor(var[:, :], var[:, :], z[:, :], ALU.mult))
                    link(dve.tensor_tensor(var[:, :], var[:, :], z[:, :], ALU.mult))
                inverse_root(var[:, :], rstd[:, :])
                if ysum is not None:
                    link(dve.tensor_tensor(rstd[:, :], rstd[:, :], z[:, :], ALU.mult))
                with dve.Fori(0, T // 4) as i:
                    for u in range(4):
                        t = i * 4 + u
                        dve.tensor_scalar(y[:, t, 0:D], y[:, t, 0:D], mean[:, bass.ds(t, 1)],
                                          rstd[:, bass.ds(t, 1)], ALU.subtract, ALU.mult).then_inc(applied, 1)
                dve.wait_ge(applied, T)
                with dve.Fori(0, T // 4) as i:
                    for u in range(4):
                        t = i * 4 + u
                        dve.tensor_tensor(x[:, t, :], x[:, t, :], y[:, t, 0:D], ALU.add).then_inc(added, 1)
                dve.wait_ge(added, T)
            if last:
                return
            stats(src)
            inverse_root(var[:, :], rstd[:, :])
            if twice:
                link(dve.tensor_tensor(var[:, :], rstd[:, :], rstd[:, :], ALU.mult))
                link(dve.tensor_scalar(var[:, :], var[:, :], -LN_EPS, 1.0, ALU.mult, ALU.add))
                inverse_root(var[:, :], rstd2[:, :])
                link(dve.tensor_tensor(rstd2[:, :], rstd2[:, :], rstd[:, :], ALU.mult))
            for_turn = rstd2 if twice else rstd
            with dve.Fori(0, T // 4) as i:
                for u in range(2):
                    s = i * 2 + u
                    dve.wait_ge(turned, s + 1)
                    for v in range(2):
                        t = s * 2 + v
                        dve.tensor_scalar(ring[:, u, v, :], src[:, t, 0:D], mean[:, bass.ds(t, 1)],
                                          for_turn[:, bass.ds(t, 1)], ALU.subtract, ALU.mult).then_inc(tile_ok, 1)
                        dve.tensor_scalar(xn[:, t, :], src[:, t, 0:D], mean[:, bass.ds(t, 1)],
                                          rstd[:, bass.ds(t, 1)], ALU.subtract, ALU.mult)

        @block.scalar
        def _(act):
            if not last:
                act.sem_inc(moved, 2)
            for r in range(n_roots):
                act.wait_ge(var_ok, r + 1)
                act.activation(root[:, :], var[:, :], ACT.Sqrt).then_inc(root_ok, 1)
            if last:
                return
            with act.Fori(0, T // 4) as i:
                for u in range(2):
                    s = i * 2 + u
                    act.wait_ge(turned, s + 3)
                    if xT_dram is not None:
                        act.wait_ge(stored[u], 16 * (i + 1))
                    if gain is None:
                        dst = ot[:, u, :, :] if xT_dram is not None else xT_sb[:, :, bass.ds(s * 2 * P, 2 * P)]
                        act.activation(dst, tp[u][:, :, :], ACT.Copy).then_inc(moved, 1)
                    else:
                        act.sem_inc(seen, 1)
                        for k in range(KD):
                            m = act.activation(xT_sb[:, k, bass.ds(s * 2 * P, 2 * P)], tp[u][:, k, :], ACT.Identity,
                                               scale=gain[0][:, k:k + 1], bias=gain[1][:, k:k + 1])
                        m.then_inc(moved, 1)

        @block.tensor
        def _(pe):
            if last:
                return
            pe.sem_inc(turned, 2)
            with pe.Fori(0, T // 4) as i:
                for u in range(2):
                    s = i * 2 + u
                    pe.wait_ge(tile_ok, 2 * s + 2)
                    pe.wait_ge(moved, s + 1)
                    for k in range(KD):
                        for v in range(2):
                            m = pe.transpose(tp[u][:, k, v * P:(v + 1) * P], ring[:, u, v, k * P:(k + 1) * P],
                                             ident[:, :])
                    m.then_inc(turned, 1)


def setup_phase(nc, ident, zeros):
    with ExitStack() as ctx:
        made = ctx.enter_context(nc.semaphore("setup_made"))
        block = ctx.enter_context(nc.Block())

        @block.gpsimd
        def _(pool):
            pool.memset(zeros[:, :], 0.0)
            pool.memset(ident[:, :], 0.0).then_inc(made, 1)
            pool.wait_ge(made, 1)
            pool.affine_select(out=ident[:, :], in_=ident[:, :], compare_op=ALU.not_equal, fill=1.0, base=0,
                               pattern=[[-1, P]], channel_multiplier=1)


def layer0_attention(nc, w, xn, xT, y, ident):
    C = 512
    with ExitStack() as ctx:
        def sb(name, shape, dt=F32):
            return ctx.enter_context(nc.sbuf_tensor(f"a0_{name}", shape, dt))

        def ps(name, shape):
            return ctx.enter_context(nc.psum_tensor(f"a0_{name}", shape, F32))

        def sem(name):
            return ctx.enter_context(nc.semaphore(f"a0_{name}"))

        wq, wk, wv = (sb(n, [P, KD, D]) for n in ("wq", "wk", "wv"))
        proj = sb("proj", [P, KD, PROJ])
        map_w = sb("map_w", [P, KD, 2 * PROJ])
        wvT = sb("wvT", [P, KD, D])
        low = sb("low", [P, 2, C])
        fm = sb("fm", [P, 2, C])
        kt = sb("kt", [P, TB, PROJ])
        kx = sb("kx", [P, D])
        kxT = sb("kxT", [P, KD, PROJ])
        kv = sb("kv", [PROJ, D + 1])
        pre = [ps(f"pre{i}", [P, C]) for i in range(2)]
        turn = [ps(f"turn{i}", [P, 4, P]) for i in range(2)]
        small = ps("small", [P, 512])
        num = [ps(f"num{i}", [P, 512]) for i in range(2)]
        w_in, w_turned, w_ok, pre_ok, low_ok, exp_ok, fm_ok, turn_ok, kt_ok, mid, mid_ok, num_ok, y_ok, ones_ok = (
            sem(n) for n in ("w_in", "w_turned", "w_ok", "pre_ok", "low_ok", "exp_ok", "fm_ok", "turn_ok", "kt_ok",
                             "mid", "mid_ok", "num_ok", "y_ok", "ones_ok"))
        block = ctx.enter_context(nc.Block())

        @block.sync
        def _(sp):
            for dst, src in ((wq, w["L0_attn_Wq"]), (wk, w["L0_attn_Wk"]), (wv, w["L0_attn_Wv"]),
                             (proj, w["L0_attn_proj"])):
                sp.dma_start(dst[:, :, :], src.rearrange("(k p) n -> p k n", p=P)).then_inc(w_in, 16)

        @block.gpsimd
        def _(pool):
            pool.memset(kx[:, :], 0.0)
            pool.memset(kv[:, :], 1.0).then_inc(ones_ok, 1)

        @block.tensor
        def _(pe):
            pe.wait_ge(w_in, 64)
            for s, wt in enumerate((wq, wk)):
                for kd in range(KD):
                    for ke in range(KD):
                        pe.matmul(turn[0][:, s * KD + kd, 0:PROJ], wt[:, ke, kd * P:(kd + 1) * P], proj[:, ke, :],
                                  start=(ke == 0), stop=(ke == KD - 1))
            for ke in range(KD):
                for kd in range(KD):
                    m = pe.transpose(turn[1][:, ke * KD + kd, :], wv[:, kd, ke * P:(ke + 1) * P], ident[:, :])
            m.then_inc(w_turned, 1)
            pe.wait_ge(w_ok, 2)
            with pe.Fori(0, B) as b:
                for c in range(2):
                    for k in range(KD):
                        m = pe.matmul(pre[c][:, :], map_w[:, k, :], xT[:, k, bass.ds(b * L + c * C, C)],
                                      start=(k == 0), stop=(k == KD - 1))
                    m.then_inc(pre_ok, 1)
                for c in range(2):
                    pe.wait_ge(fm_ok, b * 2 + c + 1)
                    for t in range(4):
                        m = pe.transpose(turn[c][:, t, :], fm[:, c, t * P:(t + 1) * P], ident[:, :])
                    m.then_inc(turn_ok, 1)
                pe.wait_ge(kt_ok, b * 2 + 2)
                for t in range(TB):
                    m = pe.matmul(small[0:PROJ, 0:D], kt[:, t, :], xn[:, b * TB + t, :],
                                  start=(t == 0), stop=(t == TB - 1))
                m.then_inc(mid, 1)
                pe.wait_ge(mid_ok, b * 3 + 1)
                for k in range(KD):
                    m = pe.transpose(small[:, k * P:(k + 1) * P], kx[:, k * P:(k + 1) * P], ident[:, :])
                m.then_inc(mid, 1)
                pe.wait_ge(mid_ok, b * 3 + 2)
                for k in range(KD):
                    m = pe.matmul(small[0:PROJ, 0:D], kxT[:, k, :], wvT[:, k, :], start=(k == 0), stop=(k == KD - 1))
                m.then_inc(mid, 1)
                pe.wait_ge(mid_ok, b * 3 + 3)
                for t in range(TB):
                    pe.wait_ge(y_ok, b * TB + t + 1)
                    pe.matmul(num[t % 2][:, 0:D + 1], fm[0:PROJ, t // 4, t % 4 * P:(t % 4 + 1) * P], kv[:, :],
                              start=True, stop=True).then_inc(num_ok, 1)

        @block.vector
        def _(dve):
            dve.wait_ge(w_turned, 1)
            dve.tensor_copy(map_w[:, :, 0:PROJ], turn[0][:, 0:2, 0:PROJ])
            dve.tensor_copy(map_w[:, :, PROJ:2 * PROJ], turn[0][:, 2:4, 0:PROJ]).then_inc(w_ok, 1)
            dve.tensor_copy(wvT[:, :, :], turn[1][:, :, :].rearrange("p (k c) n -> p k (c n)", k=KD)).then_inc(w_ok, 1)
            dve.wait_ge(ones_ok, 1)
            with dve.Fori(0, B) as b:
                for c in range(2):
                    dve.wait_ge(pre_ok, b * 2 + c + 1)
                    dve.tensor_scalar(low[:, c, :], pre[c][:, :], 0.0, None, ALU.min).then_inc(low_ok, 1)
                for c in range(2):
                    dve.wait_ge(exp_ok, b * 2 + c + 1)
                    if c == 0:
                        dve.wait_ge(num_ok, b * TB)
                    dve.scalar_tensor_tensor(out=fm[:, c, :], in0=pre[c][:, :], scalar=0.0, in1=low[:, c, :],
                                             op0=ALU.max, op1=ALU.add).then_inc(fm_ok, 1)
                for c in range(2):
                    dve.wait_ge(turn_ok, b * 2 + c + 1)
                    dve.tensor_copy(kt[:, c * 4:c * 4 + 4, :], turn[c][:, :, PROJ:2 * PROJ]).then_inc(kt_ok, 1)
                dve.wait_ge(mid, b * 3 + 1)
                dve.tensor_copy(kx[0:PROJ, :], small[0:PROJ, 0:D]).then_inc(mid_ok, 1)
                dve.wait_ge(mid, b * 3 + 2)
                dve.tensor_copy(kxT[:, :, :], small[:, 0:KD * P].rearrange("p (k n) -> p k n", k=KD)[:, :, 0:PROJ])\
                   .then_inc(mid_ok, 1)
                dve.wait_ge(mid, b * 3 + 3)
                dve.tensor_copy(kv[:, 0:D], small[0:PROJ, 0:D]).then_inc(mid_ok, 1)

        @block.scalar
        def _(act):
            act.sem_inc(y_ok, 2)
            with act.Fori(0, B) as b:
                for c in range(2):
                    act.wait_ge(low_ok, b * 2 + c + 1)
                    act.activation(low[:, c, :], low[:, c, :], ACT.Exp).then_inc(exp_ok, 1)
                for t in range(TB):
                    act.wait_ge(num_ok, b * TB + t + 1)
                    act.activation(y[:, b * TB + t, :], num[t % 2][:, 0:D + 1], ACT.Copy).then_inc(y_ok, 1)


def clear_phase(nc):
    spent = sorted(nc.released_uncleared_semaphores)
    with nc.Block() as block:

        @block.gpsimd
        def _(pool):
            start = 0
            for i in range(1, len(spent) + 1):
                if i == len(spent) or spent[i] != spent[i - 1] + 1:
                    pool.sem_clear(range(spent[start], spent[i - 1] + 1))
                    start = i


ROWS0 = (BLK0 + 1) // 2 * 2 * P
BLOCKS0 = ROWS0 // P
ROWS1 = E * CAP
FETCHES = 4
FAR = 1 << 20


def make_router(nc, ctx, whole, tag):
    def sem(name):
        return whole.enter_context(nc.semaphore(f"{tag}_{name}"))

    def sb(name, shape, dt=F32):
        return ctx.enter_context(nc.sbuf_tensor(f"{tag}_{name}", shape, dt))
    return {"put": [sb(f"put{i}", [P, T], U32) for i in range(2)],
            "take": [sb(f"take{i}", [P, T], U32) for i in range(2)],
            "weight": [sb(f"weight{i}", [P, T]) for i in range(2)],
            "expert": sb("expert", [P, BLOCKS0], I32),
            "scattered": sem("scattered"),
            "fetched": [[sem(f"fetched{u}_{i}") for i in range(2)] for u in range(FETCHES)]}


def route_phase(nc, tag, gate, gate_is_rows, xT, xn, ident, r, rows, capacity, shared=None):
    C = 512
    FT = (FS + P - 1) // P
    n_chunks = N // C
    with ExitStack() as ctx:
        def sb(name, shape, dt=F32):
            return ctx.enter_context(nc.sbuf_tensor(f"{tag}_{name}", shape, dt))

        def ps(name, shape):
            return ctx.enter_context(nc.psum_tensor(f"{tag}_{name}", shape, F32))

        def sem(name):
            return ctx.enter_context(nc.semaphore(f"{tag}_{name}"))

        gw = sb("gw", [P, KD, E])
        gw_rows = sb("gw_rows", [E, D])
        logT = sb("logT", [E, 2, C])
        s, one, two, mask, work, offs = (sb(n, [P, T, E]) for n in ("s", "one", "two", "mask", "work", "offs"))
        rank = sb("rank", [P, T, E])
        col, m1, m2, keep = (sb(n, [P, T]) for n in ("col", "m1", "m2", "keep"))
        before = sb("before", [P, P])
        ones = sb("ones", [P, P])
        count, blocks, end, end2 = (sb(n, [P, E]) for n in ("count", "blocks", "end", "end2"))
        edge = sb("edge", [P, E, T])
        cmp = sb("cmp", [P, E, T])
        slot_no = sb("slot_no", [P, BLOCKS0, E])
        cmp2 = sb("cmp2", [P, BLOCKS0, E])
        base = sb("base", [P, E])
        expert_f = sb("expert_f", [P, BLOCKS0])
        pl = ps("pl", [P, 512])
        pt = ps("pt", [P, T, E])
        pc = ps("pc", [P, 2, T * E])
        (w_in, gw_turned, gw_ok, log_ok, logs_in, turned, made, chain, low_ok, exp_ok, mask_ok, counted, slots_ok,
         sh_in, up_ok, silu_ok, hid_ok, down_ok, out_ok) = (sem(n) for n in (
             "w_in", "gw_turned", "gw_ok", "log_ok", "logs_in", "turned", "made", "chain", "low_ok", "exp_ok",
             "mask_ok", "counted", "slots_ok", "sh_in", "up_ok", "silu_ok", "hid_ok", "down_ok",
             "out_ok"))
        padded = sem("padded")
        if shared is not None:
            sw, y = shared
            wg, wu = (sb(n, [P, KD, FT * P]) for n in ("wg", "wu"))
            wd = sb("wd", [P, FT, D])
            act_g = sb("act_g", [P, 2, C])
            hid = sb("hid", [P, FT, C])
            pg = [ps(f"pg{i}", [P, C]) for i in range(2)]
            pu = [ps(f"pu{i}", [P, C]) for i in range(2)]
            pd = ps("pd", [P, 2, D])
        block = ctx.enter_context(nc.Block())

        def shared_up(pe, c):
            if isinstance(c, int):
                pe.wait_ge(sh_in, 64)
            for f in range(FT):
                q = c * FT + f
                pe.wait_ge(hid_ok, q + 1)
                for wt, pp in ((wg, pg), (wu, pu)):
                    for k in range(KD):
                        m = pe.matmul(pp[f % 2][:, :], wt[:, k, f * P:(f + 1) * P],
                                      xT[:, k, bass.ds(c * C, C)], start=(k == 0), stop=(k == KD - 1))
                m.then_inc(up_ok, 1)

        def shared_down(pe, c):
            pe.wait_ge(hid_ok, (c + 1) * FT + 2)
            for h in range(C // P // 2):
                pe.wait_ge(out_ok, c * 2 + h)
                for v in range(2):
                    for f in range(FT):
                        t = h * 2 + v
                        m = pe.matmul(pd[:, v, :], hid[:, f, t * P:(t + 1) * P], wd[:, f, :],
                                      start=(f == 0), stop=(f == FT - 1))
                m.then_inc(down_ok, 1)

        def shared_act(act, c):
            for f in range(FT):
                q = c * FT + f
                act.wait_ge(up_ok, q + 1)
                act.wait_ge(hid_ok, q + 1)
                act.activation(act_g[:, f % 2, :], pg[f % 2][:, :], ACT.Silu).then_inc(silu_ok, 1)
            for h in range(C // P // 2):
                act.wait_ge(down_ok, c * 2 + h + 1)
                act.activation(y[:, bass.ds(c * (C // P) + h * 2, 2), 0:D], pd[:, :, :], ACT.Copy).then_inc(out_ok, 1)

        def shared_mul(dve, c):
            for f in range(FT):
                q = c * FT + f
                dve.wait_ge(silu_ok, q + 1)
                if f == 0:
                    dve.wait_ge(down_ok, c * 2)
                dve.tensor_tensor(hid[:, f, :], act_g[:, f % 2, :], pu[f % 2][:, :], ALU.mult)\
                   .then_inc(hid_ok, 1)

        @block.sync
        def _(sp):
            if gate_is_rows:
                sp.dma_start(gw_rows[:, :], gate).then_inc(w_in, 16)
            else:
                sp.dma_start(gw[:, :, :], gate.rearrange("(k p) e -> p k e", p=P)).then_inc(w_in, 16)
            if shared is not None:
                for dst, name in ((wg, "L0_ffn_sw_gate"), (wu, "L0_ffn_sw_up")):
                    sp.dma_start(dst[:, :, 0:FS], sw[name].rearrange("(k p) n -> p k n", p=P)).then_inc(sh_in, 16)
                full, rest = FS // P, FS % P
                sp.wait_ge(padded, 1)
                sp.dma_start(wd[:, 0:full, :], sw["L0_ffn_sw_down"][0:full * P, :].rearrange("(k p) n -> p k n", p=P))\
                  .then_inc(sh_in, 16)
                sp.dma_start(wd[0:rest, full, :], sw["L0_ffn_sw_down"][full * P:FS, :]).then_inc(sh_in, 16)

        @block.tensor
        def _(pe):
            pe.wait_ge(w_in, 16)
            if gate_is_rows:
                for k in range(KD):
                    m = pe.transpose(pl[:, k * E:(k + 1) * E], gw_rows[:, k * P:(k + 1) * P], ident[0:E, 0:E])
                m.then_inc(gw_turned, 1)
                pe.wait_ge(gw_ok, 1)
            for c in range(n_chunks):
                if c >= 1:
                    pe.wait_ge(log_ok, c)
                for k in range(KD):
                    m = pe.matmul(pl[0:E, :], gw[:, k, :], xT[:, k, c * C:(c + 1) * C],
                                  start=(k == 0), stop=(k == KD - 1))
                m.then_inc(logs_in, 1)
                pe.wait_ge(log_ok, c + 1)
                for t in range(C // P):
                    m = pe.transpose(pt[:, c * (C // P) + t, :], logT[:, c % 2, t * P:(t + 1) * P], ident[0:E, 0:E])
                m.then_inc(turned, 1)
            if shared is not None:
                shared_up(pe, 0)
                shared_down(pe, 0)
            pe.wait_ge(mask_ok, 1)
            pe.wait_ge(made, 3)
            pe.matmul(pc[:, 0, :], before[:, :], mask[:, :, :].rearrange("p t e -> p (t e)"), start=True, stop=True)
            pe.matmul(pc[:, 1, :], ones[:, :], mask[:, :, :].rearrange("p t e -> p (t e)"),
                      start=True, stop=True).then_inc(counted, 1)
            if shared is not None:
                with pe.Fori(1, n_chunks) as c:
                    shared_up(pe, c)
                    shared_down(pe, c)

        @block.scalar
        def _(act):
            for c in range(n_chunks):
                act.wait_ge(logs_in, c + 1)
                if c >= 2:
                    act.wait_ge(turned, c - 1)
                act.activation(logT[:, c % 2, :], pl[0:E, :], ACT.Copy).then_inc(log_ok, 1)
            if shared is not None:
                shared_act(act, 0)
            act.wait_ge(low_ok, 1)
            act.activation(s[:, :, :], s[:, :, :], ACT.Exp).then_inc(exp_ok, 1)
            if shared is not None:
                with act.Fori(1, n_chunks) as c:
                    shared_act(act, c)

        @block.vector
        def _(dve):
            link = Chain(dve, chain).step
            if shared is not None:
                dve.sem_inc(hid_ok, 2)
            if gate_is_rows:
                dve.wait_ge(gw_turned, 1)
                dve.tensor_copy(gw[:, :, :], pl[:, 0:KD * E].rearrange("p (k e) -> p k e", k=KD)).then_inc(gw_ok, 1)
            dve.wait_ge(turned, n_chunks)
            link(dve.tensor_reduce(col[:, :], pt[:, :, :], AX.X, ALU.max))
            dve.tensor_tensor(s[:, :, :], pt[:, :, :], spread(col[:, :], E), ALU.subtract).then_inc(low_ok, 1)
            if shared is not None:
                shared_mul(dve, 0)
            dve.wait_ge(exp_ok, 1)
            link(dve.tensor_reduce(col[:, :], s[:, :, :], AX.X, ALU.add))
            link(dve.reciprocal(col[:, :], col[:, :]))
            link(dve.tensor_tensor(s[:, :, :], s[:, :, :], spread(col[:, :], E), ALU.mult))
            dve.wait_ge(made, 3)

            def pick(best, hot):
                link(dve.tensor_reduce(best[:, :], s[:, :, :], AX.X, ALU.max))
                link(dve.tensor_tensor(work[:, :, :], s[:, :, :], spread(best[:, :], E), ALU.is_ge))
                link(dve.tensor_tensor(work[:, :, :], work[:, :, :], rank[:, :, :], ALU.mult))
                link(dve.tensor_reduce(col[:, :], work[:, :, :], AX.X, ALU.max))
                link(dve.tensor_tensor(hot[:, :, :], work[:, :, :], spread(col[:, :], E), ALU.is_equal))

            pick(m1, one)
            link(dve.scalar_tensor_tensor(out=s[:, :, :], in0=one[:, :, :], scalar=-2.0, in1=s[:, :, :],
                                          op0=ALU.mult, op1=ALU.add))
            pick(m2, two)
            dve.tensor_tensor(mask[:, :, :], one[:, :, :], two[:, :, :], ALU.add).then_inc(mask_ok, 1)
            dve.wait_ge(counted, 1)
            whole = pc[:, 1, :].rearrange("p (t e) -> p t e", e=E)
            link(dve.tensor_copy(work[:, :, :], whole))
            a, b2 = work, s
            step = 1
            while step < T:
                dve.tensor_copy(b2[:, 0:step, :], a[:, 0:step, :])
                link(dve.tensor_tensor(b2[:, step:T, :], a[:, step:T, :], a[:, 0:T - step, :], ALU.add))
                a, b2 = b2, a
                step *= 2
            link(dve.tensor_copy(count[:, :], a[:, T - 1, :]))
            link(dve.tensor_tensor(offs[:, :, :], a[:, :, :], whole, ALU.subtract))
            link(dve.tensor_tensor(offs[:, :, :], offs[:, :, :], pc[:, 0, :].rearrange("p (t e) -> p t e", e=E),
                                   ALU.add))
            if capacity is None:
                link(dve.tensor_tensor(cmp[:, :, :], spread(count[:, :], T), edge[:, :, :], ALU.is_gt))
                link(dve.tensor_reduce(blocks[:, :], cmp[:, :, :], AX.X, ALU.add))
                a2, b3 = end, end2
                link(dve.tensor_copy(a2[:, :], blocks[:, :]))
                step = 1
                while step < E:
                    dve.tensor_copy(b3[:, 0:step], a2[:, 0:step])
                    link(dve.tensor_tensor(b3[:, step:E], a2[:, step:E], a2[:, 0:E - step], ALU.add))
                    a2, b3 = b3, a2
                    step *= 2
                link(dve.tensor_tensor(base[:, :], a2[:, :], blocks[:, :], ALU.subtract))
                link(dve.tensor_scalar(base[:, :], base[:, :], float(P), None, ALU.mult))
                link(dve.tensor_tensor(cmp2[:, :, :], slot_no[:, :, :],
                                       a2[:, :].unsqueeze(1).broadcast_to([P, BLOCKS0, E]), ALU.is_ge))
                link(dve.tensor_reduce(expert_f[:, :], cmp2[:, :, :], AX.X, ALU.add))
                dve.tensor_scalar(r["expert"][:, :], expert_f[:, :], float(E - 1), None, ALU.min)
            hots = ((one, m1, 0), (two, m2, 1))
            if capacity is not None:
                for hot, best, i in hots:
                    link(dve.tensor_tensor(work[:, :, :], offs[:, :, :], hot[:, :, :], ALU.mult))
                    link(dve.tensor_reduce(keep[:, :], work[:, :, :], AX.X, ALU.add))
                    link(dve.tensor_scalar(keep[:, :], keep[:, :], float(capacity), None, ALU.is_lt))
                    link(dve.tensor_tensor(r["weight"][i][:, :], best[:, :], keep[:, :], ALU.mult))
                    link(dve.tensor_tensor(work[:, :, :], offs[:, :, :],
                                           base[:, :].unsqueeze(1).broadcast_to([P, T, E]), ALU.add))
                    link(dve.tensor_tensor(work[:, :, :], work[:, :, :], hot[:, :, :], ALU.mult))
                    link(dve.tensor_reduce(col[:, :], work[:, :, :], AX.X, ALU.add))
                    link(dve.tensor_tensor(col[:, :], col[:, :], keep[:, :], ALU.mult))
                    dve.tensor_copy(r["take"][i][:, :], col[:, :])
                    link(dve.tensor_scalar(keep[:, :], keep[:, :], -float(FAR), float(FAR), ALU.mult, ALU.add))
                    dve.tensor_tensor(r["put"][i][:, :], col[:, :], keep[:, :], ALU.add).then_inc(slots_ok, 1)
                    dve.wait_ge(slots_ok, i + 1)
            else:
                link(dve.tensor_tensor(offs[:, :, :], offs[:, :, :],
                                       base[:, :].unsqueeze(1).broadcast_to([P, T, E]), ALU.add))
                for hot, best, i in hots:
                    link(dve.tensor_tensor(work[:, :, :], offs[:, :, :], hot[:, :, :], ALU.mult))
                    link(dve.tensor_reduce(col[:, :], work[:, :, :], AX.X, ALU.add))
                    dve.tensor_copy(r["take"][i][:, :], col[:, :])
                    dve.tensor_copy(r["put"][i][:, :], col[:, :]).then_inc(slots_ok, 1)
                    dve.wait_ge(slots_ok, i + 1)
            if capacity is None:
                link(dve.tensor_tensor(col[:, :], m1[:, :], m2[:, :], ALU.add))
                link(dve.tensor_scalar(col[:, :], col[:, :], 1e-20, None, ALU.add))
                link(dve.reciprocal(col[:, :], col[:, :]))
                link(dve.tensor_scalar(col[:, :], col[:, :], ROUTE_SCALE, None, ALU.mult))
                for best, i in ((m1, 0), (m2, 1)):
                    dve.tensor_tensor(r["weight"][i][:, :], best[:, :], col[:, :], ALU.mult)
            if shared is not None:
                with dve.Fori(1, n_chunks) as c:
                    shared_mul(dve, c)

        @block.gpsimd
        def _(pool):
            if shared is not None:
                pool.memset(wg[:, :, FS:FT * P], 0.0)
                pool.memset(wu[:, :, FS:FT * P], 0.0)
                pool.memset(wd[:, FT - 1, :], 0.0).then_inc(padded, 1)
            pool.iota(rank[:, :, :], pattern=[[0, T], [-1, E]], base=E, channel_multiplier=0,
                      allow_small_or_imprecise_dtypes=True)
            pool.iota(edge[:, :, :], pattern=[[0, E], [P, T]], base=0, channel_multiplier=0,
                      allow_small_or_imprecise_dtypes=True)
            pool.iota(slot_no[:, :, :], pattern=[[1, BLOCKS0], [0, E]], base=0, channel_multiplier=0,
                      allow_small_or_imprecise_dtypes=True)
            if capacity is not None:
                pool.iota(base[:, :], pattern=[[capacity, E]], base=0, channel_multiplier=0,
                          allow_small_or_imprecise_dtypes=True)
            pool.memset(ones[:, :], 1.0)
            pool.memset(before[:, :], 1.0).then_inc(made, 2)
            pool.wait_ge(made, 2)
            pool.affine_select(out=before[:, :], in_=before[:, :], compare_op=ALU.is_gt, fill=0.0, base=0,
                               pattern=[[1, P]], channel_multiplier=-1).then_inc(made, 1)
            for i in range(2):
                pool.wait_ge(slots_ok, i + 1)
                for t in range(T):
                    pool.indirect_dma_start(rows[:, :], bass.IndirectOffsetOnAxis(ap=r["put"][i][:, t:t + 1], axis=0),
                                            xn[:, t, :], None, bounds_check=rows.shape[0] - 1, oob_is_err=False)\
                        .then_inc(r["scattered"], 16)
            pool.wait_ge(r["scattered"], 16 * 2 * T)


def layer0_experts(nc, w, r, rows, outs, ident):
    FT = (F0 + P - 1) // P
    with ExitStack() as ctx:
        def sb(name, shape, dt=F32):
            return ctx.enter_context(nc.sbuf_tensor(f"e0_{name}", shape, dt))

        def ps(name, shape):
            return ctx.enter_context(nc.psum_tensor(f"e0_{name}", shape, F32))

        def sem(name):
            return ctx.enter_context(nc.semaphore(f"e0_{name}"))

        wg, wu = (sb(n, [P, KD, E * F0]) for n in ("wg", "wu"))
        wd = sb("wd", [P, FT, E * D])
        xg = sb("xg", [P, 2, D])
        xgT = sb("xgT", [P, 2, KD, P])
        sg = sb("sg", [P, 2, F0])
        h = sb("h", [P, 2, F0])
        hT = sb("hT", [P, 2, FT, P])
        yo = sb("yo", [P, 2, D])
        px = ps("px", [P, KD, P])
        pg = [ps(f"pg{i}", [P, 512]) for i in range(2)]
        pu = [ps(f"pu{i}", [P, 512]) for i in range(2)]
        ph = ps("ph", [P, FT, P])
        py = ps("py", [P, D])
        w_in, x_turned, xT_ok, up_ok, silu_ok, h_ok, h_turned, hT_ok, y_done, y_ok = (
            sem(n) for n in ("w_in", "x_turned", "xT_ok", "up_ok", "silu_ok", "h_ok", "h_turned", "hT_ok",
                             "y_done", "y_ok"))
        x_in, stored = ([sem(f"{n}{i}") for i in range(2)] for n in ("x_in", "stored"))
        block = ctx.enter_context(nc.Block())

        def width(f):
            return min(P, F0 - f * P)

        def walk(engine, head, step, tail):
            head()
            with engine.Fori(0, (BLOCKS0 - 2) // 2) as i:
                step(i * 2 + 1, 1, i, i)
                step(i * 2 + 2, 0, i + 1, i)
            step(BLOCKS0 - 1, 1, BLOCKS0 // 2 - 1, BLOCKS0 // 2 - 1)
            tail()

        @block.sync
        def _(sp):
            x_rows = rows.rearrange("(j p) d -> j p d", p=P)
            y_rows = outs.rearrange("(j p) d -> j p d", p=P)

            def load(j, slot):
                sp.wait_ge(x_turned, j + 1)
                sp.dma_start(xg[:, slot, :], x_rows[bass.ds(j, 1), :, :].rearrange("o p d -> p (o d)"))\
                  .then_inc(x_in[slot], 16)

            def store(j, slot):
                sp.wait_ge(y_ok, j + 1)
                sp.dma_start(y_rows[bass.ds(j, 1), :, :].rearrange("o p d -> p (o d)"), yo[:, slot, :])\
                  .then_inc(stored[slot], 16)

            load(0, 0)
            for dst, name, width_all in ((wg, "L0_ffn_w_gate", D), (wu, "L0_ffn_w_up", D), (wd, "L0_ffn_w_down", F0)):
                for k in range((width_all + P - 1) // P):
                    n = min(P, width_all - k * P)
                    sp.dma_start(dst[0:n, k, :].rearrange("p (e n) -> p e n", e=E),
                                 w[name][:, k * P:k * P + n, :].rearrange("e p n -> p e n")).then_inc(w_in, 16)

            def step(j, slot, n, m):
                load(j, slot)
                store(j - 1, 1 - slot)
            for q in stored:
                sp.sem_inc(q, 16)
            walk(sp, lambda: None, step, lambda: store(BLOCKS0 - 1, 1))
            for q in stored:
                sp.wait_ge(q, 16 * (BLOCKS0 // 2 + 1))

        @block.tensor
        def _(pe):
            pe.sem_inc(x_turned, 2)

            def turn_x(j, slot, n):
                pe.wait_ge(x_in[slot], 16 * (n + 1))
                pe.wait_ge(xT_ok, j)
                for k in range(KD):
                    m = pe.transpose(px[:, k, :], xg[:, slot, k * P:(k + 1) * P], ident[:, :])
                m.then_inc(x_turned, 1)

            def up(j, slot):
                e = pe.value_load(r["expert"][0:1, bass.ds(j, 1)], min_val=0, max_val=E - 1)
                pe.wait_ge(xT_ok, j + 1)
                pe.wait_ge(h_ok, j + 1)
                for wt, pp in ((wg, pg), (wu, pu)):
                    for k in range(KD):
                        m = pe.matmul(pp[slot][:, 0:F0], xgT[:, slot, k, :], wt[:, k, bass.ds(e * F0, F0)],
                                      start=(k == 0), stop=(k == KD - 1))
                m.then_inc(up_ok, 1)
                return e

            def down(j, slot):
                e = pe.value_load(r["expert"][0:1, bass.ds(j, 1)], min_val=0, max_val=E - 1)
                pe.wait_ge(h_ok, j + 3)
                for f in range(FT):
                    n = width(f)
                    m = pe.transpose(ph[0:n, f, :], h[:, slot, f * P:f * P + n], ident[:, :])
                m.then_inc(h_turned, 1)
                pe.wait_ge(hT_ok, j + 1)
                pe.wait_ge(y_ok, j)
                for f in range(FT):
                    n = width(f)
                    m = pe.matmul(py[:, :], hT[0:n, slot, f, :], wd[0:n, f, bass.ds(e * D, D)],
                                  start=(f == 0), stop=(f == FT - 1))
                m.then_inc(y_done, 1)

            def head():
                turn_x(0, 0, 0)
                pe.wait_ge(w_in, 16 * (2 * KD + FT))
                up(0, 0)

            def step(j, slot, n, m):
                turn_x(j, slot, n)
                up(j, slot)
                down(j - 1, 1 - slot)
            walk(pe, head, step, lambda: down(BLOCKS0 - 1, 1))

        @block.scalar
        def _(act):
            def xT(j, slot):
                act.wait_ge(x_turned, j + 3)
                act.activation(xgT[:, slot, :, :], px[:, :, :], ACT.Copy).then_inc(xT_ok, 1)

            def silu(j, slot):
                act.wait_ge(up_ok, j + 1)
                act.activation(sg[:, slot, :], pg[slot][:, 0:F0], ACT.Silu).then_inc(silu_ok, 1)

            def y(j, slot, n):
                act.wait_ge(y_done, j + 1)
                act.wait_ge(stored[slot], 16 * (n + 1))
                act.activation(yo[:, slot, :], py[:, :], ACT.Copy).then_inc(y_ok, 1)

            def head():
                xT(0, 0)
                silu(0, 0)

            def step(j, slot, n, m):
                xT(j, slot)
                silu(j, slot)
                y(j - 1, 1 - slot, m)
            walk(act, head, step, lambda: y(BLOCKS0 - 1, 1, BLOCKS0 // 2 - 1))

        @block.vector
        def _(dve):
            dve.sem_inc(h_ok, 2)

            def hidden(j, slot):
                dve.wait_ge(silu_ok, j + 1)
                dve.tensor_tensor(h[:, slot, :], sg[:, slot, :], pu[slot][:, 0:F0], ALU.mult).then_inc(h_ok, 1)

            def hiddenT(j, slot):
                dve.wait_ge(h_turned, j + 1)
                full = F0 // P
                dve.tensor_copy(hT[:, slot, 0:full, :], ph[:, 0:full, :])
                dve.tensor_copy(hT[0:width(full), slot, full, :], ph[0:width(full), full, :]).then_inc(hT_ok, 1)

            def step(j, slot, n, m):
                hiddenT(j - 1, 1 - slot)
                hidden(j, slot)
            walk(dve, lambda: hidden(0, 0), step, lambda: hiddenT(BLOCKS0 - 1, 1))


def combine_phase(nc, tag, r, outs, y, base_rows=None):
    R, fetched = FETCHES, r["fetched"]
    with ExitStack() as ctx:
        got = ctx.enter_context(nc.sbuf_tensor(f"{tag}_got", [P, R, 2, D], F32))
        added = ctx.enter_context(nc.semaphore(f"{tag}_added"))
        block = ctx.enter_context(nc.Block())

        @block.gpsimd
        def _(pool):
            for t in range(T):
                if t >= R:
                    pool.wait_ge(added, 2 * (t - R + 1))
                for i in range(2):
                    pool.indirect_dma_start(got[:, t % R, i, :], None, outs[:, :],
                                            bass.IndirectOffsetOnAxis(ap=r["take"][i][:, t:t + 1], axis=0))\
                        .then_inc(fetched[t % R][i], 16)

        @block.vector
        def _(dve):
            with dve.Fori(0, T // R) as g:
                for u in range(R):
                    t = g * R + u
                    for i in range(2):
                        dve.wait_ge(fetched[u][i], 16 * (g + 1))
                        dve.scalar_tensor_tensor(out=y[:, t, 0:D], in0=got[:, u, i, :],
                                                 scalar=r["weight"][i][:, bass.ds(t, 1)], in1=y[:, t, 0:D],
                                                 op0=ALU.mult, op1=ALU.add).then_inc(added, 1)
                        dve.wait_ge(added, 2 * t + i + 1)


SPAN = 512
MAX_UNITS = [(q, a, min(a + SPAN, (q + 1) * P)) for q in range(TB) for a in range(0, (q + 1) * P, SPAN)]
MAX_SHARE = [0, 1, 2, 2, 2, 2, 2, 1]
PT_AT = [sum(L - P * j for j in range(k)) for k in range(TB + 1)]
MASKED = -1e30


def attention_phase(nc, tag, wide, ident, q_src, out_cols, w=None, xT_dram=None, y=None):
    dh = DK if wide else HD
    pairs = (HA if wide else H1) // 2
    n_pairs = B * pairs
    scale = dh ** -0.5
    n_prep = 4
    n_v = 2 if wide else 0
    n_ot = 2 if wide else 0
    n_out = 4 if wide else 0
    n_max = len(MAX_UNITS)
    NARROW = 64
    with ExitStack() as ctx:
        def sb(name, shape, dt=F32):
            return ctx.enter_context(nc.sbuf_tensor(f"{tag}_{name}", shape, dt))

        def sem(name):
            return ctx.enter_context(nc.semaphore(f"{tag}_{name}"))

        if wide:
            xb = sb("xb", [P, 2, KD, L])
            wqk = sb("wqk", [P, 2, 3, KD, P])
            wo = sb("wo", [P, pairs, D])
            q1, q2, k1, k2 = ([[sb(f"{n}_{s}{c}", [P, L], F32R) for c in range(2)] for s in range(2)]
                              for n in ("q1", "q2", "k1", "k2"))
            o = sb("o", [P, TB, 2 * dh])
            oT = sb("oT", [P, L])
        else:
            qT, kT = ([sb(f"{n}_{s}", [P, L], F32R) for s in range(2)] for n in ("qT", "kT"))
            qc, kc = (sb(n, [P, TB, 2, NARROW]) for n in ("qc", "kc"))
            hi = sb("hi", [P, 2, TB, 2 * dh], F32R)
        v = [sb(f"v{s}", [P, TB, 2, dh + 1]) for s in range(2)]
        pt = [sb(f"pt{c}", [P, PT_AT[TB]]) for c in range(2)]
        parts = [sb(f"parts{c}", [P, TB, 2]) for c in range(2)]
        neg = sb("neg", [P, TB])
        mm = sb("mm", [P, 2, 2, TB], F32R)
        mt = sb("mt", [2 * TB, 2, P], F32R)
        rec = sb("rec", [P, TB])
        ident16 = sb("ident16", [P, P], BF16)
        late = sb("late", [P, P], BF16)
        lateT = sb("lateT", [P, P], BF16)
        g = [ctx.enter_context(nc.psum_tensor(f"{tag}_g{i}", [P, SPAN], F32)) for i in range(2)]
        stp = [ctx.enter_context(nc.psum_tensor(f"{tag}_st{i}", [P, L], F32)) for i in range(2)]
        po = [ctx.enter_context(nc.psum_tensor(f"{tag}_po{i}", [P, 4, P], F32)) for i in range(2)]
        (consts, prep, hi_ok, prep_ok, dup_ok, v_mm, v_ok, mx, max_ok, m_ok, mt_mm, mt_ok, st, pt_ok, pv, o_ok,
         ot_mm, ot_ok, out_mm, out_ok, chain, low_ok, rec_ok) = (sem(n) for n in (
             "consts", "prep", "hi_ok", "prep_ok", "dup_ok", "v_mm", "v_ok", "mx", "max_ok", "m_ok", "mt_mm", "mt_ok",
             "st", "pt_ok", "pv", "o_ok", "ot_mm", "ot_ok", "out_mm", "out_ok", "chain", "low_ok", "rec_ok"))
        passed, chain_pool = sem("passed"), sem("chain_pool")
        wo_in = sem("wo_in")
        loaded = [sem(f"loaded{s}") for s in range(2)]
        rows_out = [sem(f"rows_out{c}") for c in range(2)]
        rows_in = [sem(f"rows_in{c}") for c in range(2)]
        m_dram = [nc.dram_tensor(f"{tag}_m{c}", (2, L), F32).ap() for c in range(2)]
        block = ctx.enter_context(nc.Block())

        def walk(engine, step):
            step(-1, 1, False, False, True)
            step(0, 0, True, False, True)
            with engine.Fori(0, (n_pairs - 2) // 2) as j:
                step(j * 2 + 1, 1, True, True, True)
                step(j * 2 + 2, 0, True, True, True)
            step(n_pairs - 1, 1, True, True, False)
            step(n_pairs, 0, False, True, False)

        def shares(k):
            return range(sum(MAX_SHARE[:k]), sum(MAX_SHARE[:k + 1]))

        def head_rows(c, n):
            return slice(NARROW * c, NARROW * c + n)

        def max_operands(s, c):
            if wide:
                return q1[s][c], k1[s][c], slice(0, P)
            return qT[s], kT[s], head_rows(c, dh)

        def score_passes(s, c):
            if wide:
                return [(k1[s][c], q1[s][c], slice(0, P)), (k2[s][c], q2[s][c], slice(0, dh + 2))]
            return [(kT[s], qT[s], head_rows(c, 3 * dh + 2))]

        @block.sync
        def _(sp):
            def load(i, s):
                b, p = i // pairs, i % pairs
                sp.dma_start(xb[:, s, :, :], xT_dram[:, :, bass.ds(b * L, L)]).then_inc(loaded[s], 16)
                for n, name in enumerate(("L1_attn_Wq", "L1_attn_Wk", "L1_attn_Wv")):
                    sp.dma_start(wqk[:, s, n, :, :],
                                 w[name].rearrange("(k p) n -> p k n", p=P)[:, :, bass.ds(p * P, P)])\
                      .then_inc(loaded[s], 16)

            def step(i, s, nxt, more):
                if wide and more:
                    sp.wait_ge(v_mm, n_v * (i + 1))
                    load(i + 2, s)
                if nxt:
                    for c in range(2):
                        sp.wait_ge(mt_ok, 2 * (i + 1) + c + 1)
                        dst = q2[1 - s][c][dh:dh + 2, :] if wide else qT[1 - s][NARROW * c + 3 * dh:
                                                                              NARROW * c + 3 * dh + 2, :]
                        sp.dma_start(m_dram[c].rearrange("h (t q) -> (h t) q", q=P), mt[:, c, :].bitcast(F32))\
                          .then_inc(rows_out[c], 16)
                        sp.wait_ge(rows_out[c], 16 * (i + 2))
                        sp.dma_start(dst.bitcast(F32), m_dram[c]).then_inc(rows_in[c], 16)

            if wide:
                load(0, 0)
                load(1, 1)
                sp.dma_start(wo[:, :, :], w["L1_attn_Wo"].rearrange("(c p) n -> p c n", p=P)).then_inc(wo_in, 16)
            step(-1, 1, True, False)
            step(0, 0, True, True)
            with sp.Fori(0, (n_pairs - 4) // 2) as j:
                step(j * 2 + 1, 1, True, True)
                step(j * 2 + 2, 0, True, True)
            step(n_pairs - 3, 1, True, True)
            step(n_pairs - 2, 0, True, False)

        @block.tensor
        def _(pe):
            fills = []

            def fill(i, i_of, reader, per_pair, index):
                n = len(fills)
                if n >= 2:
                    sem_, per, off, at = fills[-2]
                    pe.wait_ge(sem_, (i + off) * per + at + 1)
                fills.append((reader, per_pair, i_of, index))
                return g[n % 2]

            def shift():
                fills[:] = [(a, b_, off - 1, d) for a, b_, off, d in fills]

            def project(i, s):
                if wide:
                    pe.wait_ge(loaded[s], 64 * ((i + 1) // 2 + 1))
                if not wide:
                    pe.wait_ge(low_ok, 4 * (i + 2))
                    pe.wait_ge(dup_ok, 4 * (i + 2))
                for n in range(2):
                    for h in range(2):
                        u = n * 2 + h
                        bank = fill(i, 1, prep_ok, n_prep, u)
                        if wide:
                            for k in range(KD):
                                m = pe.matmul(bank[:, :], wqk[:, s, n, k, :], xb[:, s, k, h * SPAN:(h + 1) * SPAN],
                                              start=(k == 0), stop=(k == KD - 1))
                        else:
                            for t in range(4):
                                m = pe.transpose(bank[:, t * P:(t + 1) * P],
                                                 (qc, kc)[n][:, h * 4 + t, :, :].rearrange("p c n -> p (c n)"),
                                                 ident[:, :])
                        m.then_inc(prep, 1)

            def project_v(i, s):
                for h in range(n_v):
                    bank = fill(i, 1, v_ok, n_v, h)
                    for t in range(4):
                        for k in range(KD):
                            m = pe.matmul(bank[:, t * P:(t + 1) * P],
                                          xb[:, s, k, (h * 4 + t) * P:(h * 4 + t + 1) * P], wqk[:, s, 2, k, :],
                                          start=(k == 0), stop=(k == KD - 1))
                    m.then_inc(v_mm, 1)

            def max_unit(i, s, c, u):
                if u == 0 and c == 0:
                    if wide:
                        pe.wait_ge(dup_ok, 4 * (i + 2))
                    pe.wait_ge(prep_ok, n_prep * (i + 2))
                tile, a, z = MAX_UNITS[u]
                bank = fill(i, 1, max_ok, 2 * n_max, c * n_max + u)
                q_, k_, rows = max_operands(s, c)
                diagonal = z == (tile + 1) * P
                m = pe.matmul(bank[:, 0:z - a], q_[rows, tile * P:(tile + 1) * P], k_[rows, a:z],
                              start=True, stop=not diagonal)
                if diagonal:
                    m = pe.matmul(bank[:, z - a - P:z - a], ident16[:, :], late[:, :], start=False, stop=True)
                m.then_inc(mx, 1)

            def turn_max(i, c):
                pe.wait_ge(m_ok, 2 * (i + 1) + c + 1)
                bank = fill(i, 1, mt_ok, 2, c)
                pe.transpose(bank[0:2 * TB, 0:P], mm[:, c, :, :].rearrange("p h t -> p (h t)").bitcast(F32),
                             ident[:, :]).then_inc(mt_mm, 1)

            def score(i, s, c, k):
                pe.wait_ge(pt_ok, 2 * TB * i + c * TB + k + 1)
                if k == 0:
                    pe.wait_ge(rows_in[c], 16 * (i + 1))
                spans = [(a, z) for a, z in ((0, SPAN), (SPAN, L)) if z > k * P]
                for a, z in spans:
                    a = max(a, k * P)
                    for n, (k_, q_, rows) in enumerate(score_passes(s, c)):
                        last = n == len(score_passes(s, c)) - 1 and a != k * P
                        m = pe.matmul(stp[k % 2][:, a:z], k_[rows, k * P:(k + 1) * P], q_[rows, a:z],
                                      start=(n == 0), stop=last)
                    if a == k * P:
                        m = pe.matmul(stp[k % 2][:, a:a + P], ident16[:, :], lateT[:, :], start=False, stop=True)
                m.then_inc(st, 1)

            def weigh(i, s, c, k):
                pe.wait_ge(pt_ok, 2 * TB * i + c * TB + k + 3)
                if k == 0:
                    pe.wait_ge(o_ok, 2 * i + c)
                    if c == 0:
                        pe.wait_ge(v_ok, (n_v or 1) * (i + 1))
                for t in range(k, TB):
                    at = PT_AT[k] + (t - k) * P
                    m = pe.matmul(po[t // 4][:, t % 4, 0:dh + 1], pt[c][:, at:at + P], v[s][:, k, c, :],
                                  start=(k == 0 and t % 4 == 0), stop=(t == k), skip_group_check=True)
                if k == TB - 1:
                    m.then_inc(pv, 1)

            def turn_o(i):
                for h in range(n_ot):
                    if h == 0:
                        pe.wait_ge(o_ok, 2 * i)
                    bank = fill(i, -1, ot_ok, n_ot, h)
                    for t in range(4):
                        m = pe.transpose(bank[:, t * P:(t + 1) * P], o[:, h * 4 + t, :], ident[:, :])
                    m.then_inc(ot_mm, 1)

            def project_o(i, u):
                if u == 0:
                    pe.wait_ge(ot_ok, n_ot * i)
                bank = fill(i, -1, out_ok, n_out, u)
                for h in range(2):
                    t = u * 2 + h
                    m = pe.matmul(bank[:, h * D:(h + 1) * D], oT[:, t * P:(t + 1) * P], wo[:, (i - 1) % pairs, :],
                                  start=True, stop=True)
                m.then_inc(out_mm, 1)

            def step(i, s, cur, prev, nxt):
                if nxt:
                    project(i, 1 - s)
                for k in range(TB):
                    if cur:
                        score(i, s, 0, k)
                    if prev:
                        weigh(i - 1, 1 - s, 1, k)
                    if nxt:
                        for u in shares(k):
                            max_unit(i, 1 - s, 0, u)
                if nxt:
                    project_v(i, 1 - s)
                    turn_max(i, 0)
                if prev:
                    turn_o(i)
                for k in range(TB):
                    if cur:
                        score(i, s, 1, k)
                        weigh(i, s, 0, k)
                    if prev and 2 <= k < 2 + n_out:
                        project_o(i, k - 2)
                    if nxt:
                        for u in shares(k):
                            max_unit(i, 1 - s, 1, u)
                if nxt:
                    turn_max(i, 1)
                shift()

            pe.wait_ge(consts, 2)
            if wide:
                pe.wait_ge(wo_in, 16)
            walk(pe, step)

        @block.scalar
        def _(act):
            act.sem_inc(pt_ok, 2)

            def high(i, s):
                for n in range(2):
                    for h in range(2):
                        u = n * 2 + h
                        at = slice(h * SPAN, (h + 1) * SPAN)
                        act.wait_ge(prep, n_prep * (i + 1) + u + 1)
                        if wide:
                            for c in range(2):
                                rows = slice(c * dh, (c + 1) * dh)
                                m = act.activation((q1, k1)[n][s][c][rows, at], g[u % 2][rows, :], ACT.Copy,
                                                   scale=scale if n == 0 else 1.0)
                            m.then_inc(hi_ok, 1)
                        else:
                            act.activation((qT, kT)[n][s][:, at], g[u % 2][:, :], ACT.Copy).then_inc(prep_ok, 1)

            def values(i, s):
                for h in range(n_v):
                    act.wait_ge(v_mm, n_v * (i + 1) + h + 1)
                    for c in range(2):
                        m = act.activation(v[s][:, h * 4:h * 4 + 4, c, 0:dh],
                                           g[h % 2][:, :].rearrange("p (t c n) -> p t c n", t=4, c=2)[:, :, c, :],
                                           ACT.Copy)
                    m.then_inc(v_ok, 1)

            def exps(i, c):
                for k in range(TB):
                    act.wait_ge(st, 2 * TB * i + c * TB + k + 1)
                    act.activation(pt[c][:, PT_AT[k]:PT_AT[k + 1]], stp[k % 2][:, k * P:L], ACT.Exp)\
                       .then_inc(pt_ok, 1)

            def outT(i, nxt):
                for h in range(n_ot):
                    act.wait_ge(ot_mm, n_ot * (i - 1) + h + 1)
                    n = (n_prep + n_max + n_v + 1 if nxt else 0) + h
                    act.activation(oT[:, h * SPAN:(h + 1) * SPAN], g[n % 2][:, :], ACT.Copy).then_inc(ot_ok, 1)

            def step(i, s, cur, prev, nxt):
                if nxt:
                    high(i, 1 - s)
                if cur:
                    exps(i, 0)
                if nxt:
                    values(i, 1 - s)
                if prev:
                    outT(i, nxt)
                if cur:
                    exps(i, 1)
            walk(act, step)

        @block.vector
        def _(dve):
            def low(i, s):
                for n in range(2):
                    for h in range(2):
                        u = n * 2 + h
                        at = slice(h * SPAN, (h + 1) * SPAN)
                        dve.wait_ge(hi_ok, n_prep * (i + 1) + u + 1)
                        for c in range(2):
                            rows = slice(c * dh, (c + 1) * dh)
                            if n == 0:
                                dst = q1[s][c][(1 - c) * dh:(2 - c) * dh, at]
                            else:
                                dst = k2[s][c][0:dh, at]
                            m = dve.scalar_tensor_tensor(out=dst, in0=g[u % 2][rows, :],
                                                         scalar=scale if n == 0 else 1.0,
                                                         in1=(q1, k1)[n][s][c][rows, at].bitcast(F32),
                                                         op0=ALU.mult, op1=ALU.subtract)
                        m.then_inc(prep_ok, 1)

            def stack(i, s):
                b, p = (i + 1) // pairs, (i + 1) % pairs
                dve.wait_ge(prep, n_prep * (i + 1))
                for n in range(2):
                    src = q_src[:, bass.ds(b * TB, TB), bass.ds(n * D + p * 2 * dh, 2 * dh)]
                    dve.tensor_scalar(hi[:, n, :, :], src, scale if n == 0 else 1.0, None, ALU.mult).then_inc(hi_ok, 1)
                dve.wait_ge(hi_ok, 2 * (i + 2))
                for n in range(2):
                    for c in range(2):
                        src = q_src[:, bass.ds(b * TB, TB), bass.ds(n * D + p * 2 * dh + c * dh, dh)]
                        dst = (qc[:, :, c, dh:2 * dh], kc[:, :, c, 2 * dh:3 * dh])[n]
                        dve.scalar_tensor_tensor(out=dst, in0=src, scalar=scale if n == 0 else 1.0,
                                                 in1=hi[:, n, :, c * dh:(c + 1) * dh].bitcast(F32),
                                                 op0=ALU.mult, op1=ALU.subtract).then_inc(low_ok, 1)

            def max_unit(i, c, u, bank):
                tile, a, z = MAX_UNITS[u]
                dve.wait_ge(mx, 2 * n_max * (i + 1) + c * n_max + u + 1)
                dve.tensor_reduce(parts[c][:, tile, a // SPAN:a // SPAN + 1], bank[:, 0:z - a], AX.X, ALU.max)\
                   .then_inc(max_ok, 1)

            def minus_max(i, c):
                dve.wait_ge(max_ok, 2 * n_max * (i + 1) + (c + 1) * n_max)
                dve.tensor_reduce(neg[:, :], parts[c][:, :, :], AX.X, ALU.max, negate=True).then_inc(chain, 1)
                dve.wait_ge(chain, 2 * (2 * (i + 1) + c) + 1)
                dve.tensor_copy(mm[:, c, 0, :], neg[:, :]).then_inc(chain, 1)
                dve.wait_ge(chain, 2 * (2 * (i + 1) + c) + 2)
                dve.tensor_tensor(mm[:, c, 1, :], neg[:, :], mm[:, c, 0, :].bitcast(F32), ALU.subtract)\
                   .then_inc(m_ok, 1)

            def max_rows(i, c, bank):
                dve.wait_ge(mt_mm, 2 * (i + 1) + c + 1)
                dve.tensor_copy(mt[:, c, :], bank[0:2 * TB, 0:P]).then_inc(mt_ok, 1)

            def normalise(i, s, c):
                dve.wait_ge(pv, 2 * i + c + 1)
                for h in range(2):
                    r = dve.reciprocal(rec[:, 4 * h:4 * h + 4], po[h][:, :, dh])
                r.then_inc(rec_ok, 1)
                dve.wait_ge(rec_ok, 2 * i + c + 1)
                if wide and c == 0:
                    dve.wait_ge(ot_mm, n_ot * i)
                for h in range(2):
                    if wide:
                        dst = o[:, 4 * h:4 * h + 4, c * dh:(c + 1) * dh]
                    else:
                        b, p = i // pairs, i % pairs
                        dst = q_src[:, bass.ds(b * TB + 4 * h, 4), bass.ds(p * 2 * dh + c * dh, dh)]
                    m = dve.tensor_tensor(dst, po[h][:, :, 0:dh], spread(rec[:, 4 * h:4 * h + 4], dh), ALU.mult)
                m.then_inc(o_ok, 1)

            def add_out(i, u, bank):
                dve.wait_ge(out_mm, n_out * (i - 1) + u + 1)
                b = (i - 1) // pairs
                rows = y[:, bass.ds(b * TB + u * 2, 2), :]
                dve.tensor_tensor(rows, bank[:, :].rearrange("p (t d) -> p t d", t=2), rows, ALU.add)\
                   .then_inc(out_ok, 1)

            def step(i, s, cur, prev, nxt):
                n = 0
                if nxt:
                    (low if wide else stack)(i, 1 - s)
                    n += n_prep
                    for u in range(n_max):
                        max_unit(i, 0, u, g[(n + u) % 2])
                    n += n_max
                    minus_max(i, 0)
                if prev:
                    normalise(i - 1, 1 - s, 1)
                if nxt:
                    n += n_v
                    max_rows(i, 0, g[n % 2])
                    n += 1
                if prev:
                    n += n_ot
                for k in range(TB):
                    if prev and 2 <= k < 2 + n_out:
                        add_out(i, k - 2, g[n % 2])
                        n += 1
                    if nxt:
                        for u in shares(k):
                            max_unit(i, 1, u, g[n % 2])
                            n += 1
                if nxt:
                    minus_max(i, 1)
                if cur:
                    normalise(i, s, 0)
                if nxt:
                    max_rows(i, 1, g[n % 2])
            dve.wait_ge(consts, 2)
            walk(dve, step)

        @block.gpsimd
        def _(pool):
            link = Chain(pool, chain_pool).step
            for c in range(2):
                link(pool.memset(parts[c][:, :, 1:2], MASKED))
            for s in range(2):
                if wide:
                    for c in range(2):
                        link(pool.memset(k2[s][c][dh:dh + 2, :].bitcast(F32), 1.0))
                link(pool.memset(v[s][:, :, :, dh:dh + 1], 1.0))
            if not wide:
                link(pool.memset(qc[:, :, :, :], 0.0))
                link(pool.memset(kc[:, :, :, :], 0.0))
                link(pool.memset(kc[:, :, :, 3 * dh:3 * dh + 2], 1.0))
            link(pool.tensor_copy(ident16[:, :], ident[:, :]))
            link(pool.memset(late[:, :], 0.0))
            link(pool.memset(lateT[:, :], 0.0))
            pool.affine_select(out=late[:, :], in_=late[:, :], compare_op=ALU.is_ge, fill=MASKED, base=0,
                               pattern=[[-1, P]], channel_multiplier=1).then_inc(consts, 1)
            pool.affine_select(out=lateT[:, :], in_=lateT[:, :], compare_op=ALU.is_ge, fill=MASKED, base=0,
                               pattern=[[1, P]], channel_multiplier=-1).then_inc(consts, 1)
            pool.wait_ge(consts, 2)

            def copies(i, s):
                for n in range(2):
                    pool.wait_ge(hi_ok, n_prep * (i + 1) + 2 * n + 2)
                    pool.sem_inc(passed, 1)
                    for c in range(2):
                        rows, other = slice(c * dh, (c + 1) * dh), slice((1 - c) * dh, (2 - c) * dh)
                        if n == 0:
                            m = pool.tensor_copy(q2[s][c][0:dh, :], q1[s][c][rows, :].bitcast(F32))
                        else:
                            m = pool.tensor_copy(k1[s][c][other, :], k1[s][c][rows, :].bitcast(F32))
                        m.then_inc(dup_ok, 1)
                        pool.wait_ge(dup_ok, 4 * (i + 1) + 2 * n + c + 1)
                        pool.sem_inc(passed, 1)

            def stack_high(i, s):
                b, p = (i + 1) // pairs, (i + 1) % pairs
                pool.wait_ge(hi_ok, 2 * (i + 2))
                pool.sem_inc(passed, 1)
                for n, places in ((0, (0, 2)), (1, (0, 1))):
                    for at in places:
                        pool.tensor_copy((qc, kc)[n][:, :, :, at * dh:(at + 1) * dh],
                                         hi[:, n, :, :].bitcast(F32).rearrange("p t (c n) -> p t c n", c=2))\
                            .then_inc(dup_ok, 1)
                pool.wait_ge(pv, 2 * i if not isinstance(i, int) or i >= 0 else 0)
                pool.sem_inc(passed, 1)
                pool.tensor_copy(v[s][:, :, :, 0:dh],
                                 q_src[:, bass.ds(b * TB, TB), bass.ds(2 * D + p * 2 * dh, 2 * dh)]
                                 .rearrange("p t (c n) -> p t c n", c=2)).then_inc(v_ok, 1)

            def step(i, s, cur, prev, nxt):
                if nxt:
                    (copies if wide else stack_high)(i, 1 - s)
            walk(pool, step)


def qkv_phase(nc, w, tables, hT, qkv):
    G = 3 * D
    with ExitStack() as ctx:
        def sb(name, shape, dt=F32):
            return ctx.enter_context(nc.sbuf_tensor(f"qkv_{name}", shape, dt))

        def sem(name):
            return ctx.enter_context(nc.semaphore(f"qkv_{name}"))

        half = HD // 2
        heads = 2 * H1
        raw = sb("raw", [P, KD, G])
        wt = sb("wt", [P, KD, G])
        cos, sin = (sb(n, [P, TB, half]) for n in ("cos", "sin"))
        stage = sb("stage", [P, 2, KD, P])
        prods = [[sb(f"prod{i}_{u}", [P, heads, half]) for i in range(4)] for u in range(2)]
        pa = [ctx.enter_context(nc.psum_tensor(f"qkv_pa{i}", [P, 2 * D], F32)) for i in range(2)]
        pb = [ctx.enter_context(nc.psum_tensor(f"qkv_pb{i}", [P, D], F32)) for i in range(2)]
        w_in, w_ok, staged, done, rotated, v_ok, prod_ok, seen = (
            sem(n) for n in ("w_in", "w_ok", "staged", "done", "rotated", "v_ok", "prod_ok", "seen"))
        block = ctx.enter_context(nc.Block())

        @block.sync
        def _(sp):
            sp.dma_start(raw[:, :, :], w["L1_ffn_Wqkv"].rearrange("(k p) n -> p k n", p=P)).then_inc(w_in, 16)
            for dst, src in ((cos, tables[0]), (sin, tables[1])):
                sp.dma_start(dst[:, :, :], tiles_of(src)).then_inc(w_in, 16)

        @block.gpsimd
        def _(pool):
            pool.wait_ge(w_in, 48)
            for kind in range(3):
                for k in range(KD):
                    pool.tensor_copy(wt[:, k, kind * D:(kind + 1) * D].rearrange("p (h n) -> p h n", n=HD),
                                     raw[:, k, :].rearrange("p (h c n) -> p h c n", c=3, n=HD)[:, :, kind, :])\
                        .then_inc(w_ok, 1)

        @block.scalar
        def _(act):
            act.sem_inc(v_ok, 2)

            def copy_in(t, u):
                act.wait_ge(done, t + 1)
                act.activation(stage[:, u % 2, :, :], hT[:, :, bass.ds(t * P, P)], ACT.Copy).then_inc(staged, 1)

            with act.Fori(0, T // TB) as b:
                for u in range(TB):
                    t = b * TB + u
                    copy_in(t, u)
                    act.wait_ge(done, t + 3)
                    act.activation(qkv[:, t, 2 * D:G], pb[u % 2][:, :], ACT.Copy).then_inc(v_ok, 1)

        @block.tensor
        def _(pe):
            pe.sem_inc(done, 2)
            pe.wait_ge(w_ok, 6)
            with pe.Fori(0, T // TB) as b:
                for u in range(TB):
                    t = b * TB + u
                    pe.wait_ge(staged, t + 1)
                    pe.wait_ge(v_ok, t + 1)
                    pe.wait_ge(rotated, t + 1)
                    for out, a, z in ((pa, 0, 2 * D), (pb, 2 * D, G)):
                        for k in range(KD):
                            m = pe.matmul(out[u % 2][:, :], stage[:, u % 2, k, :], wt[:, k, a:z],
                                          start=(k == 0), stop=(k == KD - 1))
                    m.then_inc(done, 1)

        @block.vector
        def _(dve):
            dve.sem_inc(rotated, 2)
            with dve.Fori(0, T // TB) as b:
                for u in range(TB):
                    t = b * TB + u
                    dve.wait_ge(done, t + 3)
                    dve.sem_inc(seen, 1)
                    dve.wait_ge(rotated, t + 1)
                    prod = prods[u % 2]
                    x = pa[u % 2][:, :].rearrange("p (h c n) -> p h c n", c=2, n=half)
                    for n, (part, table) in enumerate(((0, cos), (1, sin), (0, sin), (1, cos))):
                        dve.tensor_tensor(prod[n][:, :, :], x[:, :, part, :],
                                          table[:, u, :].unsqueeze(1).broadcast_to([P, heads, half]), ALU.mult)\
                           .then_inc(prod_ok, 1)
                    dve.wait_ge(prod_ok, 4 * (t + 1))
                    y = qkv[:, t, 0:2 * D].rearrange("p (h c n) -> p h c n", c=2, n=half)
                    dve.tensor_tensor(y[:, :, 0, :], prod[0][:, :, :], prod[1][:, :, :], ALU.subtract)
                    dve.tensor_tensor(y[:, :, 1, :], prod[2][:, :, :], prod[3][:, :, :], ALU.add).then_inc(rotated, 1)


def output_phase(nc, w, ident, o, y):
    with ExitStack() as ctx:
        def sem(name):
            return ctx.enter_context(nc.semaphore(f"op_{name}"))

        wp = ctx.enter_context(nc.sbuf_tensor("op_w", [P, KD, D], F32))
        stage = ctx.enter_context(nc.sbuf_tensor("op_stage", [P, 2, 2, D], F32))
        oT = ctx.enter_context(nc.sbuf_tensor("op_oT", [P, 2, 4, P], F32))
        pt = [ctx.enter_context(nc.psum_tensor(f"op_pt{i}", [P, 4, P], F32)) for i in range(2)]
        py = [ctx.enter_context(nc.psum_tensor(f"op_py{i}", [P, 2, D], F32)) for i in range(2)]
        w_in, staged, turned, oT_ok, done, added, seen = (
            sem(n) for n in ("w_in", "staged", "turned", "oT_ok", "done", "added", "seen"))
        block = ctx.enter_context(nc.Block())

        @block.sync
        def _(sp):
            sp.dma_start(wp[:, :, :], w["L1_ffn_Wproj"].rearrange("(k p) n -> p k n", p=P)).then_inc(w_in, 16)

        @block.gpsimd
        def _(pool):
            with pool.Fori(0, T // 4) as i:
                for u in range(2):
                    s = i * 2 + u
                    pool.wait_ge(turned, s + 1)
                    pool.sem_inc(seen, 1)
                    pool.tensor_copy(stage[:, u, :, :], o[:, bass.ds(s * 2, 2), 0:D]).then_inc(staged, 1)

        @block.tensor
        def _(pe):
            pe.sem_inc(turned, 2)
            pe.wait_ge(w_in, 16)
            with pe.Fori(0, T // 4) as i:
                for u in range(2):
                    s = i * 2 + u
                    pe.wait_ge(staged, s + 1)
                    for v in range(2):
                        for k in range(KD):
                            m = pe.transpose(pt[u][:, v * KD + k, :], stage[:, u, v, k * P:(k + 1) * P], ident[:, :])
                    m.then_inc(turned, 1)
                    pe.wait_ge(oT_ok, s + 1)
                    pe.wait_ge(added, s + 1)
                    for v in range(2):
                        for k in range(KD):
                            m = pe.matmul(py[u][:, v, :], oT[:, u, v * KD + k, :], wp[:, k, :],
                                          start=(k == 0), stop=(k == KD - 1))
                    m.then_inc(done, 1)

        @block.scalar
        def _(act):
            with act.Fori(0, T // 4) as i:
                for u in range(2):
                    s = i * 2 + u
                    act.wait_ge(turned, s + 3)
                    act.activation(oT[:, u, :, :], pt[u][:, :, :], ACT.Copy).then_inc(oT_ok, 1)

        @block.vector
        def _(dve):
            dve.sem_inc(added, 2)
            with dve.Fori(0, T // 4) as i:
                for u in range(2):
                    s = i * 2 + u
                    dve.wait_ge(done, s + 1)
                    rows = y[:, bass.ds(s * 2, 2), :]
                    dve.tensor_tensor(rows, py[u][:, :, :], rows, ALU.add).then_inc(added, 1)


def layer1_experts(nc, w, gain, rows, outs, ident):
    FT = F1 // P
    STEPS = ROWS1 // SPAN
    PER = CAP // SPAN
    with ExitStack() as ctx:
        def sb(name, shape, dt=F32):
            return ctx.enter_context(nc.sbuf_tensor(f"e1_{name}", shape, dt))

        def ps(name, shape):
            return ctx.enter_context(nc.psum_tensor(f"e1_{name}", shape, F32))

        def sem(name):
            return ctx.enter_context(nc.semaphore(f"e1_{name}"))

        w1 = sb("w1", [P, 2, KD, F1])
        w2 = sb("w2", [P, 2, FT, D])
        b1_rows = sb("b1_rows", [E * FT, P])
        b1 = sb("b1", [P, E, FT])
        b2 = sb("b2", [P, 2, D])
        xg = sb("xg", [P, 2, SPAN // P, D])
        xT = sb("xT", [P, 2, KD, SPAN])
        hid = sb("hid", [P, FT, SPAN])
        yo = sb("yo", [P, 2, 2, D])
        px = [ps(f"px{k}", [P, SPAN]) for k in range(KD)]
        ph = [ps(f"ph{i}", [P, SPAN]) for i in range(2)]
        py = [ps(f"py{i}", [P, 2, D]) for i in range(2)]
        pb = ps("pb", [P, E * FT])
        b_in, b_turned, b_ok, x_turned, xT_ok, up_ok, hid_ok, y_done, y_ok, seen = (
            sem(n) for n in ("b_in", "b_turned", "b_ok", "x_turned", "xT_ok", "up_ok", "hid_ok", "y_done", "y_ok",
                             "seen"))
        w_in, x_in, stored = ([sem(f"{n}{i}") for i in range(2)] for n in ("w_in", "x_in", "stored"))
        block = ctx.enter_context(nc.Block())

        x_rows = tiles_of(rows)
        y_rows = tiles_of(outs)

        @block.sync
        def _(sp):
            def load_w(e, s):
                sp.dma_start(w1[:, s, :, :], w["L1_ffn_W1"][bass.ds(e, 1), :, :].rearrange("o (k p) n -> p (o k) n", p=P))\
                  .then_inc(w_in[s], 16)
                sp.dma_start(w2[:, s, :, :], w["L1_ffn_W2"][bass.ds(e, 1), :, :].rearrange("o (k p) n -> p (o k) n", p=P))\
                  .then_inc(w_in[s], 16)
                sp.dma_start(b2[:, s, :], w["L1_ffn_b2"][bass.ds(e, 1), :].broadcast_to([P, D])).then_inc(w_in[s], 16)

            def load_x(q, s):
                sp.dma_start(xg[:, s, :, :], x_rows[:, bass.ds(q * (SPAN // P), SPAN // P), :]).then_inc(x_in[s], 16)

            sp.dma_start(b1_rows[:, :], w["L1_ffn_b1"].rearrange("e (f p) -> (e f) p", p=P)).then_inc(b_in, 16)
            load_x(0, 0)
            load_w(0, 0)
            load_x(1, 1)
            load_w(1, 1)

            def store(q):
                for h in range(2):
                    sp.wait_ge(y_ok, 2 * q + h + 3)
                    sp.dma_start(y_rows[:, bass.ds(q * 4 + h * 2, 2), :], yo[:, h, :, :]).then_inc(stored[h], 16)

            def step(q, v, e, more_x, more_w):
                if more_x:
                    sp.wait_ge(x_turned, q + 1)
                    load_x(q + 2, v % 2)
                store(q)
                if v % PER == PER - 1 and more_w:
                    load_w(e + 2, v // PER)

            for s in stored:
                sp.sem_inc(s, 16)
            with sp.Fori(0, E // 2 - 1) as j:
                for v in range(4):
                    step(j * 4 + v, v, j * 2 + v // PER, True, True)
            for v in range(4):
                step(STEPS - 4 + v, v, E - 2 + v // PER, v < 2, False)
            for s in stored:
                sp.wait_ge(s, 16 * (STEPS + 1))

        @block.tensor
        def _(pe):
            def turn_x(q, s, n):
                pe.wait_ge(x_in[s], 16 * (n + 1))
                pe.wait_ge(xT_ok, q)
                for k in range(KD):
                    for t in range(SPAN // P):
                        m = pe.transpose(px[k][:, t * P:(t + 1) * P], xg[:, s, t, k * P:(k + 1) * P], ident[:, :])
                m.then_inc(x_turned, 1)

            def up(q, s, ws):
                pe.wait_ge(xT_ok, q + 1)
                for f in range(FT):
                    pe.wait_ge(hid_ok, q * FT + f + 1)
                    for k in range(KD):
                        m = pe.matmul(ph[f % 2][:, :], w1[:, ws, k, f * P:(f + 1) * P], xT[:, s, k, :],
                                      start=(k == 0), stop=(k == KD - 1))
                    m.then_inc(up_ok, 1)

            def down(q, ws):
                pe.wait_ge(hid_ok, (q + 1) * FT + 2)
                for h in range(2):
                    pe.wait_ge(y_ok, 2 * q + h + 1)
                    for v in range(2):
                        t = h * 2 + v
                        for f in range(FT):
                            m = pe.matmul(py[h][:, v, :], hid[:, f, t * P:(t + 1) * P], w2[:, ws, f, :],
                                          start=(f == 0), stop=(f == FT - 1))
                    m.then_inc(y_done, 1)

            def step(q, v, j, more):
                ws = v // PER
                if v % PER == 0:
                    pe.wait_ge(w_in[ws], 48 * (j + 1))
                up(q, v % 2, ws)
                if more:
                    turn_x(q + 1, (v + 1) % 2, j * 2 + (v + 1) // 2)
                down(q, ws)

            pe.wait_ge(b_in, 16)
            pe.transpose(pb[:, :], b1_rows[:, :], ident[0:E * FT, 0:E * FT]).then_inc(b_turned, 1)
            turn_x(0, 0, 0)
            steps(pe, step)

        @block.scalar
        def _(act):
            act.sem_inc(hid_ok, 2)

            def scale_x(q, s):
                act.wait_ge(x_turned, q + 1)
                for k in range(KD):
                    m = act.activation(xT[:, s, k, :], px[k][:, :], ACT.Identity, scale=gain[0][:, k:k + 1],
                                       bias=gain[1][:, k:k + 1])
                m.then_inc(xT_ok, 1)

            def step(q, v, j, more):
                for f in range(FT):
                    act.wait_ge(up_ok, q * FT + f + 1)
                    act.sem_inc(seen, 1)
                    act.activation(hid[:, f, :], ph[f % 2][:, :], ACT.Gelu,
                                   bias=b1[:, bass.ds(j * 2 + v // PER, 1), f:f + 1].rearrange("p o f -> p (o f)"))\
                       .then_inc(hid_ok, 1)
                if more:
                    scale_x(q + 1, (v + 1) % 2)

            act.wait_ge(b_ok, 1)
            scale_x(0, 0)
            steps(act, step)

        @block.vector
        def _(dve):
            dve.wait_ge(b_turned, 1)
            dve.tensor_copy(b1[:, :, :], pb[:, :].rearrange("p (e f) -> p e f", e=E)).then_inc(b_ok, 1)
            dve.sem_inc(y_ok, 2)

            def step(q, v, j, more):
                for h in range(2):
                    dve.wait_ge(y_done, 2 * q + h + 1)
                    dve.wait_ge(stored[h], 16 * (q + 1))
                    dve.tensor_tensor(yo[:, h, :, :], py[h][:, :, :],
                                      b2[:, v // PER, :].unsqueeze(1).broadcast_to([P, 2, D]), ALU.add).then_inc(y_ok, 1)
            steps(dve, step)


def steps(engine, step):
    with engine.Fori(0, E // 2 - 1) as j:
        for v in range(4):
            step(j * 4 + v, v, j, True)
    for v in range(4):
        step(E * 2 - 4 + v, v, E // 2 - 1, v < 3)


def load_gains(nc, ctx, w, ident):
    names = ("ln1_g", "ln1_b", "ln2_g", "ln2_b")
    cols = ctx.enter_context(nc.sbuf_tensor("gain_cols", [P, len(names) * KD], F32))
    with ExitStack() as inner:
        rows = inner.enter_context(nc.sbuf_tensor("gain_rows", [len(names) * KD, P], F32))
        turned = inner.enter_context(nc.psum_tensor("gain_turned", [P, len(names) * KD], F32))
        loaded, turned_ok = (inner.enter_context(nc.semaphore(f"gain_{n}")) for n in ("loaded", "turned_ok"))
        block = inner.enter_context(nc.Block())

        @block.sync
        def _(sp):
            for i, name in enumerate(names):
                sp.dma_start(rows[i * KD:(i + 1) * KD, :], w["L1_ffn_" + name].rearrange("(k p) -> k p", p=P))\
                  .then_inc(loaded, 16)

        @block.tensor
        def _(pe):
            pe.wait_ge(loaded, 16 * len(names))
            pe.transpose(turned[:, :], rows[:, :], ident[0:len(names) * KD, 0:len(names) * KD]).then_inc(turned_ok, 1)

        @block.vector
        def _(dve):
            dve.wait_ge(turned_ok, 1)
            dve.tensor_copy(cols[:, :], turned[:, :])
    cols = [cols[:, i * KD:(i + 1) * KD] for i in range(len(names))]
    return [(cols[0], cols[1]), (cols[2], cols[3])]


def build(nc, w, tables, out):
    with ExitStack() as ctx:
        def sb(name, shape, dt=F32):
            return ctx.enter_context(nc.sbuf_tensor(name, shape, dt))
        ident, zeros = sb("ident", [P, P]), sb("zeros", [P, D])
        flat = w["L0_attn_x"].rearrange("b l d -> (b l) d")
        result = out.rearrange("b l d -> (b l) d")
        rows = nc.dram_tensor("sorted_rows", (ROWS0, D), F32).ap()
        outs = nc.dram_tensor("expert_rows", (ROWS0, D), F32).ap()
        rows1 = nc.dram_tensor("sorted_rows1", (ROWS1, D), F32).ap()
        outs1 = nc.dram_tensor("expert_rows1", (ROWS1, D), F32).ap()
        x_kept2 = nc.dram_tensor("x_kept2", (N, D), F32).ap()
        x_kept = nc.dram_tensor("x_kept", (N, D), F32).ap()
        xT_dram = nc.dram_tensor("xT", (P, KD, N), F32).ap()
        setup_phase(nc, ident, zeros)
        with ExitStack() as s0:
            xn_a = s0.enter_context(nc.sbuf_tensor("xn_a", [P, T, D], F32))
            with ExitStack() as s1:
                x = s1.enter_context(nc.sbuf_tensor("x", [P, T, D], F32))
                y = s1.enter_context(nc.sbuf_tensor("y0", [P, T, D + 1], F32))
                r = make_router(nc, s1, ctx, "r0")
                with ExitStack() as s2:
                    xT = s2.enter_context(nc.sbuf_tensor("xT0", [P, KD, N], F32))
                    norm_phase(nc, "n0", x, ident, x_src=flat, xn=xn_a, xT_sb=xT, zero=(zeros, rows))
                    layer0_attention(nc, w, xn_a, xT, y, ident)
                    norm_phase(nc, "n1", x, ident, y=y, ysum=y[:, :, D], xn=xn_a, xT_sb=xT)
                    route_phase(nc, "r0", w["L0_ffn_gate_w"], True, xT, xn_a, ident, r, rows, None, shared=(w, y))
                layer0_experts(nc, w, r, rows, outs, ident)
                combine_phase(nc, "c0", r, outs, y)
                norm_phase(nc, "n2", x, ident, y=y, xn=xn_a, xT_dram=xT_dram, x_save=x_kept)
            clear_phase(nc)
            attention_phase(nc, "a1", True, ident, None, None, w=w, xT_dram=xT_dram, y=xn_a)
            gains = load_gains(nc, s0, w, ident)
            with ExitStack() as s1:
                qkv = s1.enter_context(nc.sbuf_tensor("qkv", [P, T, 3 * D], F32))
                with ExitStack() as s2:
                    hT = s2.enter_context(nc.sbuf_tensor("hT", [P, KD, N], F32))
                    with ExitStack() as s3:
                        x = s3.enter_context(nc.sbuf_tensor("x1", [P, T, D], F32))
                        norm_phase(nc, "n3", x, ident, y=xn_a, xn=xn_a, xT_sb=hT, twice=True, gain=gains[0],
                                   x_load=x_kept, x_save=x_kept2)
                    qkv_phase(nc, w, tables, hT, qkv)
                attention_phase(nc, "a2", False, ident, qkv, None)
                output_phase(nc, w, ident, qkv, xn_a)
            clear_phase(nc)
            with ExitStack() as s1:
                r = make_router(nc, s1, ctx, "r1")
                with ExitStack() as s2:
                    xT = s2.enter_context(nc.sbuf_tensor("xT1", [P, KD, N], F32))
                    h_raw = s2.enter_context(nc.sbuf_tensor("h_raw", [P, T, D], F32))
                    norm_phase(nc, "n4", None, ident, y=xn_a, residual=False, xn=h_raw, xT_sb=xT, gain=gains[1],
                               zero=(zeros, rows1))
                    route_phase(nc, "r1", w["L1_ffn_Wgate"], False, xT, h_raw, ident, r, rows1, CAP)
                layer1_experts(nc, w, gains[1], rows1, outs1, ident)
                combine_phase(nc, "c1", r, outs1, xn_a)
            with ExitStack() as s1:
                x = s1.enter_context(nc.sbuf_tensor("x2", [P, T, D], F32))
                norm_phase(nc, "n5", x, ident, y=xn_a, x_load=x_kept2, out_dst=result)


_SHAPES = {
    "L0_attn_x": (B, L, D), "L0_attn_Wq": (D, D), "L0_attn_Wk": (D, D), "L0_attn_Wv": (D, D),
    "L0_attn_proj": (D, PROJ), "L0_ffn_gate_w": (E, D), "L0_ffn_w_gate": (E, D, F0), "L0_ffn_w_up": (E, D, F0),
    "L0_ffn_w_down": (E, F0, D), "L0_ffn_sw_gate": (D, FS), "L0_ffn_sw_up": (D, FS), "L0_ffn_sw_down": (FS, D),
    "L1_attn_Wq": (D, HA * DK), "L1_attn_Wk": (D, HA * DK), "L1_attn_Wv": (D, HA * DK), "L1_attn_Wo": (HA * DK, D),
    "L1_ffn_ln1_g": (D,), "L1_ffn_ln1_b": (D,), "L1_ffn_Wqkv": (D, 3 * D), "L1_ffn_Wproj": (D, D),
    "L1_ffn_ln2_g": (D,), "L1_ffn_ln2_b": (D,), "L1_ffn_Wgate": (D, E), "L1_ffn_W1": (E, D, F1),
    "L1_ffn_b1": (E, F1), "L1_ffn_W2": (E, F1, D), "L1_ffn_b2": (E, D),
}


def kernel(**inputs):
    import concourse.bacc as bacc
    from concourse.bass_utils import run_bass_kernel_spmd

    nc = bacc.Bacc("TRN2", target_bir_lowering=False, num_devices=1)
    arrays = {f"in_{name}": np.ascontiguousarray(inputs[name]) for name in _SHAPES}
    w = {name: nc.dram_tensor(f"in_{name}", shape, F32, kind="ExternalInput").ap() for name, shape in _SHAPES.items()}
    out = nc.dram_tensor("out", (B, L, D), F32, kind="ExternalOutput").ap()
    inv_freq = np.float32(1.0) / np.float32(10000.0) ** (np.arange(0, HD, 2, dtype=np.float32) / np.float32(HD))
    angle = np.arange(L, dtype=np.float32)[:, None] * inv_freq
    arrays["cos"], arrays["sin"] = np.cos(angle), np.sin(angle)
    tables = [nc.dram_tensor(name, (L, HD // 2), F32, kind="ExternalInput").ap() for name in ("cos", "sin")]
    build(nc, w, tables, out)
    return run_bass_kernel_spmd(nc, [arrays], core_ids=[0]).results[0]["out"]
```

```python
from contextlib import ExitStack

import numpy as np

import concourse.bass as bass
from concourse import mybir

F32 = mybir.dt.float32
F32R = mybir.dt.float32r
BF16 = mybir.dt.bfloat16
I32 = mybir.dt.int32
U32 = mybir.dt.uint32
ALU = mybir.AluOpType
ACT = mybir.ActivationFunctionType
AX = mybir.AxisListType

P = 128
B, L, D = 4, 1024, 256
N = B * L
T = N // P
TB = L // P
KD = D // P
LN_EPS = 1e-5

PROJ = 64
ATT_EPS = 1e-8

E = 8
F0, FS = 352, 704
ROUTE_SCALE = 2.5
BLK0 = (2 * N + E * (P - 1)) // P

HA, DK = 16, 64
H1, HD = 16, 16
F1 = 4 * D
CAP = 2 * N // E


def tiles_of(rows):
    return rows.rearrange("(t p) w -> p t w", p=P)


def spread(ap, n):
    return ap.unsqueeze(2).broadcast_to([ap.shape[0], ap.shape[1], n])


class Chain:

    def __init__(self, engine, sem):
        self.engine, self.sem, self.n = engine, sem, 0

    def step(self, instruction):
        self.n += 1
        instruction.then_inc(self.sem, 1)
        self.engine.wait_ge(self.sem, self.n)


def row_stats(dve, link, st, mean, var, tmp):
    link(dve.tensor_tensor(tmp, st[:, :, 1], st[:, :, 4], ALU.subtract))
    link(dve.tensor_tensor(tmp, tmp, tmp, ALU.mult))
    link(dve.tensor_tensor(mean, st[:, :, 1], st[:, :, 4], ALU.add))
    link(dve.tensor_scalar(mean, mean, 0.5, None, ALU.mult))
    link(dve.tensor_tensor(var, st[:, :, 2], st[:, :, 5], ALU.add))
    link(dve.tensor_scalar(var, var, 1.0 / D, None, ALU.mult))
    link(dve.scalar_tensor_tensor(out=var, in0=tmp, scalar=0.25, in1=var, op0=ALU.mult, op1=ALU.add))


def refine_rstd(dve, link, rstd, root, var_eps, tmp):
    link(dve.reciprocal(rstd, root))
    link(dve.tensor_tensor(tmp, rstd, rstd, ALU.mult))
    link(dve.tensor_tensor(tmp, tmp, var_eps, ALU.mult))
    link(dve.tensor_scalar(tmp, tmp, -0.5, 1.5, ALU.mult, ALU.add))
    link(dve.tensor_tensor(rstd, rstd, tmp, ALU.mult))


def norm_phase(nc, tag, x, ident, y=None, ysum=None, x_src=None, residual=True, xn=None, xT_sb=None,
               xT_dram=None, twice=False, gain=None, out_dst=None, x_save=None, x_load=None, zero=None):
    last = out_dst is not None
    first = y is not None and residual
    src = x if residual else y
    ZEROS = 8
    with ExitStack() as ctx:
        def sb(name, shape, dt=F32):
            return ctx.enter_context(nc.sbuf_tensor(f"{tag}_{name}", shape, dt))

        def sem(name):
            return ctx.enter_context(nc.semaphore(f"{tag}_{name}"))

        st = sb("st", [P, T, 6])
        mean, var, root, rstd, rstd2, tmp, z = (
            sb(n, [P, T]) for n in ("mean", "var", "root", "rstd", "rstd2", "tmp", "z"))
        ring = sb("ring", [P, 2, 2, D])
        ot = sb("ot", [P, 2, KD, 2 * P]) if xT_dram is not None else None
        tp = [ctx.enter_context(nc.psum_tensor(f"{tag}_tp{i}", [P, KD, 2 * P], F32)) for i in range(2)]
        x_in, chain, var_ok, root_ok, stats_ok, applied, added, tile_ok, turned, moved, saved, cleared, seen = (
            sem(n) for n in ("x_in", "chain", "var_ok", "root_ok", "stats_ok", "applied", "added", "tile_ok",
                             "turned", "moved", "saved", "cleared", "seen"))
        stored = [sem(f"stored{i}") for i in range(2)]
        block = ctx.enter_context(nc.Block())
        n_roots = int(first) + (0 if last else 1) + int(twice)

        @block.sync
        def _(sp):
            if x_src is not None:
                sp.dma_start(x[:, :, :], tiles_of(x_src)).then_inc(x_in, 16)
            if zero is not None:
                zeros, rows = zero
                n_rows = rows.shape[0] // P
                for c in range(ZEROS):
                    a, z_end = n_rows * c // ZEROS, n_rows * (c + 1) // ZEROS
                    sp.dma_start(tiles_of(rows)[:, a:z_end, :],
                                 zeros[:, :].unsqueeze(1).broadcast_to([P, z_end - a, D])).then_inc(cleared, 16)
            if x_load is not None:
                sp.dma_start(x[:, :, :], tiles_of(x_load)).then_inc(x_in, 16)
            if x_save is not None:
                sp.wait_ge(added, T)
                sp.dma_start(tiles_of(x_save), x[:, :, :]).then_inc(saved, 16)
                sp.wait_ge(saved, 16)
            if xT_dram is not None:
                for q in stored:
                    sp.sem_inc(q, 16)
                with sp.Fori(0, T // 4) as i:
                    for u in range(2):
                        s = i * 2 + u
                        sp.wait_ge(moved, s + 3)
                        sp.dma_start(xT_dram[:, :, bass.ds(s * 2 * P, 2 * P)], ot[:, u, :, :]).then_inc(stored[u], 16)
                for q in stored:
                    sp.wait_ge(q, 16 + 16 * (T // 4))
            if last:
                for c in range(4):
                    sp.wait_ge(added, T // 4 * (c + 1))
                    sp.dma_start(tiles_of(out_dst)[:, T // 4 * c:T // 4 * (c + 1), :],
                                 x[:, T // 4 * c:T // 4 * (c + 1), :]).then_inc(saved, 16)
                sp.wait_ge(saved, 64)
            if zero is not None:
                sp.wait_ge(cleared, 16 * ZEROS)

        @block.vector
        def _(dve):
            link = Chain(dve, chain).step
            rounds = [0, 0]

            def stats(rows):
                with dve.Fori(0, T // 4) as i:
                    for u in range(4):
                        dve.bn_stats(st[:, i * 4 + u, :], rows[:, i * 4 + u, 0:D]).then_inc(stats_ok, 1)
                rounds[0] += 1
                dve.wait_ge(stats_ok, T * rounds[0])
                row_stats(dve, link, st, mean[:, :], var[:, :], tmp[:, :])

            def inverse_root(v, r):
                dve.tensor_scalar(v, v, LN_EPS, None, ALU.add).then_inc(var_ok, 1)
                rounds[1] += 1
                dve.wait_ge(var_ok, rounds[1])
                dve.wait_ge(root_ok, rounds[1])
                refine_rstd(dve, link, r, root[:, :], v, tmp[:, :])

            if x_src is not None or x_load is not None:
                dve.wait_ge(x_in, 16)
            if first:
                stats(y)
                if ysum is not None:
                    link(dve.tensor_scalar(z[:, :], ysum, ATT_EPS, None, ALU.add))
                    link(dve.reciprocal(z[:, :], z[:, :]))
                    link(dve.tensor_tensor(var[:, :], var[:, :], z[:, :], ALU.mult))
                    link(dve.tensor_tensor(var[:, :], var[:, :], z[:, :], ALU.mult))
                inverse_root(var[:, :], rstd[:, :])
                if ysum is not None:
                    link(dve.tensor_tensor(rstd[:, :], rstd[:, :], z[:, :], ALU.mult))
                with dve.Fori(0, T // 4) as i:
                    for u in range(4):
                        t = i * 4 + u
                        dve.tensor_scalar(y[:, t, 0:D], y[:, t, 0:D], mean[:, bass.ds(t, 1)],
                                          rstd[:, bass.ds(t, 1)], ALU.subtract, ALU.mult).then_inc(applied, 1)
                dve.wait_ge(applied, T)
                with dve.Fori(0, T // 4) as i:
                    for u in range(4):
                        t = i * 4 + u
                        dve.tensor_tensor(x[:, t, :], x[:, t, :], y[:, t, 0:D], ALU.add).then_inc(added, 1)
                dve.wait_ge(added, T)
            if last:
                return
            stats(src)
            inverse_root(var[:, :], rstd[:, :])
            if twice:
                link(dve.tensor_tensor(var[:, :], rstd[:, :], rstd[:, :], ALU.mult))
                link(dve.tensor_scalar(var[:, :], var[:, :], -LN_EPS, 1.0, ALU.mult, ALU.add))
                inverse_root(var[:, :], rstd2[:, :])
                link(dve.tensor_tensor(rstd2[:, :], rstd2[:, :], rstd[:, :], ALU.mult))
            for_turn = rstd2 if twice else rstd
            with dve.Fori(0, T // 4) as i:
                for u in range(2):
                    s = i * 2 + u
                    dve.wait_ge(turned, s + 1)
                    for v in range(2):
                        t = s * 2 + v
                        dve.tensor_scalar(ring[:, u, v, :], src[:, t, 0:D], mean[:, bass.ds(t, 1)],
                                          for_turn[:, bass.ds(t, 1)], ALU.subtract, ALU.mult).then_inc(tile_ok, 1)
                        dve.tensor_scalar(xn[:, t, :], src[:, t, 0:D], mean[:, bass.ds(t, 1)],
                                          rstd[:, bass.ds(t, 1)], ALU.subtract, ALU.mult)

        @block.scalar
        def _(act):
            if not last:
                act.sem_inc(moved, 2)
            for r in range(n_roots):
                act.wait_ge(var_ok, r + 1)
                act.activation(root[:, :], var[:, :], ACT.Sqrt).then_inc(root_ok, 1)
            if last:
                return
            with act.Fori(0, T // 4) as i:
                for u in range(2):
                    s = i * 2 + u
                    act.wait_ge(turned, s + 3)
                    if xT_dram is not None:
                        act.wait_ge(stored[u], 16 * (i + 1))
                    if gain is None:
                        dst = ot[:, u, :, :] if xT_dram is not None else xT_sb[:, :, bass.ds(s * 2 * P, 2 * P)]
                        act.activation(dst, tp[u][:, :, :], ACT.Copy).then_inc(moved, 1)
                    else:
                        act.sem_inc(seen, 1)
                        for k in range(KD):
                            m = act.activation(xT_sb[:, k, bass.ds(s * 2 * P, 2 * P)], tp[u][:, k, :], ACT.Identity,
                                               scale=gain[0][:, k:k + 1], bias=gain[1][:, k:k + 1])
                        m.then_inc(moved, 1)

        @block.tensor
        def _(pe):
            if last:
                return
            pe.sem_inc(turned, 2)
            with pe.Fori(0, T // 4) as i:
                for u in range(2):
                    s = i * 2 + u
                    pe.wait_ge(tile_ok, 2 * s + 2)
                    pe.wait_ge(moved, s + 1)
                    for k in range(KD):
                        for v in range(2):
                            m = pe.transpose(tp[u][:, k, v * P:(v + 1) * P], ring[:, u, v, k * P:(k + 1) * P],
                                             ident[:, :])
                    m.then_inc(turned, 1)


def setup_phase(nc, ident, zeros):
    with ExitStack() as ctx:
        made = ctx.enter_context(nc.semaphore("setup_made"))
        block = ctx.enter_context(nc.Block())

        @block.gpsimd
        def _(pool):
            pool.memset(zeros[:, :], 0.0)
            pool.memset(ident[:, :], 0.0).then_inc(made, 1)
            pool.wait_ge(made, 1)
            pool.affine_select(out=ident[:, :], in_=ident[:, :], compare_op=ALU.not_equal, fill=1.0, base=0,
                               pattern=[[-1, P]], channel_multiplier=1)


def layer0_attention(nc, w, xn, xT, y, ident):
    C = 512
    with ExitStack() as ctx:
        def sb(name, shape, dt=F32):
            return ctx.enter_context(nc.sbuf_tensor(f"a0_{name}", shape, dt))

        def ps(name, shape):
            return ctx.enter_context(nc.psum_tensor(f"a0_{name}", shape, F32))

        def sem(name):
            return ctx.enter_context(nc.semaphore(f"a0_{name}"))

        wq, wk, wv = (sb(n, [P, KD, D]) for n in ("wq", "wk", "wv"))
        proj = sb("proj", [P, KD, PROJ])
        map_w = sb("map_w", [P, KD, 2 * PROJ])
        wvT = sb("wvT", [P, KD, D])
        low = sb("low", [P, 2, C])
        fm = sb("fm", [P, 2, C])
        kt = sb("kt", [P, TB, PROJ])
        kx = sb("kx", [P, D])
        kxT = sb("kxT", [P, KD, PROJ])
        kv = sb("kv", [PROJ, D + 1])
        pre = [ps(f"pre{i}", [P, C]) for i in range(2)]
        turn = [ps(f"turn{i}", [P, 4, P]) for i in range(2)]
        small = ps("small", [P, 512])
        num = [ps(f"num{i}", [P, 512]) for i in range(2)]
        w_in, w_turned, w_ok, pre_ok, low_ok, exp_ok, fm_ok, turn_ok, kt_ok, mid, mid_ok, num_ok, y_ok, ones_ok = (
            sem(n) for n in ("w_in", "w_turned", "w_ok", "pre_ok", "low_ok", "exp_ok", "fm_ok", "turn_ok", "kt_ok",
                             "mid", "mid_ok", "num_ok", "y_ok", "ones_ok"))
        block = ctx.enter_context(nc.Block())

        @block.sync
        def _(sp):
            for dst, src in ((wq, w["L0_attn_Wq"]), (wk, w["L0_attn_Wk"]), (wv, w["L0_attn_Wv"]),
                             (proj, w["L0_attn_proj"])):
                sp.dma_start(dst[:, :, :], src.rearrange("(k p) n -> p k n", p=P)).then_inc(w_in, 16)

        @block.gpsimd
        def _(pool):
            pool.memset(kx[:, :], 0.0)
            pool.memset(kv[:, :], 1.0).then_inc(ones_ok, 1)

        @block.tensor
        def _(pe):
            pe.wait_ge(w_in, 64)
            for s, wt in enumerate((wq, wk)):
                for kd in range(KD):
                    for ke in range(KD):
                        pe.matmul(turn[0][:, s * KD + kd, 0:PROJ], wt[:, ke, kd * P:(kd + 1) * P], proj[:, ke, :],
                                  start=(ke == 0), stop=(ke == KD - 1))
            for ke in range(KD):
                for kd in range(KD):
                    m = pe.transpose(turn[1][:, ke * KD + kd, :], wv[:, kd, ke * P:(ke + 1) * P], ident[:, :])
            m.then_inc(w_turned, 1)
            pe.wait_ge(w_ok, 2)
            with pe.Fori(0, B) as b:
                for c in range(2):
                    for k in range(KD):
                        m = pe.matmul(pre[c][:, :], map_w[:, k, :], xT[:, k, bass.ds(b * L + c * C, C)],
                                      start=(k == 0), stop=(k == KD - 1))
                    m.then_inc(pre_ok, 1)
                for c in range(2):
                    pe.wait_ge(fm_ok, b * 2 + c + 1)
                    for t in range(4):
                        m = pe.transpose(turn[c][:, t, :], fm[:, c, t * P:(t + 1) * P], ident[:, :])
                    m.then_inc(turn_ok, 1)
                pe.wait_ge(kt_ok, b * 2 + 2)
                for t in range(TB):
                    m = pe.matmul(small[0:PROJ, 0:D], kt[:, t, :], xn[:, b * TB + t, :],
                                  start=(t == 0), stop=(t == TB - 1))
                m.then_inc(mid, 1)
                pe.wait_ge(mid_ok, b * 3 + 1)
                for k in range(KD):
                    m = pe.transpose(small[:, k * P:(k + 1) * P], kx[:, k * P:(k + 1) * P], ident[:, :])
                m.then_inc(mid, 1)
                pe.wait_ge(mid_ok, b * 3 + 2)
                for k in range(KD):
                    m = pe.matmul(small[0:PROJ, 0:D], kxT[:, k, :], wvT[:, k, :], start=(k == 0), stop=(k == KD - 1))
                m.then_inc(mid, 1)
                pe.wait_ge(mid_ok, b * 3 + 3)
                for t in range(TB):
                    pe.wait_ge(y_ok, b * TB + t + 1)
                    pe.matmul(num[t % 2][:, 0:D + 1], fm[0:PROJ, t // 4, t % 4 * P:(t % 4 + 1) * P], kv[:, :],
                              start=True, stop=True).then_inc(num_ok, 1)

        @block.vector
        def _(dve):
            dve.wait_ge(w_turned, 1)
            dve.tensor_copy(map_w[:, :, 0:PROJ], turn[0][:, 0:2, 0:PROJ])
            dve.tensor_copy(map_w[:, :, PROJ:2 * PROJ], turn[0][:, 2:4, 0:PROJ]).then_inc(w_ok, 1)
            dve.tensor_copy(wvT[:, :, :], turn[1][:, :, :].rearrange("p (k c) n -> p k (c n)", k=KD)).then_inc(w_ok, 1)
            dve.wait_ge(ones_ok, 1)
            with dve.Fori(0, B) as b:
                for c in range(2):
                    dve.wait_ge(pre_ok, b * 2 + c + 1)
                    dve.tensor_scalar(low[:, c, :], pre[c][:, :], 0.0, None, ALU.min).then_inc(low_ok, 1)
                for c in range(2):
                    dve.wait_ge(exp_ok, b * 2 + c + 1)
                    if c == 0:
                        dve.wait_ge(num_ok, b * TB)
                    dve.scalar_tensor_tensor(out=fm[:, c, :], in0=pre[c][:, :], scalar=0.0, in1=low[:, c, :],
                                             op0=ALU.max, op1=ALU.add).then_inc(fm_ok, 1)
                for c in range(2):
                    dve.wait_ge(turn_ok, b * 2 + c + 1)
                    dve.tensor_copy(kt[:, c * 4:c * 4 + 4, :], turn[c][:, :, PROJ:2 * PROJ]).then_inc(kt_ok, 1)
                dve.wait_ge(mid, b * 3 + 1)
                dve.tensor_copy(kx[0:PROJ, :], small[0:PROJ, 0:D]).then_inc(mid_ok, 1)
                dve.wait_ge(mid, b * 3 + 2)
                dve.tensor_copy(kxT[:, :, :], small[:, 0:KD * P].rearrange("p (k n) -> p k n", k=KD)[:, :, 0:PROJ])\
                   .then_inc(mid_ok, 1)
                dve.wait_ge(mid, b * 3 + 3)
                dve.tensor_copy(kv[:, 0:D], small[0:PROJ, 0:D]).then_inc(mid_ok, 1)

        @block.scalar
        def _(act):
            act.sem_inc(y_ok, 2)
            with act.Fori(0, B) as b:
                for c in range(2):
                    act.wait_ge(low_ok, b * 2 + c + 1)
                    act.activation(low[:, c, :], low[:, c, :], ACT.Exp).then_inc(exp_ok, 1)
                for t in range(TB):
                    act.wait_ge(num_ok, b * TB + t + 1)
                    act.activation(y[:, b * TB + t, :], num[t % 2][:, 0:D + 1], ACT.Copy).then_inc(y_ok, 1)


def clear_phase(nc):
    spent = sorted(nc.released_uncleared_semaphores)
    with nc.Block() as block:

        @block.gpsimd
        def _(pool):
            start = 0
            for i in range(1, len(spent) + 1):
                if i == len(spent) or spent[i] != spent[i - 1] + 1:
                    pool.sem_clear(range(spent[start], spent[i - 1] + 1))
                    start = i


ROWS0 = (BLK0 + 1) // 2 * 2 * P
BLOCKS0 = ROWS0 // P
ROWS1 = E * CAP
FETCHES = 4
FAR = 1 << 20


def make_router(nc, ctx, whole, tag):
    def sem(name):
        return whole.enter_context(nc.semaphore(f"{tag}_{name}"))

    def sb(name, shape, dt=F32):
        return ctx.enter_context(nc.sbuf_tensor(f"{tag}_{name}", shape, dt))
    return {"put": [sb(f"put{i}", [P, T], U32) for i in range(2)],
            "take": [sb(f"take{i}", [P, T], U32) for i in range(2)],
            "weight": [sb(f"weight{i}", [P, T]) for i in range(2)],
            "expert": sb("expert", [P, BLOCKS0], I32),
            "scattered": sem("scattered"),
            "fetched": [[sem(f"fetched{u}_{i}") for i in range(2)] for u in range(FETCHES)]}


def route_phase(nc, tag, gate, gate_is_rows, xT, xn, ident, r, rows, capacity, shared=None):
    C = 512
    FT = (FS + P - 1) // P
    n_chunks = N // C
    with ExitStack() as ctx:
        def sb(name, shape, dt=F32):
            return ctx.enter_context(nc.sbuf_tensor(f"{tag}_{name}", shape, dt))

        def ps(name, shape):
            return ctx.enter_context(nc.psum_tensor(f"{tag}_{name}", shape, F32))

        def sem(name):
            return ctx.enter_context(nc.semaphore(f"{tag}_{name}"))

        gw = sb("gw", [P, KD, E])
        gw_rows = sb("gw_rows", [E, D])
        logT = sb("logT", [E, 2, C])
        s, one, two, mask, work, offs = (sb(n, [P, T, E]) for n in ("s", "one", "two", "mask", "work", "offs"))
        rank = sb("rank", [P, T, E])
        col, m1, m2, keep = (sb(n, [P, T]) for n in ("col", "m1", "m2", "keep"))
        before = sb("before", [P, P])
        ones = sb("ones", [P, P])
        count, blocks, end, end2 = (sb(n, [P, E]) for n in ("count", "blocks", "end", "end2"))
        edge = sb("edge", [P, E, T])
        cmp = sb("cmp", [P, E, T])
        slot_no = sb("slot_no", [P, BLOCKS0, E])
        cmp2 = sb("cmp2", [P, BLOCKS0, E])
        base = sb("base", [P, E])
        expert_f = sb("expert_f", [P, BLOCKS0])
        pl = ps("pl", [P, 512])
        pt = ps("pt", [P, T, E])
        pc = ps("pc", [P, 2, T * E])
        (w_in, gw_turned, gw_ok, log_ok, logs_in, turned, made, chain, low_ok, exp_ok, mask_ok, counted, slots_ok,
         sh_in, up_ok, silu_ok, hid_ok, down_ok, out_ok) = (sem(n) for n in (
             "w_in", "gw_turned", "gw_ok", "log_ok", "logs_in", "turned", "made", "chain", "low_ok", "exp_ok",
             "mask_ok", "counted", "slots_ok", "sh_in", "up_ok", "silu_ok", "hid_ok", "down_ok",
             "out_ok"))
        padded = sem("padded")
        if shared is not None:
            sw, y = shared
            wg, wu = (sb(n, [P, KD, FT * P]) for n in ("wg", "wu"))
            wd = sb("wd", [P, FT, D])
            act_g = sb("act_g", [P, 2, C])
            hid = sb("hid", [P, FT, C])
            pg = [ps(f"pg{i}", [P, C]) for i in range(2)]
            pu = [ps(f"pu{i}", [P, C]) for i in range(2)]
            pd = ps("pd", [P, 2, D])
        block = ctx.enter_context(nc.Block())

        def shared_up(pe, c):
            if isinstance(c, int):
                pe.wait_ge(sh_in, 64)
            for f in range(FT):
                q = c * FT + f
                pe.wait_ge(hid_ok, q + 1)
                for wt, pp in ((wg, pg), (wu, pu)):
                    for k in range(KD):
                        m = pe.matmul(pp[f % 2][:, :], wt[:, k, f * P:(f + 1) * P],
                                      xT[:, k, bass.ds(c * C, C)], start=(k == 0), stop=(k == KD - 1))
                m.then_inc(up_ok, 1)

        def shared_down(pe, c):
            pe.wait_ge(hid_ok, (c + 1) * FT + 2)
            for h in range(C // P // 2):
                pe.wait_ge(out_ok, c * 2 + h)
                for v in range(2):
                    for f in range(FT):
                        t = h * 2 + v
                        m = pe.matmul(pd[:, v, :], hid[:, f, t * P:(t + 1) * P], wd[:, f, :],
                                      start=(f == 0), stop=(f == FT - 1))
                m.then_inc(down_ok, 1)

        def shared_act(act, c):
            for f in range(FT):
                q = c * FT + f
                act.wait_ge(up_ok, q + 1)
                act.wait_ge(hid_ok, q + 1)
                act.activation(act_g[:, f % 2, :], pg[f % 2][:, :], ACT.Silu).then_inc(silu_ok, 1)
            for h in range(C // P // 2):
                act.wait_ge(down_ok, c * 2 + h + 1)
                act.activation(y[:, bass.ds(c * (C // P) + h * 2, 2), 0:D], pd[:, :, :], ACT.Copy).then_inc(out_ok, 1)

        def shared_mul(dve, c):
            for f in range(FT):
                q = c * FT + f
                dve.wait_ge(silu_ok, q + 1)
                if f == 0:
                    dve.wait_ge(down_ok, c * 2)
                dve.tensor_tensor(hid[:, f, :], act_g[:, f % 2, :], pu[f % 2][:, :], ALU.mult)\
                   .then_inc(hid_ok, 1)

        @block.sync
        def _(sp):
            if gate_is_rows:
                sp.dma_start(gw_rows[:, :], gate).then_inc(w_in, 16)
            else:
                sp.dma_start(gw[:, :, :], gate.rearrange("(k p) e -> p k e", p=P)).then_inc(w_in, 16)
            if shared is not None:
                for dst, name in ((wg, "L0_ffn_sw_gate"), (wu, "L0_ffn_sw_up")):
                    sp.dma_start(dst[:, :, 0:FS], sw[name].rearrange("(k p) n -> p k n", p=P)).then_inc(sh_in, 16)
                full, rest = FS // P, FS % P
                sp.wait_ge(padded, 1)
                sp.dma_start(wd[:, 0:full, :], sw["L0_ffn_sw_down"][0:full * P, :].rearrange("(k p) n -> p k n", p=P))\
                  .then_inc(sh_in, 16)
                sp.dma_start(wd[0:rest, full, :], sw["L0_ffn_sw_down"][full * P:FS, :]).then_inc(sh_in, 16)

        @block.tensor
        def _(pe):
            pe.wait_ge(w_in, 16)
            if gate_is_rows:
                for k in range(KD):
                    m = pe.transpose(pl[:, k * E:(k + 1) * E], gw_rows[:, k * P:(k + 1) * P], ident[0:E, 0:E])
                m.then_inc(gw_turned, 1)
                pe.wait_ge(gw_ok, 1)
            for c in range(n_chunks):
                if c >= 1:
                    pe.wait_ge(log_ok, c)
                for k in range(KD):
                    m = pe.matmul(pl[0:E, :], gw[:, k, :], xT[:, k, c * C:(c + 1) * C],
                                  start=(k == 0), stop=(k == KD - 1))
                m.then_inc(logs_in, 1)
                pe.wait_ge(log_ok, c + 1)
                for t in range(C // P):
                    m = pe.transpose(pt[:, c * (C // P) + t, :], logT[:, c % 2, t * P:(t + 1) * P], ident[0:E, 0:E])
                m.then_inc(turned, 1)
            if shared is not None:
                shared_up(pe, 0)
                shared_down(pe, 0)
            pe.wait_ge(mask_ok, 1)
            pe.wait_ge(made, 3)
            pe.matmul(pc[:, 0, :], before[:, :], mask[:, :, :].rearrange("p t e -> p (t e)"), start=True, stop=True)
            pe.matmul(pc[:, 1, :], ones[:, :], mask[:, :, :].rearrange("p t e -> p (t e)"),
                      start=True, stop=True).then_inc(counted, 1)
            if shared is not None:
                with pe.Fori(1, n_chunks) as c:
                    shared_up(pe, c)
                    shared_down(pe, c)

        @block.scalar
        def _(act):
            for c in range(n_chunks):
                act.wait_ge(logs_in, c + 1)
                if c >= 2:
                    act.wait_ge(turned, c - 1)
                act.activation(logT[:, c % 2, :], pl[0:E, :], ACT.Copy).then_inc(log_ok, 1)
            if shared is not None:
                shared_act(act, 0)
            act.wait_ge(low_ok, 1)
            act.activation(s[:, :, :], s[:, :, :], ACT.Exp).then_inc(exp_ok, 1)
            if shared is not None:
                with act.Fori(1, n_chunks) as c:
                    shared_act(act, c)

        @block.vector
        def _(dve):
            link = Chain(dve, chain).step
            if shared is not None:
                dve.sem_inc(hid_ok, 2)
            if gate_is_rows:
                dve.wait_ge(gw_turned, 1)
                dve.tensor_copy(gw[:, :, :], pl[:, 0:KD * E].rearrange("p (k e) -> p k e", k=KD)).then_inc(gw_ok, 1)
            dve.wait_ge(turned, n_chunks)
            link(dve.tensor_reduce(col[:, :], pt[:, :, :], AX.X, ALU.max))
            dve.tensor_tensor(s[:, :, :], pt[:, :, :], spread(col[:, :], E), ALU.subtract).then_inc(low_ok, 1)
            if shared is not None:
                shared_mul(dve, 0)
            dve.wait_ge(exp_ok, 1)
            link(dve.tensor_reduce(col[:, :], s[:, :, :], AX.X, ALU.add))
            link(dve.reciprocal(col[:, :], col[:, :]))
            link(dve.tensor_tensor(s[:, :, :], s[:, :, :], spread(col[:, :], E), ALU.mult))
            dve.wait_ge(made, 3)

            def pick(best, hot):
                link(dve.tensor_reduce(best[:, :], s[:, :, :], AX.X, ALU.max))
                link(dve.tensor_tensor(work[:, :, :], s[:, :, :], spread(best[:, :], E), ALU.is_ge))
                link(dve.tensor_tensor(work[:, :, :], work[:, :, :], rank[:, :, :], ALU.mult))
                link(dve.tensor_reduce(col[:, :], work[:, :, :], AX.X, ALU.max))
                link(dve.tensor_tensor(hot[:, :, :], work[:, :, :], spread(col[:, :], E), ALU.is_equal))

            pick(m1, one)
            link(dve.scalar_tensor_tensor(out=s[:, :, :], in0=one[:, :, :], scalar=-2.0, in1=s[:, :, :],
                                          op0=ALU.mult, op1=ALU.add))
            pick(m2, two)
            dve.tensor_tensor(mask[:, :, :], one[:, :, :], two[:, :, :], ALU.add).then_inc(mask_ok, 1)
            dve.wait_ge(counted, 1)
            whole = pc[:, 1, :].rearrange("p (t e) -> p t e", e=E)
            link(dve.tensor_copy(work[:, :, :], whole))
            a, b2 = work, s
            step = 1
            while step < T:
                dve.tensor_copy(b2[:, 0:step, :], a[:, 0:step, :])
                link(dve.tensor_tensor(b2[:, step:T, :], a[:, step:T, :], a[:, 0:T - step, :], ALU.add))
                a, b2 = b2, a
                step *= 2
            link(dve.tensor_copy(count[:, :], a[:, T - 1, :]))
            link(dve.tensor_tensor(offs[:, :, :], a[:, :, :], whole, ALU.subtract))
            link(dve.tensor_tensor(offs[:, :, :], offs[:, :, :], pc[:, 0, :].rearrange("p (t e) -> p t e", e=E),
                                   ALU.add))
            if capacity is None:
                link(dve.tensor_tensor(cmp[:, :, :], spread(count[:, :], T), edge[:, :, :], ALU.is_gt))
                link(dve.tensor_reduce(blocks[:, :], cmp[:, :, :], AX.X, ALU.add))
                a2, b3 = end, end2
                link(dve.tensor_copy(a2[:, :], blocks[:, :]))
                step = 1
                while step < E:
                    dve.tensor_copy(b3[:, 0:step], a2[:, 0:step])
                    link(dve.tensor_tensor(b3[:, step:E], a2[:, step:E], a2[:, 0:E - step], ALU.add))
                    a2, b3 = b3, a2
                    step *= 2
                link(dve.tensor_tensor(base[:, :], a2[:, :], blocks[:, :], ALU.subtract))
                link(dve.tensor_scalar(base[:, :], base[:, :], float(P), None, ALU.mult))
                link(dve.tensor_tensor(cmp2[:, :, :], slot_no[:, :, :],
                                       a2[:, :].unsqueeze(1).broadcast_to([P, BLOCKS0, E]), ALU.is_ge))
                link(dve.tensor_reduce(expert_f[:, :], cmp2[:, :, :], AX.X, ALU.add))
                dve.tensor_scalar(r["expert"][:, :], expert_f[:, :], float(E - 1), None, ALU.min)
            hots = ((one, m1, 0), (two, m2, 1))
            if capacity is not None:
                for hot, best, i in hots:
                    link(dve.tensor_tensor(work[:, :, :], offs[:, :, :], hot[:, :, :], ALU.mult))
                    link(dve.tensor_reduce(keep[:, :], work[:, :, :], AX.X, ALU.add))
                    link(dve.tensor_scalar(keep[:, :], keep[:, :], float(capacity), None, ALU.is_lt))
                    link(dve.tensor_tensor(r["weight"][i][:, :], best[:, :], keep[:, :], ALU.mult))
                    link(dve.tensor_tensor(work[:, :, :], offs[:, :, :],
                                           base[:, :].unsqueeze(1).broadcast_to([P, T, E]), ALU.add))
                    link(dve.tensor_tensor(work[:, :, :], work[:, :, :], hot[:, :, :], ALU.mult))
                    link(dve.tensor_reduce(col[:, :], work[:, :, :], AX.X, ALU.add))
                    link(dve.tensor_tensor(col[:, :], col[:, :], keep[:, :], ALU.mult))
                    dve.tensor_copy(r["take"][i][:, :], col[:, :])
                    link(dve.tensor_scalar(keep[:, :], keep[:, :], -float(FAR), float(FAR), ALU.mult, ALU.add))
                    dve.tensor_tensor(r["put"][i][:, :], col[:, :], keep[:, :], ALU.add).then_inc(slots_ok, 1)
                    dve.wait_ge(slots_ok, i + 1)
            else:
                link(dve.tensor_tensor(offs[:, :, :], offs[:, :, :],
                                       base[:, :].unsqueeze(1).broadcast_to([P, T, E]), ALU.add))
                for hot, best, i in hots:
                    link(dve.tensor_tensor(work[:, :, :], offs[:, :, :], hot[:, :, :], ALU.mult))
                    link(dve.tensor_reduce(col[:, :], work[:, :, :], AX.X, ALU.add))
                    dve.tensor_copy(r["take"][i][:, :], col[:, :])
                    dve.tensor_copy(r["put"][i][:, :], col[:, :]).then_inc(slots_ok, 1)
                    dve.wait_ge(slots_ok, i + 1)
            if capacity is None:
                link(dve.tensor_tensor(col[:, :], m1[:, :], m2[:, :], ALU.add))
                link(dve.tensor_scalar(col[:, :], col[:, :], 1e-20, None, ALU.add))
                link(dve.reciprocal(col[:, :], col[:, :]))
                link(dve.tensor_scalar(col[:, :], col[:, :], ROUTE_SCALE, None, ALU.mult))
                for best, i in ((m1, 0), (m2, 1)):
                    dve.tensor_tensor(r["weight"][i][:, :], best[:, :], col[:, :], ALU.mult)
            if shared is not None:
                with dve.Fori(1, n_chunks) as c:
                    shared_mul(dve, c)

        @block.gpsimd
        def _(pool):
            if shared is not None:
                pool.memset(wg[:, :, FS:FT * P], 0.0)
                pool.memset(wu[:, :, FS:FT * P], 0.0)
                pool.memset(wd[:, FT - 1, :], 0.0).then_inc(padded, 1)
            pool.iota(rank[:, :, :], pattern=[[0, T], [-1, E]], base=E, channel_multiplier=0,
                      allow_small_or_imprecise_dtypes=True)
            pool.iota(edge[:, :, :], pattern=[[0, E], [P, T]], base=0, channel_multiplier=0,
                      allow_small_or_imprecise_dtypes=True)
            pool.iota(slot_no[:, :, :], pattern=[[1, BLOCKS0], [0, E]], base=0, channel_multiplier=0,
                      allow_small_or_imprecise_dtypes=True)
            if capacity is not None:
                pool.iota(base[:, :], pattern=[[capacity, E]], base=0, channel_multiplier=0,
                          allow_small_or_imprecise_dtypes=True)
            pool.memset(ones[:, :], 1.0)
            pool.memset(before[:, :], 1.0).then_inc(made, 2)
            pool.wait_ge(made, 2)
            pool.affine_select(out=before[:, :], in_=before[:, :], compare_op=ALU.is_gt, fill=0.0, base=0,
                               pattern=[[1, P]], channel_multiplier=-1).then_inc(made, 1)
            for i in range(2):
                pool.wait_ge(slots_ok, i + 1)
                for t in range(T):
                    pool.indirect_dma_start(rows[:, :], bass.IndirectOffsetOnAxis(ap=r["put"][i][:, t:t + 1], axis=0),
                                            xn[:, t, :], None, bounds_check=rows.shape[0] - 1, oob_is_err=False)\
                        .then_inc(r["scattered"], 16)
            pool.wait_ge(r["scattered"], 16 * 2 * T)


def layer0_experts(nc, w, r, rows, outs, ident):
    FT = (F0 + P - 1) // P
    with ExitStack() as ctx:
        def sb(name, shape, dt=F32):
            return ctx.enter_context(nc.sbuf_tensor(f"e0_{name}", shape, dt))

        def ps(name, shape):
            return ctx.enter_context(nc.psum_tensor(f"e0_{name}", shape, F32))

        def sem(name):
            return ctx.enter_context(nc.semaphore(f"e0_{name}"))

        wg, wu = (sb(n, [P, KD, E * F0]) for n in ("wg", "wu"))
        wd = sb("wd", [P, FT, E * D])
        xg = sb("xg", [P, 2, D])
        xgT = sb("xgT", [P, 2, KD, P])
        sg = sb("sg", [P, 2, F0])
        h = sb("h", [P, 2, F0])
        hT = sb("hT", [P, 2, FT, P])
        yo = sb("yo", [P, 2, D])
        px = ps("px", [P, KD, P])
        pg = [ps(f"pg{i}", [P, 512]) for i in range(2)]
        pu = [ps(f"pu{i}", [P, 512]) for i in range(2)]
        ph = ps("ph", [P, FT, P])
        py = ps("py", [P, D])
        w_in, x_turned, xT_ok, up_ok, silu_ok, h_ok, h_turned, hT_ok, y_done, y_ok = (
            sem(n) for n in ("w_in", "x_turned", "xT_ok", "up_ok", "silu_ok", "h_ok", "h_turned", "hT_ok",
                             "y_done", "y_ok"))
        x_in, stored = ([sem(f"{n}{i}") for i in range(2)] for n in ("x_in", "stored"))
        block = ctx.enter_context(nc.Block())

        def width(f):
            return min(P, F0 - f * P)

        def walk(engine, head, step, tail):
            head()
            with engine.Fori(0, (BLOCKS0 - 2) // 2) as i:
                step(i * 2 + 1, 1, i, i)
                step(i * 2 + 2, 0, i + 1, i)
            step(BLOCKS0 - 1, 1, BLOCKS0 // 2 - 1, BLOCKS0 // 2 - 1)
            tail()

        @block.sync
        def _(sp):
            x_rows = rows.rearrange("(j p) d -> j p d", p=P)
            y_rows = outs.rearrange("(j p) d -> j p d", p=P)

            def load(j, slot):
                sp.wait_ge(x_turned, j + 1)
                sp.dma_start(xg[:, slot, :], x_rows[bass.ds(j, 1), :, :].rearrange("o p d -> p (o d)"))\
                  .then_inc(x_in[slot], 16)

            def store(j, slot):
                sp.wait_ge(y_ok, j + 1)
                sp.dma_start(y_rows[bass.ds(j, 1), :, :].rearrange("o p d -> p (o d)"), yo[:, slot, :])\
                  .then_inc(stored[slot], 16)

            load(0, 0)
            for dst, name, width_all in ((wg, "L0_ffn_w_gate", D), (wu, "L0_ffn_w_up", D), (wd, "L0_ffn_w_down", F0)):
                for k in range((width_all + P - 1) // P):
                    n = min(P, width_all - k * P)
                    sp.dma_start(dst[0:n, k, :].rearrange("p (e n) -> p e n", e=E),
                                 w[name][:, k * P:k * P + n, :].rearrange("e p n -> p e n")).then_inc(w_in, 16)

            def step(j, slot, n, m):
                load(j, slot)
                store(j - 1, 1 - slot)
            for q in stored:
                sp.sem_inc(q, 16)
            walk(sp, lambda: None, step, lambda: store(BLOCKS0 - 1, 1))
            for q in stored:
                sp.wait_ge(q, 16 * (BLOCKS0 // 2 + 1))

        @block.tensor
        def _(pe):
            pe.sem_inc(x_turned, 2)

            def turn_x(j, slot, n):
                pe.wait_ge(x_in[slot], 16 * (n + 1))
                pe.wait_ge(xT_ok, j)
                for k in range(KD):
                    m = pe.transpose(px[:, k, :], xg[:, slot, k * P:(k + 1) * P], ident[:, :])
                m.then_inc(x_turned, 1)

            def up(j, slot):
                e = pe.value_load(r["expert"][0:1, bass.ds(j, 1)], min_val=0, max_val=E - 1)
                pe.wait_ge(xT_ok, j + 1)
                pe.wait_ge(h_ok, j + 1)
                for wt, pp in ((wg, pg), (wu, pu)):
                    for k in range(KD):
                        m = pe.matmul(pp[slot][:, 0:F0], xgT[:, slot, k, :], wt[:, k, bass.ds(e * F0, F0)],
                                      start=(k == 0), stop=(k == KD - 1))
                m.then_inc(up_ok, 1)
                return e

            def down(j, slot):
                e = pe.value_load(r["expert"][0:1, bass.ds(j, 1)], min_val=0, max_val=E - 1)
                pe.wait_ge(h_ok, j + 3)
                for f in range(FT):
                    n = width(f)
                    m = pe.transpose(ph[0:n, f, :], h[:, slot, f * P:f * P + n], ident[:, :])
                m.then_inc(h_turned, 1)
                pe.wait_ge(hT_ok, j + 1)
                pe.wait_ge(y_ok, j)
                for f in range(FT):
                    n = width(f)
                    m = pe.matmul(py[:, :], hT[0:n, slot, f, :], wd[0:n, f, bass.ds(e * D, D)],
                                  start=(f == 0), stop=(f == FT - 1))
                m.then_inc(y_done, 1)

            def head():
                turn_x(0, 0, 0)
                pe.wait_ge(w_in, 16 * (2 * KD + FT))
                up(0, 0)

            def step(j, slot, n, m):
                turn_x(j, slot, n)
                up(j, slot)
                down(j - 1, 1 - slot)
            walk(pe, head, step, lambda: down(BLOCKS0 - 1, 1))

        @block.scalar
        def _(act):
            def xT(j, slot):
                act.wait_ge(x_turned, j + 3)
                act.activation(xgT[:, slot, :, :], px[:, :, :], ACT.Copy).then_inc(xT_ok, 1)

            def silu(j, slot):
                act.wait_ge(up_ok, j + 1)
                act.activation(sg[:, slot, :], pg[slot][:, 0:F0], ACT.Silu).then_inc(silu_ok, 1)

            def y(j, slot, n):
                act.wait_ge(y_done, j + 1)
                act.wait_ge(stored[slot], 16 * (n + 1))
                act.activation(yo[:, slot, :], py[:, :], ACT.Copy).then_inc(y_ok, 1)

            def head():
                xT(0, 0)
                silu(0, 0)

            def step(j, slot, n, m):
                xT(j, slot)
                silu(j, slot)
                y(j - 1, 1 - slot, m)
            walk(act, head, step, lambda: y(BLOCKS0 - 1, 1, BLOCKS0 // 2 - 1))

        @block.vector
        def _(dve):
            dve.sem_inc(h_ok, 2)

            def hidden(j, slot):
                dve.wait_ge(silu_ok, j + 1)
                dve.tensor_tensor(h[:, slot, :], sg[:, slot, :], pu[slot][:, 0:F0], ALU.mult).then_inc(h_ok, 1)

            def hiddenT(j, slot):
                dve.wait_ge(h_turned, j + 1)
                full = F0 // P
                dve.tensor_copy(hT[:, slot, 0:full, :], ph[:, 0:full, :])
                dve.tensor_copy(hT[0:width(full), slot, full, :], ph[0:width(full), full, :]).then_inc(hT_ok, 1)

            def step(j, slot, n, m):
                hiddenT(j - 1, 1 - slot)
                hidden(j, slot)
            walk(dve, lambda: hidden(0, 0), step, lambda: hiddenT(BLOCKS0 - 1, 1))


def combine_phase(nc, tag, r, outs, y, base_rows=None):
    R, fetched = FETCHES, r["fetched"]
    with ExitStack() as ctx:
        got = ctx.enter_context(nc.sbuf_tensor(f"{tag}_got", [P, R, 2, D], F32))
        added = ctx.enter_context(nc.semaphore(f"{tag}_added"))
        block = ctx.enter_context(nc.Block())

        @block.gpsimd
        def _(pool):
            for t in range(T):
                if t >= R:
                    pool.wait_ge(added, 2 * (t - R + 1))
                for i in range(2):
                    pool.indirect_dma_start(got[:, t % R, i, :], None, outs[:, :],
                                            bass.IndirectOffsetOnAxis(ap=r["take"][i][:, t:t + 1], axis=0))\
                        .then_inc(fetched[t % R][i], 16)

        @block.vector
        def _(dve):
            with dve.Fori(0, T // R) as g:
                for u in range(R):
                    t = g * R + u
                    for i in range(2):
                        dve.wait_ge(fetched[u][i], 16 * (g + 1))
                        dve.scalar_tensor_tensor(out=y[:, t, 0:D], in0=got[:, u, i, :],
                                                 scalar=r["weight"][i][:, bass.ds(t, 1)], in1=y[:, t, 0:D],
                                                 op0=ALU.mult, op1=ALU.add).then_inc(added, 1)
                        dve.wait_ge(added, 2 * t + i + 1)


SPAN = 512
MAX_UNITS = [(q, a, min(a + SPAN, (q + 1) * P)) for q in range(TB) for a in range(0, (q + 1) * P, SPAN)]
PT_AT = [sum(L - P * j for j in range(k)) for k in range(TB + 1)]
MASKED = -1e30


def attention_order(wide, cur, prev, nxt, bank):
    n_max = len(MAX_UNITS)
    beside = {(c, k): [] for c in range(2) for k in range(TB)}
    if cur:
        beside[0, 0].append(("turn", 1, 0))
    if prev and wide:
        beside[0, 2].append(("invert", 0, 0))
        beside[0, 5].append(("scale", 0, 0))
        beside[1, 2].append(("invert", 1, 0))
        beside[1, 5].append(("scale", 1, 0))
        for u, k in enumerate((5, 6, 7, 7)):
            beside[1, k].append(("out", 0, u))
    if nxt:
        for u in range(4):
            beside[0, u if wide else u // 2].append(("prep", 0, u))
        if wide:
            places = [(0, k) for k in (4, 5, 6, 7)] + [(1, k) for k in range(TB)]
            places = [q for q in places for _ in range(2)]
            for h in range(2):
                beside[1, h].append(("v", 0, h))
        else:
            places = [(0, k) for k in range(2, TB) for _ in range(2)]
            places += [(1, k) for k, n in enumerate((1, 1, 2, 2, 2, 2, 1, 1)) for _ in range(n)]
        for m, at in enumerate(places):
            beside[at].append(("max", m // n_max, m % n_max))
        beside[1, 3 if wide else 1].append(("turn", 0, 0))
    order = []
    for c in range(2):
        for k in range(TB):
            main = []
            if cur:
                main.append(("score", c, k))
            if c == 0 and prev or c == 1 and cur:
                main.append(("weigh", 1 - c, k))
            extra = beside[c, k]
            mixed = []
            for m in main:
                mixed += extra[:1] + [m]
                extra = extra[1:]
            for name, a, n in mixed + extra:
                if name in ("score", "weigh", "invert", "scale"):
                    order.append((name, a, n, None))
                else:
                    order.append((name, a, n, bank))
                    bank = 1 - bank
    return order, bank


def attention_phase(nc, tag, wide, ident, q_src=None, oT_dram=None, w=None, xT_dram=None, y=None):
    dh = DK if wide else HD
    pairs = (HA if wide else H1) // 2
    n_pairs = B * pairs
    scale = dh ** -0.5
    n_prep = 4
    n_v = 2 if wide else 0
    n_po = P if wide else 4 * dh
    heads = 2 if wide else 1
    n_out = 4 if wide else 0
    n_max = len(MAX_UNITS)
    NARROW = 64
    with ExitStack() as ctx:
        def sb(name, shape, dt=F32):
            return ctx.enter_context(nc.sbuf_tensor(f"{tag}_{name}", shape, dt))

        def sem(name):
            return ctx.enter_context(nc.semaphore(f"{tag}_{name}"))

        if wide:
            xb = sb("xb", [P, 2, KD, L])
            wqk = sb("wqk", [P, 2, 3, KD, P])
            wo = sb("wo", [P, pairs, D])
            q1, q2, k1, k2 = ([[sb(f"{n}_{s}{c}", [P, L], F32R) for c in range(2)] for s in range(2)]
                              for n in ("q1", "q2", "k1", "k2"))
            oT = sb("oT", [P, L])
        else:
            qT, kT = ([sb(f"{n}_{s}", [P, L], F32R) for s in range(2)] for n in ("qT", "kT"))
            qc, kc = (sb(n, [P, TB, 2, NARROW]) for n in ("qc", "kc"))
            hi = sb("hi", [P, 2, TB, 2 * dh], F32R)
            stored = [sem(f"stored{s}") for s in range(2)]
        v = [sb(f"v{s}", [P, TB, 2, n_po]) for s in range(2)]
        half = n_po // 2
        v_at = (slice(0, dh), slice(dh, 2 * dh))
        one_at = (slice(dh, 2 * dh), slice(0, dh)) if wide else (slice(2 * dh, 3 * dh), slice(3 * dh, 4 * dh))
        raw = [sb(f"raw{c}", [P, L]) for c in range(heads)]
        if wide:
            sums = [sb(f"sums{c}", [P, TB]) for c in range(2)]
            inverse = [sb(f"inverse{c}", [P, TB]) for c in range(2)]
            factor = sb("factor", [P, L])
            sums_dram, inverse_dram = ([nc.dram_tensor(f"{tag}_{n}_dram{c}", (L,), F32).ap() for c in range(2)]
                                       for n in ("sums", "inverse"))
            sums_out, sums_in, inverse_out, inverse_in = ([sem(f"{n}{c}") for c in range(2)] for n in (
                "sums_out", "sums_in", "inverse_out", "inverse_in"))
        pt = [sb(f"pt{c}", [P, PT_AT[TB]]) for c in range(2)]
        parts = [sb(f"parts{c}", [P, TB, 2]) for c in range(2)]
        neg = sb("neg", [P, TB])
        mm = sb("mm", [P, 2, 2, TB], F32R)
        mt = sb("mt", [2 * TB, 2, P], F32R)
        ident16 = sb("ident16", [P, P], BF16)
        late = sb("late", [P, P], BF16)
        lateT = sb("lateT", [P, P], BF16)
        g = [ctx.enter_context(nc.psum_tensor(f"{tag}_g{i}", [P, SPAN], F32)) for i in range(2)]
        stp = [ctx.enter_context(nc.psum_tensor(f"{tag}_st{i}", [P, L], F32)) for i in range(2)]
        po = [ctx.enter_context(nc.psum_tensor(f"{tag}_po{i}", [P, SPAN], F32)) for i in range(2)]
        (consts, prep, hi_ok, prep_ok, dup_ok, v_mm, v_ok, mx, max_ok, m_ok, mt_mm, mt_ok, st, pt_ok, pv, raw_ok,
         inverse_ok, scaled, out_mm, out_ok, chain, low_ok) = (sem(n) for n in (
             "consts", "prep", "hi_ok", "prep_ok", "dup_ok", "v_mm", "v_ok", "mx", "max_ok", "m_ok", "mt_mm", "mt_ok",
             "st", "pt_ok", "pv", "raw_ok", "inverse_ok", "scaled", "out_mm", "out_ok", "chain", "low_ok"))
        passed, chain_pool, passed_act = sem("passed"), sem("chain_pool"), sem("passed_act")
        wo_in = sem("wo_in")
        loaded = [sem(f"loaded{s}") for s in range(2)]
        rows_out = [sem(f"rows_out{c}") for c in range(2)]
        rows_in = [sem(f"rows_in{c}") for c in range(2)]
        m_dram = [nc.dram_tensor(f"{tag}_m{c}", (2, L), F32).ap() for c in range(2)]
        block = ctx.enter_context(nc.Block())

        def walk(engine, step):
            bank = 0

            def one(i, s, cur, prev, nxt, nxt2):
                nonlocal bank
                order, bank = attention_order(wide, cur, prev, nxt, bank)
                step(i, s, order, nxt, nxt2)

            one(-1, 1, False, False, True, True)
            one(0, 0, True, False, True, True)
            with engine.Fori(0, (n_pairs - 4) // 2) as j:
                one(j * 2 + 1, 1, True, True, True, True)
                one(j * 2 + 2, 0, True, True, True, True)
            one(n_pairs - 3, 1, True, True, True, True)
            one(n_pairs - 2, 0, True, True, True, False)
            one(n_pairs - 1, 1, True, True, False, False)
            one(n_pairs, 0, False, True, False, False)

        def head_rows(c, n):
            return slice(NARROW * c, NARROW * c + n)

        def max_operands(s, c):
            if wide:
                return q1[s][c], k1[s][c], slice(c * dh, (c + 1) * dh)
            return qT[s], kT[s], head_rows(c, dh)

        def score_passes(s, c):
            if wide:
                return [(k1[s][c], q1[s][c], slice(0, P)), (k2[s][c], q2[s][c], slice(0, dh + 2))]
            return [(kT[s], qT[s], head_rows(c, 3 * dh + 2))]

        @block.sync
        def _(sp):
            def load(i, s):
                b, p = i // pairs, i % pairs
                sp.dma_start(xb[:, s, :, :], xT_dram[:, :, bass.ds(b * L, L)]).then_inc(loaded[s], 16)
                for n, name in enumerate(("L1_attn_Wq", "L1_attn_Wk", "L1_attn_Wv")):
                    sp.dma_start(wqk[:, s, n, :, :],
                                 w[name].rearrange("(k p) n -> p k n", p=P)[:, :, bass.ds(p * P, P)])\
                      .then_inc(loaded[s], 16)

            def store(i, s):
                b, p = (i - 1) // pairs, (i - 1) % pairs
                sp.wait_ge(raw_ok, 2 * i)
                first = (1 - s) * n_po
                sp.dma_start(oT_dram[0][bass.ds(p * 2 * dh, 2 * dh), bass.ds(b * L, L)],
                             raw[0][first:first + 2 * dh, :]).then_inc(stored[1 - s], 16)
                for c in range(2):
                    at = first + one_at[c].start
                    sp.dma_start(oT_dram[1][bass.ds(p * 2 + c, 1), bass.ds(b * L, L)], raw[0][at:at + 1, :])\
                      .then_inc(stored[1 - s], 16)

            def spread_sums(i, c):
                sp.wait_ge(raw_ok, (2 * i + c + 1) * 2)
                at = one_at[c].start
                sp.dma_start(sums_dram[c].rearrange("(o n) -> o n", o=1), raw[c][at:at + 1, :]).then_inc(sums_out[c], 16)
                sp.wait_ge(sums_out[c], 16 * (i + 1))
                sp.dma_start(sums[c][:, :], sums_dram[c].rearrange("(p t) -> p t", p=P)).then_inc(sums_in[c], 16)

            def spread_inverse(i, c):
                sp.wait_ge(inverse_ok, 2 * i + c + 1)
                sp.dma_start(inverse_dram[c].rearrange("(p t) -> p t", p=P), inverse[c][:, :])\
                  .then_inc(inverse_out[c], 16)
                sp.wait_ge(inverse_out[c], 16 * (i + 1))
                sp.dma_start(factor[v_at[c], :], inverse_dram[c].rearrange("(o n) -> o n", o=1).broadcast_to([dh, L]))\
                  .then_inc(inverse_in[c], 16)

            def spread_max(i, s, c):
                sp.wait_ge(mt_ok, 2 * i + c + 1)
                dst = q2[s][c][dh:dh + 2, :] if wide else qT[s][NARROW * c + 3 * dh:NARROW * c + 3 * dh + 2, :]
                sp.dma_start(m_dram[c].rearrange("h (t q) -> (h t) q", q=P), mt[:, c, :].bitcast(F32))\
                  .then_inc(rows_out[c], 16)
                sp.wait_ge(rows_out[c], 16 * (i + 1))
                sp.dma_start(dst.bitcast(F32), m_dram[c]).then_inc(rows_in[c], 16)

            def step(i, s, cur, prev, nxt, more):
                if prev and wide:
                    spread_sums(i - 1, 0)
                if cur:
                    spread_max(i, s, 1)
                if prev and wide:
                    spread_inverse(i - 1, 0)
                    spread_sums(i - 1, 1)
                if prev and not wide:
                    store(i, s)
                if wide and more:
                    sp.wait_ge(v_mm, n_v * (i + 1))
                    load(i + 2, s)
                if prev and wide:
                    spread_inverse(i - 1, 1)
                if nxt:
                    spread_max(i + 1, 1 - s, 0)

            if wide:
                load(0, 0)
                load(1, 1)
                sp.dma_start(wo[:, :, :], w["L1_attn_Wo"].rearrange("(c p) n -> p c n", p=P)).then_inc(wo_in, 16)
            if not wide:
                for q in stored:
                    sp.sem_inc(q, 48)
            step(-1, 1, False, False, True, False)
            step(0, 0, True, False, True, True)
            with sp.Fori(0, (n_pairs - 4) // 2) as j:
                step(j * 2 + 1, 1, True, True, True, True)
                step(j * 2 + 2, 0, True, True, True, True)
            step(n_pairs - 3, 1, True, True, True, True)
            step(n_pairs - 2, 0, True, True, True, False)
            step(n_pairs - 1, 1, True, True, False, False)
            step(n_pairs, 0, False, True, False, False)
            if not wide:
                for q in stored:
                    sp.wait_ge(q, 48 + 48 * (n_pairs // 2))

        @block.tensor
        def _(pe):
            fills = []

            def fill(i, i_of, reader, per_pair, index):
                n = len(fills)
                if n >= 2:
                    sem_, per, off, at = fills[-2]
                    pe.wait_ge(sem_, (i + off) * per + at + 1)
                fills.append((reader, per_pair, i_of, index))
                return g[n % 2]

            def shift():
                fills[:] = [(a, b_, off - 1, d) for a, b_, off, d in fills]

            def project(i, s, u):
                n, h = u // 2, u % 2
                if u == 0:
                    if wide:
                        pe.wait_ge(loaded[s], 64 * ((i + 1) // 2 + 1))
                    else:
                        pe.wait_ge(low_ok, 4 * (i + 2))
                        pe.wait_ge(dup_ok, 4 * (i + 2))
                bank = fill(i, 1, prep_ok, n_prep, u)
                if wide:
                    for k in range(KD):
                        m = pe.matmul(bank[:, :], wqk[:, s, n, k, :], xb[:, s, k, h * SPAN:(h + 1) * SPAN],
                                      start=(k == 0), stop=(k == KD - 1))
                else:
                    for t in range(4):
                        m = pe.transpose(bank[:, t * P:(t + 1) * P],
                                         (qc, kc)[n][:, h * 4 + t, :, :].rearrange("p c n -> p (c n)"), ident[:, :])
                m.then_inc(prep, 1)

            def project_v(i, s, h):
                bank = fill(i, 1, v_ok, n_v, h)
                for t in range(4):
                    for k in range(KD):
                        m = pe.matmul(bank[:, t * P:(t + 1) * P],
                                      xb[:, s, k, (h * 4 + t) * P:(h * 4 + t + 1) * P], wqk[:, s, 2, k, :],
                                      start=(k == 0), stop=(k == KD - 1))
                m.then_inc(v_mm, 1)

            def max_unit(i, s, c, u):
                if u == 0 and c == 0:
                    pe.wait_ge(hi_ok if wide else prep_ok, n_prep * (i + 2))
                tile, a, z = MAX_UNITS[u]
                bank = fill(i, 1, max_ok, 2 * n_max, c * n_max + u)
                q_, k_, rows = max_operands(s, c)
                diagonal = z == (tile + 1) * P
                m = pe.matmul(bank[:, 0:z - a], q_[rows, tile * P:(tile + 1) * P], k_[rows, a:z],
                              start=True, stop=not diagonal)
                if diagonal:
                    m = pe.matmul(bank[:, z - a - P:z - a], ident16[:, :], late[:, :], start=False, stop=True)
                m.then_inc(mx, 1)

            def turn_max(i, c):
                pe.wait_ge(m_ok, 2 * (i + 1 - c) + c + 1)
                bank = fill(i, 1 - c, mt_ok, 2, c)
                pe.transpose(bank[0:2 * TB, 0:P], mm[:, c, :, :].rearrange("p h t -> p (h t)").bitcast(F32),
                             ident[:, :]).then_inc(mt_mm, 1)

            def score(i, s, c, k):
                pe.wait_ge(pt_ok, 2 * TB * i + c * TB + k + 1)
                if k == 0:
                    pe.wait_ge(rows_in[c], 16 * (i + 1))
                    if wide and c == 0:
                        pe.wait_ge(dup_ok, 4 * (i + 1))
                        pe.wait_ge(prep_ok, n_prep * (i + 1))
                spans = [(a, z) for a, z in ((0, SPAN), (SPAN, L)) if z > k * P]
                for a, z in spans:
                    a = max(a, k * P)
                    for n, (k_, q_, rows) in enumerate(score_passes(s, c)):
                        last = n == len(score_passes(s, c)) - 1 and a != k * P
                        m = pe.matmul(stp[k % 2][:, a:z], k_[rows, k * P:(k + 1) * P], q_[rows, a:z],
                                      start=(n == 0), stop=last)
                    if a == k * P:
                        m = pe.matmul(stp[k % 2][:, a:a + P], ident16[:, :], lateT[:, :], start=False, stop=True)
                m.then_inc(st, 1)

            def weigh(i, s, c, k):
                pe.wait_ge(pt_ok, 2 * TB * i + c * TB + k + 3)
                if k == 0 and c < heads:
                    pe.wait_ge(raw_ok, (heads * i + c) * 2)
                if k == 0 and c == 0:
                    pe.wait_ge(v_ok, 2 * (i + 1))
                for h in range(k // 4, 2):
                    a = max(k * P - h * SPAN, 0)
                    at = PT_AT[k] + h * SPAN + a - k * P
                    m = pe.matmul(po[h][0:n_po, a:SPAN], v[s][:, k, c, :], pt[c][:, at:at + SPAN - a],
                                  start=(k == 0 and c < heads), stop=(k == h * 4 + 3 and c >= heads - 1),
                                  skip_group_check=True)
                    if k == h * 4 + 3 and (wide or c == 1):
                        m.then_inc(pv, 1)

            def project_o(i, u):
                if u == 0:
                    pe.wait_ge(scaled, 2 * i + 1)
                bank = fill(i, -1, out_ok, n_out, u)
                for h in range(2):
                    t = u * 2 + h
                    m = pe.matmul(bank[:, h * D:(h + 1) * D], oT[:, t * P:(t + 1) * P], wo[:, (i - 1) % pairs, :],
                                  start=True, stop=True)
                m.then_inc(out_mm, 1)

            def step(i, s, order, nxt, nxt2):
                for name, c, n, _ in order:
                    if name == "score":
                        score(i, s, c, n)
                    elif name == "weigh":
                        weigh(i - c, s if c == 0 else 1 - s, c, n)
                    elif name == "prep":
                        project(i, 1 - s, n)
                    elif name == "v":
                        project_v(i, 1 - s, n)
                    elif name == "max":
                        max_unit(i, 1 - s, c, n)
                    elif name == "turn":
                        turn_max(i, c)
                    elif name == "out":
                        project_o(i, n)
                shift()

            pe.wait_ge(consts, 2)
            if wide:
                pe.wait_ge(wo_in, 16)
            walk(pe, step)

        @block.scalar
        def _(act):
            act.sem_inc(pt_ok, 2)

            def high(i, s, u, bank):
                n, h = u // 2, u % 2
                at = slice(h * SPAN, (h + 1) * SPAN)
                act.wait_ge(prep, n_prep * (i + 1) + u + 1)
                if wide:
                    for c in range(2):
                        rows = slice(c * dh, (c + 1) * dh)
                        m = act.activation((q1, k1)[n][s][c][rows, at], bank[rows, :], ACT.Copy,
                                           scale=scale if n == 0 else 1.0)
                    m.then_inc(hi_ok, 1)
                else:
                    act.activation((qT, kT)[n][s][:, at], bank[:, :], ACT.Copy).then_inc(prep_ok, 1)

            def values(i, s, h, bank):
                act.wait_ge(v_mm, n_v * (i + 1) + h + 1)
                for c in range(2):
                    m = act.activation(v[s][:, h * 4:h * 4 + 4, c, v_at[c]],
                                       bank[:, :].rearrange("p (t c n) -> p t c n", t=4, c=2)[:, :, c, :], ACT.Copy)
                m.then_inc(v_ok, 1)

            def exp(i, c, k):
                act.wait_ge(st, 2 * TB * i + c * TB + k + 1)
                act.activation(pt[c][:, PT_AT[k]:PT_AT[k + 1]], stp[k % 2][:, k * P:L], ACT.Exp).then_inc(pt_ok, 1)

            def drain(i, s, c):
                if wide:
                    act.wait_ge(scaled, 2 * i + c)
                else:
                    act.wait_ge(stored[s], 48 * ((i + 2) // 2))
                act.sem_inc(passed_act, 1)
                for h in range(2):
                    act.wait_ge(pv, (heads * i + (c if wide else 0)) * 2 + h + 1)
                    dst = raw[c] if wide else raw[0][s * half * 2:s * half * 2 + n_po, :]
                    act.activation(dst[:, h * SPAN:(h + 1) * SPAN], po[h][0:n_po, :], ACT.Copy).then_inc(raw_ok, 1)

            def step(i, s, order, nxt, nxt2):
                for name, c, n, bank in order:
                    if name == "prep":
                        high(i, 1 - s, n, g[bank])
                    elif name == "score":
                        exp(i, c, n)
                    elif name == "v":
                        values(i, 1 - s, n, g[bank])
                    elif name == "weigh" and n == TB - 1 and (wide or c == 1):
                        drain(i - c, s if c == 0 else 1 - s, c)
            walk(act, step)

        @block.vector
        def _(dve):
            def low(i, s, u, bank):
                n, h = u // 2, u % 2
                at = slice(h * SPAN, (h + 1) * SPAN)
                dve.wait_ge(hi_ok, n_prep * (i + 1) + u + 1)
                for c in range(2):
                    rows = slice(c * dh, (c + 1) * dh)
                    if n == 0:
                        dst = q1[s][c][(1 - c) * dh:(2 - c) * dh, at]
                    else:
                        dst = k2[s][c][0:dh, at]
                    m = dve.scalar_tensor_tensor(out=dst, in0=bank[rows, :], scalar=scale if n == 0 else 1.0,
                                                 in1=(q1, k1)[n][s][c][rows, at].bitcast(F32),
                                                 op0=ALU.mult, op1=ALU.subtract)
                m.then_inc(prep_ok, 1)

            def stack(i):
                b, p = (i + 1) // pairs, (i + 1) % pairs
                dve.wait_ge(prep, n_prep * (i + 1))
                for n in range(2):
                    src = q_src[:, bass.ds(b * TB, TB), bass.ds(n * D + p * 2 * dh, 2 * dh)]
                    dve.tensor_scalar(hi[:, n, :, :], src, scale if n == 0 else 1.0, None, ALU.mult).then_inc(hi_ok, 1)
                dve.wait_ge(hi_ok, 2 * (i + 2))
                for n in range(2):
                    for c in range(2):
                        src = q_src[:, bass.ds(b * TB, TB), bass.ds(n * D + p * 2 * dh + c * dh, dh)]
                        dst = (qc[:, :, c, dh:2 * dh], kc[:, :, c, 2 * dh:3 * dh])[n]
                        dve.scalar_tensor_tensor(out=dst, in0=src, scalar=scale if n == 0 else 1.0,
                                                 in1=hi[:, n, :, c * dh:(c + 1) * dh].bitcast(F32),
                                                 op0=ALU.mult, op1=ALU.subtract).then_inc(low_ok, 1)

            def max_unit(i, c, u, bank):
                tile, a, z = MAX_UNITS[u]
                dve.wait_ge(mx, 2 * n_max * (i + 1) + c * n_max + u + 1)
                dve.tensor_reduce(parts[c][:, tile, a // SPAN:a // SPAN + 1], bank[:, 0:z - a], AX.X, ALU.max)\
                   .then_inc(max_ok, 1)

            def minus_max(i, c):
                dve.wait_ge(max_ok, 2 * n_max * (i + 1) + (c + 1) * n_max)
                dve.tensor_reduce(neg[:, :], parts[c][:, :, :], AX.X, ALU.max, negate=True).then_inc(chain, 1)
                dve.wait_ge(chain, 2 * (2 * (i + 1) + c) + 1)
                dve.tensor_copy(mm[:, c, 0, :], neg[:, :]).then_inc(chain, 1)
                dve.wait_ge(chain, 2 * (2 * (i + 1) + c) + 2)
                dve.tensor_tensor(mm[:, c, 1, :], neg[:, :], mm[:, c, 0, :].bitcast(F32), ALU.subtract)\
                   .then_inc(m_ok, 1)

            def max_rows(i, c, bank):
                dve.wait_ge(mt_mm, 2 * (i + 1 - c) + c + 1)
                dve.tensor_copy(mt[:, c, :], bank[0:2 * TB, 0:P]).then_inc(mt_ok, 1)

            def invert(i, c):
                dve.wait_ge(sums_in[c], 16 * (i + 1))
                dve.reciprocal(inverse[c][:, :], sums[c][:, :]).then_inc(inverse_ok, 1)

            def scale_o(i, c):
                dve.wait_ge(inverse_in[c], 16 * (i + 1))
                rows = v_at[c]
                dve.tensor_tensor(oT[rows, :], raw[c][rows, :], factor[rows, :], ALU.mult).then_inc(scaled, 1)

            def add_out(i, u, bank):
                dve.wait_ge(out_mm, n_out * (i - 1) + u + 1)
                b = (i - 1) // pairs
                rows = y[:, bass.ds(b * TB + u * 2, 2), :]
                dve.tensor_tensor(rows, bank[:, :].rearrange("p (t d) -> p t d", t=2), rows, ALU.add)\
                   .then_inc(out_ok, 1)

            def step(i, s, order, nxt, nxt2):
                for name, c, n, bank in order:
                    if name == "prep" and wide:
                        low(i, 1 - s, n, g[bank])
                    elif name == "max":
                        max_unit(i, c, n, g[bank])
                        if n == n_max - 1:
                            minus_max(i, c)
                        if n == 2 and c == 0 and nxt2 and not wide:
                            stack(i + 1)
                    elif name == "turn":
                        max_rows(i, c, g[bank])
                    elif name == "out":
                        add_out(i, n, g[bank])
                    elif name == "invert":
                        invert(i - 1, c)
                    elif name == "scale":
                        scale_o(i - 1, c)
            dve.sem_inc(scaled, 1)
            dve.wait_ge(consts, 2)
            if not wide:
                stack(-1)
            walk(dve, step)

        @block.gpsimd
        def _(pool):
            link = Chain(pool, chain_pool).step
            for c in range(2):
                link(pool.memset(parts[c][:, :, 1:2], MASKED))
            for s in range(2):
                if wide:
                    for c in range(2):
                        link(pool.memset(k2[s][c][dh:dh + 2, :].bitcast(F32), 1.0))
                if not wide:
                    link(pool.memset(v[s][:, :, :, :], 0.0))
                for c in range(2):
                    link(pool.memset(v[s][:, :, c, one_at[c]], 1.0))
            if not wide:
                link(pool.memset(qc[:, :, :, :], 0.0))
                link(pool.memset(kc[:, :, :, :], 0.0))
                link(pool.memset(kc[:, :, :, 3 * dh:3 * dh + 2], 1.0))
            link(pool.tensor_copy(ident16[:, :], ident[:, :]))
            link(pool.memset(late[:, :], 0.0))
            link(pool.memset(lateT[:, :], 0.0))
            pool.affine_select(out=late[:, :], in_=late[:, :], compare_op=ALU.is_ge, fill=MASKED, base=0,
                               pattern=[[-1, P]], channel_multiplier=1).then_inc(consts, 1)
            pool.affine_select(out=lateT[:, :], in_=lateT[:, :], compare_op=ALU.is_ge, fill=MASKED, base=0,
                               pattern=[[1, P]], channel_multiplier=-1).then_inc(consts, 1)
            pool.wait_ge(consts, 2)

            def copies(i, s):
                for n in range(2):
                    pool.wait_ge(hi_ok, n_prep * (i + 1) + 2 * n + 2)
                    pool.sem_inc(passed, 1)
                    for c in range(2):
                        rows, other = slice(c * dh, (c + 1) * dh), slice((1 - c) * dh, (2 - c) * dh)
                        if n == 0:
                            m = pool.tensor_copy(q2[s][c][0:dh, :], q1[s][c][rows, :].bitcast(F32))
                        else:
                            m = pool.tensor_copy(k1[s][c][other, :], k1[s][c][rows, :].bitcast(F32))
                        m.then_inc(dup_ok, 1)
                        pool.wait_ge(dup_ok, 4 * (i + 1) + 2 * n + c + 1)
                        pool.sem_inc(passed, 1)

            def stack_high(i):
                pool.wait_ge(hi_ok, 2 * (i + 2))
                pool.sem_inc(passed, 1)
                for n, places in ((0, (0, 2)), (1, (0, 1))):
                    for at in places:
                        pool.tensor_copy((qc, kc)[n][:, :, :, at * dh:(at + 1) * dh],
                                         hi[:, n, :, :].bitcast(F32).rearrange("p t (c n) -> p t c n", c=2))\
                            .then_inc(dup_ok, 1)

            def copy_v(i, s):
                b, p = (i + 1) // pairs, (i + 1) % pairs
                pool.wait_ge(pv, 2 * i if not isinstance(i, int) or i >= 0 else 0)
                pool.sem_inc(passed, 1)
                for c in range(2):
                    pool.tensor_copy(v[s][:, :, c, v_at[c]],
                                     q_src[:, bass.ds(b * TB, TB), bass.ds(2 * D + p * 2 * dh + c * dh, dh)])\
                        .then_inc(v_ok, 1)

            def step(i, s, order, nxt, nxt2):
                if wide and nxt:
                    copies(i, 1 - s)
                if not wide and nxt2:
                    stack_high(i + 1)
                if not wide and nxt:
                    copy_v(i, 1 - s)
            if not wide:
                stack_high(-1)
            walk(pool, step)


def qkv_phase(nc, w, tables, hT, qkv):
    G = 3 * D
    with ExitStack() as ctx:
        def sb(name, shape, dt=F32):
            return ctx.enter_context(nc.sbuf_tensor(f"qkv_{name}", shape, dt))

        def sem(name):
            return ctx.enter_context(nc.semaphore(f"qkv_{name}"))

        half = HD // 2
        heads = 2 * H1
        raw = sb("raw", [P, KD, G])
        wt = sb("wt", [P, KD, G])
        cos, sin = (sb(n, [P, TB, half]) for n in ("cos", "sin"))
        stage = sb("stage", [P, 2, KD, P])
        prods = [[sb(f"prod{i}_{u}", [P, heads, half]) for i in range(4)] for u in range(2)]
        pa = [ctx.enter_context(nc.psum_tensor(f"qkv_pa{i}", [P, 2 * D], F32)) for i in range(2)]
        pb = [ctx.enter_context(nc.psum_tensor(f"qkv_pb{i}", [P, D], F32)) for i in range(2)]
        w_in, w_ok, staged, done, rotated, v_ok, prod_ok, seen = (
            sem(n) for n in ("w_in", "w_ok", "staged", "done", "rotated", "v_ok", "prod_ok", "seen"))
        block = ctx.enter_context(nc.Block())

        @block.sync
        def _(sp):
            sp.dma_start(raw[:, :, :], w["L1_ffn_Wqkv"].rearrange("(k p) n -> p k n", p=P)).then_inc(w_in, 16)
            for dst, src in ((cos, tables[0]), (sin, tables[1])):
                sp.dma_start(dst[:, :, :], tiles_of(src)).then_inc(w_in, 16)

        @block.gpsimd
        def _(pool):
            pool.wait_ge(w_in, 48)
            for kind in range(3):
                for k in range(KD):
                    pool.tensor_copy(wt[:, k, kind * D:(kind + 1) * D].rearrange("p (h n) -> p h n", n=HD),
                                     raw[:, k, :].rearrange("p (h c n) -> p h c n", c=3, n=HD)[:, :, kind, :])\
                        .then_inc(w_ok, 1)

        @block.scalar
        def _(act):
            act.sem_inc(v_ok, 2)

            def copy_in(t, u):
                act.wait_ge(done, t + 1)
                act.activation(stage[:, u % 2, :, :], hT[:, :, bass.ds(t * P, P)], ACT.Copy).then_inc(staged, 1)

            with act.Fori(0, T // TB) as b:
                for u in range(TB):
                    t = b * TB + u
                    copy_in(t, u)
                    act.wait_ge(done, t + 3)
                    act.activation(qkv[:, t, 2 * D:G], pb[u % 2][:, :], ACT.Copy).then_inc(v_ok, 1)

        @block.tensor
        def _(pe):
            pe.sem_inc(done, 2)
            pe.wait_ge(w_ok, 6)
            with pe.Fori(0, T // TB) as b:
                for u in range(TB):
                    t = b * TB + u
                    pe.wait_ge(staged, t + 1)
                    pe.wait_ge(v_ok, t + 1)
                    pe.wait_ge(rotated, t + 1)
                    for out, a, z in ((pa, 0, 2 * D), (pb, 2 * D, G)):
                        for k in range(KD):
                            m = pe.matmul(out[u % 2][:, :], stage[:, u % 2, k, :], wt[:, k, a:z],
                                          start=(k == 0), stop=(k == KD - 1))
                    m.then_inc(done, 1)

        @block.vector
        def _(dve):
            dve.sem_inc(rotated, 2)
            with dve.Fori(0, T // TB) as b:
                for u in range(TB):
                    t = b * TB + u
                    dve.wait_ge(done, t + 3)
                    dve.sem_inc(seen, 1)
                    dve.wait_ge(rotated, t + 1)
                    prod = prods[u % 2]
                    x = pa[u % 2][:, :].rearrange("p (h c n) -> p h c n", c=2, n=half)
                    for n, (part, table) in enumerate(((0, cos), (1, sin), (0, sin), (1, cos))):
                        dve.tensor_tensor(prod[n][:, :, :], x[:, :, part, :],
                                          table[:, u, :].unsqueeze(1).broadcast_to([P, heads, half]), ALU.mult)\
                           .then_inc(prod_ok, 1)
                    dve.wait_ge(prod_ok, 4 * (t + 1))
                    y = qkv[:, t, 0:2 * D].rearrange("p (h c n) -> p h c n", c=2, n=half)
                    dve.tensor_tensor(y[:, :, 0, :], prod[0][:, :, :], prod[1][:, :, :], ALU.subtract)
                    dve.tensor_tensor(y[:, :, 1, :], prod[2][:, :, :], prod[3][:, :, :], ALU.add).then_inc(rotated, 1)


def output_phase(nc, w, oT_dram, y):
    R = 4
    PARTS = 4
    with ExitStack() as ctx:
        def sb(name, shape):
            return ctx.enter_context(nc.sbuf_tensor(f"op_{name}", shape, F32))

        def sem(name):
            return ctx.enter_context(nc.semaphore(f"op_{name}"))

        wp = sb("w", [P, KD, D])
        sums = sb("sums", [P, H1 * N // P])
        raw, factor = (sb(n, [P, KD, N]) for n in ("raw", "factor"))
        oT = sb("oT", [P, R, KD, 2 * P])
        py = [ctx.enter_context(nc.psum_tensor(f"op_py{i}", [P, 2, D], F32)) for i in range(2)]
        inverse_dram = nc.dram_tensor("op_inverse", (H1, N), F32).ap()
        w_in, sums_in, inverse_ok, inverse_out, oT_ok, done, added = (
            sem(n) for n in ("w_in", "sums_in", "inverse_ok", "inverse_out", "oT_ok", "done", "added"))
        loaded = [sem(f"loaded{c}") for c in range(PARTS)]
        block = ctx.enter_context(nc.Block())

        def across(ap):
            return ap.rearrange("h (c n) -> (h c) n", n=H1 * N // P)

        @block.sync
        def _(sp):
            sp.dma_start(sums[:, :], across(oT_dram[1])).then_inc(sums_in, 16)
            sp.dma_start(wp[:, :, :], w["L1_ffn_Wproj"].rearrange("(k p) n -> p k n", p=P)).then_inc(w_in, 16)
            for c in range(PARTS):
                at = slice(c * (N // PARTS), (c + 1) * (N // PARTS))
                sp.dma_start(raw[:, :, at], oT_dram[0].rearrange("(k p) n -> p k n", p=P)[:, :, at])\
                  .then_inc(loaded[c], 16)
            sp.wait_ge(inverse_ok, 1)
            sp.dma_start(across(inverse_dram), sums[:, :]).then_inc(inverse_out, 16)
            sp.wait_ge(inverse_out, 16)
            heads = P // HD
            for c in range(PARTS):
                at = slice(c * (N // PARTS), (c + 1) * (N // PARTS))
                for k in range(KD):
                    src = inverse_dram[k * heads:(k + 1) * heads, at]
                    sp.dma_start(factor[:, k, at], src.unsqueeze(1).broadcast_to([heads, HD, N // PARTS]))\
                      .then_inc(loaded[c], 16)

        @block.tensor
        def _(pe):
            pe.wait_ge(w_in, 16)
            with pe.Fori(0, T // 2 // R) as i:
                for u in range(R):
                    s = i * R + u
                    pe.wait_ge(oT_ok, s + 1)
                    pe.wait_ge(added, s + 1)
                    for v in range(2):
                        for k in range(KD):
                            m = pe.matmul(py[u % 2][:, v, :], oT[:, u, k, v * P:(v + 1) * P], wp[:, k, :],
                                          start=(k == 0), stop=(k == KD - 1))
                    m.then_inc(done, 1)

        @block.vector
        def _(dve):
            dve.sem_inc(added, 2)
            dve.wait_ge(sums_in, 16)
            dve.reciprocal(sums[:, :], sums[:, :]).then_inc(inverse_ok, 1)

            def divide(s, u):
                at = bass.ds(s * 2 * P, 2 * P)
                dve.tensor_tensor(oT[:, u, :, :], raw[:, :, at], factor[:, :, at], ALU.mult).then_inc(oT_ok, 1)

            def add(s, u):
                dve.wait_ge(done, s + 1)
                out = y[:, bass.ds(s * 2, 2), :]
                dve.tensor_tensor(out, py[u % 2][:, :, :], out, ALU.add).then_inc(added, 1)

            steps_per_part = T // 2 // PARTS
            for s in range(T // 2):
                if s % steps_per_part == 0:
                    dve.wait_ge(loaded[s // steps_per_part], 16 * (1 + KD))
                divide(s, s % R)
                if s >= 2:
                    add(s - 2, s % R)
            for s in range(T // 2 - 2, T // 2):
                add(s, s % R)


def layer1_experts(nc, w, gain, rows, outs, ident):
    FT = F1 // P
    STEPS = ROWS1 // SPAN
    PER = CAP // SPAN
    with ExitStack() as ctx:
        def sb(name, shape, dt=F32):
            return ctx.enter_context(nc.sbuf_tensor(f"e1_{name}", shape, dt))

        def ps(name, shape):
            return ctx.enter_context(nc.psum_tensor(f"e1_{name}", shape, F32))

        def sem(name):
            return ctx.enter_context(nc.semaphore(f"e1_{name}"))

        w1 = sb("w1", [P, 2, KD, F1])
        w2 = sb("w2", [P, 2, FT, D])
        b1_rows = sb("b1_rows", [E * FT, P])
        b1 = sb("b1", [P, E, FT])
        b2 = sb("b2", [P, 2, D])
        xg = sb("xg", [P, 2, SPAN // P, D])
        xT = sb("xT", [P, 2, KD, SPAN])
        hid = sb("hid", [P, FT, SPAN])
        yo = sb("yo", [P, 2, 2, D])
        px = [ps(f"px{k}", [P, SPAN]) for k in range(KD)]
        ph = [ps(f"ph{i}", [P, SPAN]) for i in range(2)]
        py = [ps(f"py{i}", [P, 2, D]) for i in range(2)]
        pb = ps("pb", [P, E * FT])
        b_in, b_turned, b_ok, x_turned, xT_ok, up_ok, hid_ok, y_done, y_ok, seen = (
            sem(n) for n in ("b_in", "b_turned", "b_ok", "x_turned", "xT_ok", "up_ok", "hid_ok", "y_done", "y_ok",
                             "seen"))
        w_in, x_in, stored = ([sem(f"{n}{i}") for i in range(2)] for n in ("w_in", "x_in", "stored"))
        block = ctx.enter_context(nc.Block())

        x_rows = tiles_of(rows)
        y_rows = tiles_of(outs)

        @block.sync
        def _(sp):
            def load_w(e, s):
                sp.dma_start(w1[:, s, :, :], w["L1_ffn_W1"][bass.ds(e, 1), :, :].rearrange("o (k p) n -> p (o k) n", p=P))\
                  .then_inc(w_in[s], 16)
                sp.dma_start(w2[:, s, :, :], w["L1_ffn_W2"][bass.ds(e, 1), :, :].rearrange("o (k p) n -> p (o k) n", p=P))\
                  .then_inc(w_in[s], 16)
                sp.dma_start(b2[:, s, :], w["L1_ffn_b2"][bass.ds(e, 1), :].broadcast_to([P, D])).then_inc(w_in[s], 16)

            def load_x(q, s):
                sp.dma_start(xg[:, s, :, :], x_rows[:, bass.ds(q * (SPAN // P), SPAN // P), :]).then_inc(x_in[s], 16)

            sp.dma_start(b1_rows[:, :], w["L1_ffn_b1"].rearrange("e (f p) -> (e f) p", p=P)).then_inc(b_in, 16)
            load_x(0, 0)
            load_w(0, 0)
            load_x(1, 1)
            load_w(1, 1)

            def store(q):
                for h in range(2):
                    sp.wait_ge(y_ok, 2 * q + h + 3)
                    sp.dma_start(y_rows[:, bass.ds(q * 4 + h * 2, 2), :], yo[:, h, :, :]).then_inc(stored[h], 16)

            def step(q, v, e, more_x, more_w):
                if more_x:
                    sp.wait_ge(x_turned, q + 1)
                    load_x(q + 2, v % 2)
                store(q)
                if v % PER == PER - 1 and more_w:
                    load_w(e + 2, v // PER)

            for s in stored:
                sp.sem_inc(s, 16)
            with sp.Fori(0, E // 2 - 1) as j:
                for v in range(4):
                    step(j * 4 + v, v, j * 2 + v // PER, True, True)
            for v in range(4):
                step(STEPS - 4 + v, v, E - 2 + v // PER, v < 2, False)
            for s in stored:
                sp.wait_ge(s, 16 * (STEPS + 1))

        @block.tensor
        def _(pe):
            def turn_x(q, s, n):
                pe.wait_ge(x_in[s], 16 * (n + 1))
                pe.wait_ge(xT_ok, q)
                for k in range(KD):
                    for t in range(SPAN // P):
                        m = pe.transpose(px[k][:, t * P:(t + 1) * P], xg[:, s, t, k * P:(k + 1) * P], ident[:, :])
                m.then_inc(x_turned, 1)

            def up(q, s, ws):
                pe.wait_ge(xT_ok, q + 1)
                for f in range(FT):
                    pe.wait_ge(hid_ok, q * FT + f + 1)
                    for k in range(KD):
                        m = pe.matmul(ph[f % 2][:, :], w1[:, ws, k, f * P:(f + 1) * P], xT[:, s, k, :],
                                      start=(k == 0), stop=(k == KD - 1))
                    m.then_inc(up_ok, 1)

            def down(q, ws):
                pe.wait_ge(hid_ok, (q + 1) * FT + 2)
                for h in range(2):
                    pe.wait_ge(y_ok, 2 * q + h + 1)
                    for v in range(2):
                        t = h * 2 + v
                        for f in range(FT):
                            m = pe.matmul(py[h][:, v, :], hid[:, f, t * P:(t + 1) * P], w2[:, ws, f, :],
                                          start=(f == 0), stop=(f == FT - 1))
                    m.then_inc(y_done, 1)

            def step(q, v, j, more):
                ws = v // PER
                if v % PER == 0:
                    pe.wait_ge(w_in[ws], 48 * (j + 1))
                up(q, v % 2, ws)
                if more:
                    turn_x(q + 1, (v + 1) % 2, j * 2 + (v + 1) // 2)
                down(q, ws)

            pe.wait_ge(b_in, 16)
            pe.transpose(pb[:, :], b1_rows[:, :], ident[0:E * FT, 0:E * FT]).then_inc(b_turned, 1)
            turn_x(0, 0, 0)
            steps(pe, step)

        @block.scalar
        def _(act):
            act.sem_inc(hid_ok, 2)

            def scale_x(q, s):
                act.wait_ge(x_turned, q + 1)
                for k in range(KD):
                    m = act.activation(xT[:, s, k, :], px[k][:, :], ACT.Identity, scale=gain[0][:, k:k + 1],
                                       bias=gain[1][:, k:k + 1])
                m.then_inc(xT_ok, 1)

            def step(q, v, j, more):
                for f in range(FT):
                    act.wait_ge(up_ok, q * FT + f + 1)
                    act.sem_inc(seen, 1)
                    act.activation(hid[:, f, :], ph[f % 2][:, :], ACT.Gelu,
                                   bias=b1[:, bass.ds(j * 2 + v // PER, 1), f:f + 1].rearrange("p o f -> p (o f)"))\
                       .then_inc(hid_ok, 1)
                if more:
                    scale_x(q + 1, (v + 1) % 2)

            act.wait_ge(b_ok, 1)
            scale_x(0, 0)
            steps(act, step)

        @block.vector
        def _(dve):
            dve.wait_ge(b_turned, 1)
            dve.tensor_copy(b1[:, :, :], pb[:, :].rearrange("p (e f) -> p e f", e=E)).then_inc(b_ok, 1)
            dve.sem_inc(y_ok, 2)

            def step(q, v, j, more):
                for h in range(2):
                    dve.wait_ge(y_done, 2 * q + h + 1)
                    dve.wait_ge(stored[h], 16 * (q + 1))
                    dve.tensor_tensor(yo[:, h, :, :], py[h][:, :, :],
                                      b2[:, v // PER, :].unsqueeze(1).broadcast_to([P, 2, D]), ALU.add).then_inc(y_ok, 1)
            steps(dve, step)


def steps(engine, step):
    with engine.Fori(0, E // 2 - 1) as j:
        for v in range(4):
            step(j * 4 + v, v, j, True)
    for v in range(4):
        step(E * 2 - 4 + v, v, E // 2 - 1, v < 3)


def load_gains(nc, ctx, w, ident):
    names = ("ln1_g", "ln1_b", "ln2_g", "ln2_b")
    cols = ctx.enter_context(nc.sbuf_tensor("gain_cols", [P, len(names) * KD], F32))
    with ExitStack() as inner:
        rows = inner.enter_context(nc.sbuf_tensor("gain_rows", [len(names) * KD, P], F32))
        turned = inner.enter_context(nc.psum_tensor("gain_turned", [P, len(names) * KD], F32))
        loaded, turned_ok = (inner.enter_context(nc.semaphore(f"gain_{n}")) for n in ("loaded", "turned_ok"))
        block = inner.enter_context(nc.Block())

        @block.sync
        def _(sp):
            for i, name in enumerate(names):
                sp.dma_start(rows[i * KD:(i + 1) * KD, :], w["L1_ffn_" + name].rearrange("(k p) -> k p", p=P))\
                  .then_inc(loaded, 16)

        @block.tensor
        def _(pe):
            pe.wait_ge(loaded, 16 * len(names))
            pe.transpose(turned[:, :], rows[:, :], ident[0:len(names) * KD, 0:len(names) * KD]).then_inc(turned_ok, 1)

        @block.vector
        def _(dve):
            dve.wait_ge(turned_ok, 1)
            dve.tensor_copy(cols[:, :], turned[:, :])
    cols = [cols[:, i * KD:(i + 1) * KD] for i in range(len(names))]
    return [(cols[0], cols[1]), (cols[2], cols[3])]


def build(nc, w, tables, out):
    with ExitStack() as ctx:
        def sb(name, shape, dt=F32):
            return ctx.enter_context(nc.sbuf_tensor(name, shape, dt))
        ident, zeros = sb("ident", [P, P]), sb("zeros", [P, D])
        flat = w["L0_attn_x"].rearrange("b l d -> (b l) d")
        result = out.rearrange("b l d -> (b l) d")
        rows = nc.dram_tensor("sorted_rows", (ROWS0, D), F32).ap()
        outs = nc.dram_tensor("expert_rows", (ROWS0, D), F32).ap()
        rows1 = nc.dram_tensor("sorted_rows1", (ROWS1, D), F32).ap()
        outs1 = nc.dram_tensor("expert_rows1", (ROWS1, D), F32).ap()
        x_kept2 = nc.dram_tensor("x_kept2", (N, D), F32).ap()
        oT_dram = nc.dram_tensor("oT", (D, N), F32).ap(), nc.dram_tensor("o_sums", (H1, N), F32).ap()
        x_kept = nc.dram_tensor("x_kept", (N, D), F32).ap()
        xT_dram = nc.dram_tensor("xT", (P, KD, N), F32).ap()
        setup_phase(nc, ident, zeros)
        with ExitStack() as s0:
            xn_a = s0.enter_context(nc.sbuf_tensor("xn_a", [P, T, D], F32))
            with ExitStack() as s1:
                x = s1.enter_context(nc.sbuf_tensor("x", [P, T, D], F32))
                y = s1.enter_context(nc.sbuf_tensor("y0", [P, T, D + 1], F32))
                r = make_router(nc, s1, ctx, "r0")
                with ExitStack() as s2:
                    xT = s2.enter_context(nc.sbuf_tensor("xT0", [P, KD, N], F32))
                    norm_phase(nc, "n0", x, ident, x_src=flat, xn=xn_a, xT_sb=xT, zero=(zeros, rows))
                    layer0_attention(nc, w, xn_a, xT, y, ident)
                    norm_phase(nc, "n1", x, ident, y=y, ysum=y[:, :, D], xn=xn_a, xT_sb=xT)
                    route_phase(nc, "r0", w["L0_ffn_gate_w"], True, xT, xn_a, ident, r, rows, None, shared=(w, y))
                layer0_experts(nc, w, r, rows, outs, ident)
                combine_phase(nc, "c0", r, outs, y)
                norm_phase(nc, "n2", x, ident, y=y, xn=xn_a, xT_dram=xT_dram, x_save=x_kept)
            clear_phase(nc)
            attention_phase(nc, "a1", True, ident, w=w, xT_dram=xT_dram, y=xn_a)
            gains = load_gains(nc, s0, w, ident)
            with ExitStack() as s1:
                qkv = s1.enter_context(nc.sbuf_tensor("qkv", [P, T, 3 * D], F32))
                with ExitStack() as s2:
                    hT = s2.enter_context(nc.sbuf_tensor("hT", [P, KD, N], F32))
                    with ExitStack() as s3:
                        x = s3.enter_context(nc.sbuf_tensor("x1", [P, T, D], F32))
                        norm_phase(nc, "n3", x, ident, y=xn_a, xn=xn_a, xT_sb=hT, twice=True, gain=gains[0],
                                   x_load=x_kept, x_save=x_kept2)
                    qkv_phase(nc, w, tables, hT, qkv)
                attention_phase(nc, "a2", False, ident, q_src=qkv, oT_dram=oT_dram)
            output_phase(nc, w, oT_dram, xn_a)
            clear_phase(nc)
            with ExitStack() as s1:
                r = make_router(nc, s1, ctx, "r1")
                with ExitStack() as s2:
                    xT = s2.enter_context(nc.sbuf_tensor("xT1", [P, KD, N], F32))
                    h_raw = s2.enter_context(nc.sbuf_tensor("h_raw", [P, T, D], F32))
                    norm_phase(nc, "n4", None, ident, y=xn_a, residual=False, xn=h_raw, xT_sb=xT, gain=gains[1],
                               zero=(zeros, rows1))
                    route_phase(nc, "r1", w["L1_ffn_Wgate"], False, xT, h_raw, ident, r, rows1, CAP)
                layer1_experts(nc, w, gains[1], rows1, outs1, ident)
                combine_phase(nc, "c1", r, outs1, xn_a)
            with ExitStack() as s1:
                x = s1.enter_context(nc.sbuf_tensor("x2", [P, T, D], F32))
                norm_phase(nc, "n5", x, ident, y=xn_a, x_load=x_kept2, out_dst=result)


_SHAPES = {
    "L0_attn_x": (B, L, D), "L0_attn_Wq": (D, D), "L0_attn_Wk": (D, D), "L0_attn_Wv": (D, D),
    "L0_attn_proj": (D, PROJ), "L0_ffn_gate_w": (E, D), "L0_ffn_w_gate": (E, D, F0), "L0_ffn_w_up": (E, D, F0),
    "L0_ffn_w_down": (E, F0, D), "L0_ffn_sw_gate": (D, FS), "L0_ffn_sw_up": (D, FS), "L0_ffn_sw_down": (FS, D),
    "L1_attn_Wq": (D, HA * DK), "L1_attn_Wk": (D, HA * DK), "L1_attn_Wv": (D, HA * DK), "L1_attn_Wo": (HA * DK, D),
    "L1_ffn_ln1_g": (D,), "L1_ffn_ln1_b": (D,), "L1_ffn_Wqkv": (D, 3 * D), "L1_ffn_Wproj": (D, D),
    "L1_ffn_ln2_g": (D,), "L1_ffn_ln2_b": (D,), "L1_ffn_Wgate": (D, E), "L1_ffn_W1": (E, D, F1),
    "L1_ffn_b1": (E, F1), "L1_ffn_W2": (E, F1, D), "L1_ffn_b2": (E, D),
}


def kernel(**inputs):
    import concourse.bacc as bacc
    from concourse.bass_utils import run_bass_kernel_spmd

    nc = bacc.Bacc("TRN2", target_bir_lowering=False, num_devices=1)
    arrays = {f"in_{name}": np.ascontiguousarray(inputs[name]) for name in _SHAPES}
    w = {name: nc.dram_tensor(f"in_{name}", shape, F32, kind="ExternalInput").ap() for name, shape in _SHAPES.items()}
    out = nc.dram_tensor("out", (B, L, D), F32, kind="ExternalOutput").ap()
    inv_freq = np.float32(1.0) / np.float32(10000.0) ** (np.arange(0, HD, 2, dtype=np.float32) / np.float32(HD))
    angle = np.arange(L, dtype=np.float32)[:, None] * inv_freq
    arrays["cos"], arrays["sin"] = np.cos(angle), np.sin(angle)
    tables = [nc.dram_tensor(name, (L, HD // 2), F32, kind="ExternalInput").ap() for name in ("cos", "sin")]
    build(nc, w, tables, out)
    return run_bass_kernel_spmd(nc, [arrays], core_ids=[0]).results[0]["out"]
```

```python
from contextlib import ExitStack

import numpy as np

import concourse.bass as bass
from concourse import mybir

F32 = mybir.dt.float32
F32R = mybir.dt.float32r
BF16 = mybir.dt.bfloat16
I32 = mybir.dt.int32
U32 = mybir.dt.uint32
ALU = mybir.AluOpType
ACT = mybir.ActivationFunctionType
AX = mybir.AxisListType

P = 128
B, L, D = 4, 1024, 256
N = B * L
T = N // P
TB = L // P
KD = D // P
LN_EPS = 1e-5

PROJ = 64
ATT_EPS = 1e-8

E = 8
F0, FS = 352, 704
ROUTE_SCALE = 2.5
BLK0 = (2 * N + E * (P - 1)) // P

HA, DK = 16, 64
H1, HD = 16, 16
F1 = 4 * D
CAP = 2 * N // E


def tiles_of(rows):
    return rows.rearrange("(t p) w -> p t w", p=P)


def spread(ap, n):
    return ap.unsqueeze(2).broadcast_to([ap.shape[0], ap.shape[1], n])


class Chain:

    def __init__(self, engine, sem):
        self.engine, self.sem, self.n = engine, sem, 0

    def step(self, instruction):
        self.n += 1
        instruction.then_inc(self.sem, 1)
        self.engine.wait_ge(self.sem, self.n)


def row_stats(dve, link, st, mean, var, tmp):
    link(dve.tensor_tensor(tmp, st[:, :, 1], st[:, :, 4], ALU.subtract))
    link(dve.tensor_tensor(tmp, tmp, tmp, ALU.mult))
    link(dve.tensor_tensor(mean, st[:, :, 1], st[:, :, 4], ALU.add))
    link(dve.tensor_scalar(mean, mean, 0.5, None, ALU.mult))
    link(dve.tensor_tensor(var, st[:, :, 2], st[:, :, 5], ALU.add))
    link(dve.tensor_scalar(var, var, 1.0 / D, None, ALU.mult))
    link(dve.scalar_tensor_tensor(out=var, in0=tmp, scalar=0.25, in1=var, op0=ALU.mult, op1=ALU.add))


def refine_rstd(dve, link, rstd, root, var_eps, tmp):
    link(dve.reciprocal(rstd, root))
    link(dve.tensor_tensor(tmp, rstd, rstd, ALU.mult))
    link(dve.tensor_tensor(tmp, tmp, var_eps, ALU.mult))
    link(dve.tensor_scalar(tmp, tmp, -0.5, 1.5, ALU.mult, ALU.add))
    link(dve.tensor_tensor(rstd, rstd, tmp, ALU.mult))


def norm_phase(nc, tag, x, ident, y=None, ysum=None, x_src=None, residual=True, xn=None, xT_sb=None,
               xT_dram=None, twice=False, gain=None, out_dst=None, x_save=None, x_load=None, zero=None, y_stats=None):
    last = out_dst is not None
    first = y is not None and residual
    src = x if residual else y
    ZEROS = 8
    LOADS = 4
    SAVES = 8
    with ExitStack() as ctx:
        def sb(name, shape, dt=F32):
            return ctx.enter_context(nc.sbuf_tensor(f"{tag}_{name}", shape, dt))

        def sem(name):
            return ctx.enter_context(nc.semaphore(f"{tag}_{name}"))

        st = sb("st", [P, T, 6])
        mean, var, root, rstd, rstd2, tmp, z, shift, shift2 = (
            sb(n, [P, T]) for n in ("mean", "var", "root", "rstd", "rstd2", "tmp", "z", "shift", "shift2"))
        ring = sb("ring", [P, 2, 2, D])
        ot = sb("ot", [P, 2, KD, 2 * P]) if xT_dram is not None else None
        tp = [ctx.enter_context(nc.psum_tensor(f"{tag}_tp{i}", [P, KD, 2 * P], F32)) for i in range(2)]
        x_in, chain, var_ok, root_ok, stats_ok, applied, added, tile_ok, turned, moved, saved, cleared, seen, shift_ok = (
            sem(n) for n in ("x_in", "chain", "var_ok", "root_ok", "stats_ok", "applied", "added", "tile_ok",
                             "turned", "moved", "saved", "cleared", "seen", "shift_ok"))
        seen_dve = sem("seen_dve")
        stored = [sem(f"stored{i}") for i in range(2)]
        src_in = [sem(f"src_in{c}") for c in range(LOADS)] if x_src is not None else None
        block = ctx.enter_context(nc.Block())
        n_roots = int(first) + (0 if last else 1) + int(twice)

        @block.sync
        def _(sp):
            if x_src is not None:
                for c, part in enumerate(src_in):
                    at = slice(c * (T // LOADS), (c + 1) * (T // LOADS))
                    sp.dma_start(x[:, at, :], tiles_of(x_src)[:, at, :]).then_inc(part, 16)
            if zero is not None:
                zeros, rows = zero
                n_rows = rows.shape[0] // P
                for c in range(ZEROS):
                    a, z_end = n_rows * c // ZEROS, n_rows * (c + 1) // ZEROS
                    sp.dma_start(tiles_of(rows)[:, a:z_end, :],
                                 zeros[:, :].unsqueeze(1).broadcast_to([P, z_end - a, D])).then_inc(cleared, 16)
            if x_load is not None:
                sp.dma_start(x[:, :, :], tiles_of(x_load)).then_inc(x_in, 16)
            if x_save is not None:
                sp.wait_ge(added, T)
                sp.dma_start(tiles_of(x_save), x[:, :, :]).then_inc(saved, 16)
                sp.wait_ge(saved, 16)
            if xT_dram is not None:
                for q in stored:
                    sp.sem_inc(q, 16)
                with sp.Fori(0, T // 4) as i:
                    for u in range(2):
                        s = i * 2 + u
                        sp.wait_ge(moved, s + 3)
                        sp.dma_start(xT_dram[:, :, bass.ds(s * 2 * P, 2 * P)], ot[:, u, :, :]).then_inc(stored[u], 16)
                for q in stored:
                    sp.wait_ge(q, 16 + 16 * (T // 4))
            if last:
                for c in range(SAVES):
                    at = slice(T // SAVES * c, T // SAVES * (c + 1))
                    sp.wait_ge(added, T // SAVES * (c + 1))
                    sp.dma_start(tiles_of(out_dst)[:, at, :], x[:, at, :]).then_inc(saved, 16)
                sp.wait_ge(saved, 16 * SAVES)
            if zero is not None:
                sp.wait_ge(cleared, 16 * ZEROS)

        @block.vector
        def _(dve):
            link = Chain(dve, chain).step
            rounds = [0, 0]

            def stats(rows, parts=(None,)):
                n = T // len(parts)
                for c, part in enumerate(parts):
                    if part is not None:
                        dve.wait_ge(part, 16)
                    with dve.Fori(c * n // 4, (c + 1) * n // 4) as i:
                        for u in range(4):
                            dve.bn_stats(st[:, i * 4 + u, :], rows[:, i * 4 + u, 0:D]).then_inc(stats_ok, 1)
                rounds[0] += 1
                dve.wait_ge(stats_ok, T * rounds[0])
                row_stats(dve, link, st, mean[:, :], var[:, :], tmp[:, :])

            def inverse_root(v, r):
                dve.tensor_scalar(v, v, LN_EPS, None, ALU.add).then_inc(var_ok, 1)
                rounds[1] += 1
                dve.wait_ge(var_ok, rounds[1])
                dve.wait_ge(root_ok, rounds[1])
                refine_rstd(dve, link, r, root[:, :], v, tmp[:, :])

            if first:
                if y_stats is None:
                    stats(y)
                else:
                    row_stats(dve, link, y_stats, mean[:, :], var[:, :], tmp[:, :])
                if ysum is not None:
                    link(dve.tensor_scalar(z[:, :], ysum, ATT_EPS, None, ALU.add))
                    link(dve.reciprocal(z[:, :], z[:, :]))
                    link(dve.tensor_tensor(var[:, :], var[:, :], z[:, :], ALU.mult))
                    link(dve.tensor_tensor(var[:, :], var[:, :], z[:, :], ALU.mult))
                inverse_root(var[:, :], rstd[:, :])
                if ysum is not None:
                    link(dve.tensor_tensor(rstd[:, :], rstd[:, :], z[:, :], ALU.mult))
                dve.scalar_tensor_tensor(out=shift[:, :], in0=mean[:, :], scalar=-1.0, in1=rstd[:, :],
                                         op0=ALU.mult, op1=ALU.mult).then_inc(shift_ok, 1)
                if x_load is not None:
                    dve.wait_ge(x_in, 16)
                with dve.Fori(0, T // 4) as i:
                    dve.wait_ge(applied, i * 4 + 4)
                    dve.sem_inc(seen_dve, 1)
                    for u in range(4):
                        t = i * 4 + u
                        dve.tensor_tensor(x[:, t, :], x[:, t, :], y[:, t, 0:D], ALU.add).then_inc(added, 1)
                dve.wait_ge(added, T)
            if last:
                return
            stats(src, (None,) if src_in is None else src_in)
            inverse_root(var[:, :], rstd[:, :])
            if twice:
                link(dve.tensor_tensor(var[:, :], rstd[:, :], rstd[:, :], ALU.mult))
                link(dve.tensor_scalar(var[:, :], var[:, :], -LN_EPS, 1.0, ALU.mult, ALU.add))
                inverse_root(var[:, :], rstd2[:, :])
                link(dve.tensor_tensor(rstd2[:, :], rstd2[:, :], rstd[:, :], ALU.mult))
            for_turn = rstd2 if twice else rstd
            dve.scalar_tensor_tensor(out=shift2[:, :], in0=mean[:, :], scalar=-1.0, in1=rstd[:, :],
                                     op0=ALU.mult, op1=ALU.mult).then_inc(shift_ok, 1)
            with dve.Fori(0, T // 4) as i:
                for u in range(2):
                    s = i * 2 + u
                    dve.wait_ge(turned, s + 1)
                    for v in range(2):
                        t = s * 2 + v
                        dve.tensor_scalar(ring[:, u, v, :], src[:, t, 0:D], mean[:, bass.ds(t, 1)],
                                          for_turn[:, bass.ds(t, 1)], ALU.subtract, ALU.mult).then_inc(tile_ok, 1)
                    t = s * 2
                    dve.tensor_scalar(xn[:, t, :], src[:, t, 0:D], mean[:, bass.ds(t, 1)],
                                      rstd[:, bass.ds(t, 1)], ALU.subtract, ALU.mult)

        @block.scalar
        def _(act):
            if not last:
                act.sem_inc(moved, 2)
            for r in range(n_roots):
                act.wait_ge(var_ok, r + 1)
                act.activation(root[:, :], var[:, :], ACT.Sqrt).then_inc(root_ok, 1)
                if first and r == 0:
                    act.wait_ge(shift_ok, 1)
                    with act.Fori(0, T // 4) as i:
                        for u in range(4):
                            t = i * 4 + u
                            act.activation(y[:, t, 0:D], y[:, t, 0:D], ACT.Identity, scale=rstd[:, bass.ds(t, 1)],
                                           bias=shift[:, bass.ds(t, 1)]).then_inc(applied, 1)
            if last:
                return
            act.wait_ge(shift_ok, int(first) + 1)
            with act.Fori(0, T // 4) as i:
                for u in range(2):
                    s = i * 2 + u
                    act.activation(xn[:, s * 2 + 1, :], src[:, s * 2 + 1, 0:D], ACT.Identity,
                                   scale=rstd[:, bass.ds(s * 2 + 1, 1)], bias=shift2[:, bass.ds(s * 2 + 1, 1)])
                    act.wait_ge(turned, s + 3)
                    if xT_dram is not None:
                        act.wait_ge(stored[u], 16 * (i + 1))
                    if gain is None:
                        dst = ot[:, u, :, :] if xT_dram is not None else xT_sb[:, :, bass.ds(s * 2 * P, 2 * P)]
                        act.activation(dst, tp[u][:, :, :], ACT.Copy).then_inc(moved, 1)
                    else:
                        act.sem_inc(seen, 1)
                        for k in range(KD):
                            m = act.activation(xT_sb[:, k, bass.ds(s * 2 * P, 2 * P)], tp[u][:, k, :], ACT.Identity,
                                               scale=gain[0][:, k:k + 1], bias=gain[1][:, k:k + 1])
                        m.then_inc(moved, 1)

        @block.tensor
        def _(pe):
            if last:
                return
            pe.sem_inc(turned, 2)
            with pe.Fori(0, T // 4) as i:
                for u in range(2):
                    s = i * 2 + u
                    pe.wait_ge(tile_ok, 2 * s + 2)
                    pe.wait_ge(moved, s + 1)
                    for k in range(KD):
                        for v in range(2):
                            m = pe.transpose(tp[u][:, k, v * P:(v + 1) * P], ring[:, u, v, k * P:(k + 1) * P],
                                             ident[:, :])
                    m.then_inc(turned, 1)


def setup_phase(nc, ident, zeros):
    with ExitStack() as ctx:
        made = ctx.enter_context(nc.semaphore("setup_made"))
        block = ctx.enter_context(nc.Block())

        @block.gpsimd
        def _(pool):
            pool.memset(zeros[:, :], 0.0)
            pool.memset(ident[:, :], 0.0).then_inc(made, 1)
            pool.wait_ge(made, 1)
            pool.affine_select(out=ident[:, :], in_=ident[:, :], compare_op=ALU.not_equal, fill=1.0, base=0,
                               pattern=[[-1, P]], channel_multiplier=1)


def layer0_attention(nc, w, xn, xT, y, ident):
    C = 512
    with ExitStack() as ctx:
        def sb(name, shape, dt=F32):
            return ctx.enter_context(nc.sbuf_tensor(f"a0_{name}", shape, dt))

        def ps(name, shape):
            return ctx.enter_context(nc.psum_tensor(f"a0_{name}", shape, F32))

        def sem(name):
            return ctx.enter_context(nc.semaphore(f"a0_{name}"))

        wq, wk, wv = (sb(n, [P, KD, D]) for n in ("wq", "wk", "wv"))
        proj = sb("proj", [P, KD, PROJ])
        map_w = sb("map_w", [P, KD, 2 * PROJ])
        wvT = sb("wvT", [P, KD, D])
        low = sb("low", [P, 2, C])
        fm = sb("fm", [P, 2, C])
        kt = sb("kt", [P, TB, PROJ])
        kx = sb("kx", [P, D])
        kxT = sb("kxT", [P, KD, PROJ])
        kv = sb("kv", [PROJ, D + 1])
        pre = [ps(f"pre{i}", [P, C]) for i in range(2)]
        turn = [ps(f"turn{i}", [P, 4, P]) for i in range(2)]
        small = ps("small", [P, 512])
        num = [ps(f"num{i}", [P, 512]) for i in range(2)]
        w_in, w_turned, w_ok, pre_ok, low_ok, exp_ok, fm_ok, turn_ok, kt_ok, mid, mid_ok, num_ok, y_ok, ones_ok = (
            sem(n) for n in ("w_in", "w_turned", "w_ok", "pre_ok", "low_ok", "exp_ok", "fm_ok", "turn_ok", "kt_ok",
                             "mid", "mid_ok", "num_ok", "y_ok", "ones_ok"))
        block = ctx.enter_context(nc.Block())

        @block.sync
        def _(sp):
            for dst, src in ((wq, w["L0_attn_Wq"]), (wk, w["L0_attn_Wk"]), (wv, w["L0_attn_Wv"]),
                             (proj, w["L0_attn_proj"])):
                sp.dma_start(dst[:, :, :], src.rearrange("(k p) n -> p k n", p=P)).then_inc(w_in, 16)

        @block.gpsimd
        def _(pool):
            pool.memset(kx[:, :], 0.0)
            pool.memset(kv[:, :], 1.0).then_inc(ones_ok, 1)

        @block.tensor
        def _(pe):
            pe.wait_ge(w_in, 64)
            for s, wt in enumerate((wq, wk)):
                for kd in range(KD):
                    for ke in range(KD):
                        pe.matmul(turn[0][:, s * KD + kd, 0:PROJ], wt[:, ke, kd * P:(kd + 1) * P], proj[:, ke, :],
                                  start=(ke == 0), stop=(ke == KD - 1))
            for ke in range(KD):
                for kd in range(KD):
                    m = pe.transpose(turn[1][:, ke * KD + kd, :], wv[:, kd, ke * P:(ke + 1) * P], ident[:, :])
            m.then_inc(w_turned, 1)
            pe.wait_ge(w_ok, 2)
            with pe.Fori(0, B) as b:
                for c in range(2):
                    for k in range(KD):
                        m = pe.matmul(pre[c][:, :], map_w[:, k, :], xT[:, k, bass.ds(b * L + c * C, C)],
                                      start=(k == 0), stop=(k == KD - 1))
                    m.then_inc(pre_ok, 1)
                for c in range(2):
                    pe.wait_ge(fm_ok, b * 2 + c + 1)
                    for t in range(4):
                        m = pe.transpose(turn[c][:, t, :], fm[:, c, t * P:(t + 1) * P], ident[:, :])
                    m.then_inc(turn_ok, 1)
                pe.wait_ge(kt_ok, b * 2 + 2)
                for t in range(TB):
                    m = pe.matmul(small[0:PROJ, 0:D], kt[:, t, :], xn[:, b * TB + t, :],
                                  start=(t == 0), stop=(t == TB - 1))
                m.then_inc(mid, 1)
                pe.wait_ge(mid_ok, b * 3 + 1)
                for k in range(KD):
                    m = pe.transpose(small[:, k * P:(k + 1) * P], kx[:, k * P:(k + 1) * P], ident[:, :])
                m.then_inc(mid, 1)
                pe.wait_ge(mid_ok, b * 3 + 2)
                for k in range(KD):
                    m = pe.matmul(small[0:PROJ, 0:D], kxT[:, k, :], wvT[:, k, :], start=(k == 0), stop=(k == KD - 1))
                m.then_inc(mid, 1)
                pe.wait_ge(mid_ok, b * 3 + 3)
                for t in range(TB):
                    pe.wait_ge(y_ok, b * TB + t + 1)
                    pe.matmul(num[t % 2][:, 0:D + 1], fm[0:PROJ, t // 4, t % 4 * P:(t % 4 + 1) * P], kv[:, :],
                              start=True, stop=True).then_inc(num_ok, 1)

        @block.vector
        def _(dve):
            dve.wait_ge(w_turned, 1)
            dve.tensor_copy(map_w[:, :, 0:PROJ], turn[0][:, 0:2, 0:PROJ])
            dve.tensor_copy(map_w[:, :, PROJ:2 * PROJ], turn[0][:, 2:4, 0:PROJ]).then_inc(w_ok, 1)
            dve.tensor_copy(wvT[:, :, :], turn[1][:, :, :].rearrange("p (k c) n -> p k (c n)", k=KD)).then_inc(w_ok, 1)
            dve.wait_ge(ones_ok, 1)
            with dve.Fori(0, B) as b:
                for c in range(2):
                    dve.wait_ge(pre_ok, b * 2 + c + 1)
                    dve.tensor_scalar(low[:, c, :], pre[c][:, :], 0.0, None, ALU.min).then_inc(low_ok, 1)
                for c in range(2):
                    dve.wait_ge(exp_ok, b * 2 + c + 1)
                    if c == 0:
                        dve.wait_ge(num_ok, b * TB)
                    dve.scalar_tensor_tensor(out=fm[:, c, :], in0=pre[c][:, :], scalar=0.0, in1=low[:, c, :],
                                             op0=ALU.max, op1=ALU.add).then_inc(fm_ok, 1)
                for c in range(2):
                    dve.wait_ge(turn_ok, b * 2 + c + 1)
                    dve.tensor_copy(kt[:, c * 4:c * 4 + 4, :], turn[c][:, :, PROJ:2 * PROJ]).then_inc(kt_ok, 1)
                dve.wait_ge(mid, b * 3 + 1)
                dve.tensor_copy(kx[0:PROJ, :], small[0:PROJ, 0:D]).then_inc(mid_ok, 1)
                dve.wait_ge(mid, b * 3 + 2)
                dve.tensor_copy(kxT[:, :, :], small[:, 0:KD * P].rearrange("p (k n) -> p k n", k=KD)[:, :, 0:PROJ])\
                   .then_inc(mid_ok, 1)
                dve.wait_ge(mid, b * 3 + 3)
                dve.tensor_copy(kv[:, 0:D], small[0:PROJ, 0:D]).then_inc(mid_ok, 1)

        @block.scalar
        def _(act):
            act.sem_inc(y_ok, 2)
            with act.Fori(0, B) as b:
                for c in range(2):
                    act.wait_ge(low_ok, b * 2 + c + 1)
                    act.activation(low[:, c, :], low[:, c, :], ACT.Exp).then_inc(exp_ok, 1)
                for t in range(TB):
                    act.wait_ge(num_ok, b * TB + t + 1)
                    act.activation(y[:, b * TB + t, :], num[t % 2][:, 0:D + 1], ACT.Copy).then_inc(y_ok, 1)


def clear_phase(nc):
    spent = sorted(nc.released_uncleared_semaphores)
    with nc.Block() as block:

        @block.gpsimd
        def _(pool):
            start = 0
            for i in range(1, len(spent) + 1):
                if i == len(spent) or spent[i] != spent[i - 1] + 1:
                    pool.sem_clear(range(spent[start], spent[i - 1] + 1))
                    start = i


ROWS0 = (BLK0 + 1) // 2 * 2 * P
BLOCKS0 = ROWS0 // P
ROWS1 = E * CAP
FETCHES = 4
FAR = 1 << 20


def make_router(nc, ctx, whole, tag):
    def sem(name):
        return whole.enter_context(nc.semaphore(f"{tag}_{name}"))

    def sb(name, shape, dt=F32):
        return ctx.enter_context(nc.sbuf_tensor(f"{tag}_{name}", shape, dt))
    return {"put": [sb(f"put{i}", [P, T], U32) for i in range(2)],
            "take": [sb(f"take{i}", [P, T], U32) for i in range(2)],
            "weight": [sb(f"weight{i}", [P, T]) for i in range(2)],
            "expert": sb("expert", [P, BLOCKS0], I32),
            "scattered": sem("scattered"),
            "fetched": [[sem(f"fetched{u}_{i}") for i in range(2)] for u in range(FETCHES)]}


def route_phase(nc, tag, gate, gate_is_rows, xT, xn, ident, r, rows, capacity, shared=None):
    C = 512
    FT = (FS + P - 1) // P
    n_chunks = N // C
    with ExitStack() as ctx:
        def sb(name, shape, dt=F32):
            return ctx.enter_context(nc.sbuf_tensor(f"{tag}_{name}", shape, dt))

        def ps(name, shape):
            return ctx.enter_context(nc.psum_tensor(f"{tag}_{name}", shape, F32))

        def sem(name):
            return ctx.enter_context(nc.semaphore(f"{tag}_{name}"))

        gw = sb("gw", [P, KD, E])
        gw_rows = sb("gw_rows", [E, D])
        logT = sb("logT", [E, 2, C])
        s, one, two, mask, work, offs = (sb(n, [P, T, E]) for n in ("s", "one", "two", "mask", "work", "offs"))
        rank = sb("rank", [P, T, E])
        col, m1, m2, keep = (sb(n, [P, T]) for n in ("col", "m1", "m2", "keep"))
        before = sb("before", [P, P])
        ones = sb("ones", [P, P])
        count, blocks, end, end2 = (sb(n, [P, E]) for n in ("count", "blocks", "end", "end2"))
        edge = sb("edge", [P, E, T])
        cmp = sb("cmp", [P, E, T])
        slot_no = sb("slot_no", [P, BLOCKS0, E])
        cmp2 = sb("cmp2", [P, BLOCKS0, E])
        base = sb("base", [P, E])
        expert_f = sb("expert_f", [P, BLOCKS0])
        pl = ps("pl", [P, 512])
        pt = ps("pt", [P, T, E])
        pc = ps("pc", [P, 2, T * E])
        (w_in, gw_turned, gw_ok, log_ok, logs_in, turned, made, chain, low_ok, exp_ok, mask_ok, counted, slots_ok,
         sh_in, up_ok, silu_ok, hid_ok, down_ok, out_ok) = (sem(n) for n in (
             "w_in", "gw_turned", "gw_ok", "log_ok", "logs_in", "turned", "made", "chain", "low_ok", "exp_ok",
             "mask_ok", "counted", "slots_ok", "sh_in", "up_ok", "silu_ok", "hid_ok", "down_ok",
             "out_ok"))
        padded = sem("padded")
        if shared is not None:
            sw, y = shared
            wg, wu = (sb(n, [P, KD, FT * P]) for n in ("wg", "wu"))
            wd = sb("wd", [P, FT, D])
            act_g = sb("act_g", [P, 2, C])
            hid = sb("hid", [P, FT, C])
            pg = [ps(f"pg{i}", [P, C]) for i in range(2)]
            pu = [ps(f"pu{i}", [P, C]) for i in range(2)]
            pd = ps("pd", [P, 2, D])
        block = ctx.enter_context(nc.Block())

        def shared_up(pe, c):
            if isinstance(c, int):
                pe.wait_ge(sh_in, 64)
            for f in range(FT):
                q = c * FT + f
                pe.wait_ge(hid_ok, q + 1)
                for wt, pp in ((wg, pg), (wu, pu)):
                    for k in range(KD):
                        m = pe.matmul(pp[f % 2][:, :], wt[:, k, f * P:(f + 1) * P],
                                      xT[:, k, bass.ds(c * C, C)], start=(k == 0), stop=(k == KD - 1))
                m.then_inc(up_ok, 1)

        def shared_down(pe, c):
            for h in range(C // P // 2):
                pe.wait_ge(out_ok, c * 2 + h)
                for v in range(2):
                    for f in range(FT):
                        t = h * 2 + v
                        if t == 0:
                            pe.wait_ge(hid_ok, c * FT + f + 3)
                        m = pe.matmul(pd[:, v, :], hid[:, f, t * P:(t + 1) * P], wd[:, f, :],
                                      start=(f == 0), stop=(f == FT - 1))
                m.then_inc(down_ok, 1)

        def shared_act(act, c):
            for f in range(FT):
                q = c * FT + f
                act.wait_ge(up_ok, q + 1)
                act.wait_ge(hid_ok, q + 1)
                act.activation(act_g[:, f % 2, :], pg[f % 2][:, :], ACT.Silu).then_inc(silu_ok, 1)
            for h in range(C // P // 2):
                act.wait_ge(down_ok, c * 2 + h + 1)
                act.activation(y[:, bass.ds(c * (C // P) + h * 2, 2), 0:D], pd[:, :, :], ACT.Copy).then_inc(out_ok, 1)

        def shared_mul(dve, c):
            for f in range(FT):
                q = c * FT + f
                dve.wait_ge(silu_ok, q + 1)
                if f == 0:
                    dve.wait_ge(down_ok, c * 2)
                dve.tensor_tensor(hid[:, f, :], act_g[:, f % 2, :], pu[f % 2][:, :], ALU.mult)\
                   .then_inc(hid_ok, 1)

        @block.sync
        def _(sp):
            if gate_is_rows:
                sp.dma_start(gw_rows[:, :], gate).then_inc(w_in, 16)
            else:
                sp.dma_start(gw[:, :, :], gate.rearrange("(k p) e -> p k e", p=P)).then_inc(w_in, 16)
            if shared is not None:
                for dst, name in ((wg, "L0_ffn_sw_gate"), (wu, "L0_ffn_sw_up")):
                    sp.dma_start(dst[:, :, 0:FS], sw[name].rearrange("(k p) n -> p k n", p=P)).then_inc(sh_in, 16)
                full, rest = FS // P, FS % P
                sp.wait_ge(padded, 1)
                sp.dma_start(wd[:, 0:full, :], sw["L0_ffn_sw_down"][0:full * P, :].rearrange("(k p) n -> p k n", p=P))\
                  .then_inc(sh_in, 16)
                sp.dma_start(wd[0:rest, full, :], sw["L0_ffn_sw_down"][full * P:FS, :]).then_inc(sh_in, 16)

        @block.tensor
        def _(pe):
            pe.wait_ge(w_in, 16)
            if gate_is_rows:
                for k in range(KD):
                    m = pe.transpose(pl[:, k * E:(k + 1) * E], gw_rows[:, k * P:(k + 1) * P], ident[0:E, 0:E])
                m.then_inc(gw_turned, 1)
                pe.wait_ge(gw_ok, 1)
            for c in range(n_chunks):
                if c >= 1:
                    pe.wait_ge(log_ok, c)
                for k in range(KD):
                    m = pe.matmul(pl[0:E, :], gw[:, k, :], xT[:, k, c * C:(c + 1) * C],
                                  start=(k == 0), stop=(k == KD - 1))
                m.then_inc(logs_in, 1)
                pe.wait_ge(log_ok, c + 1)
                for t in range(C // P):
                    m = pe.transpose(pt[:, c * (C // P) + t, :], logT[:, c % 2, t * P:(t + 1) * P], ident[0:E, 0:E])
                m.then_inc(turned, 1)
            if shared is not None:
                shared_up(pe, 0)
                shared_down(pe, 0)
            pe.wait_ge(mask_ok, 1)
            pe.wait_ge(made, 3)
            pe.matmul(pc[:, 0, :], before[:, :], mask[:, :, :].rearrange("p t e -> p (t e)"), start=True, stop=True)
            pe.matmul(pc[:, 1, :], ones[:, :], mask[:, :, :].rearrange("p t e -> p (t e)"),
                      start=True, stop=True).then_inc(counted, 1)
            if shared is not None:
                with pe.Fori(1, n_chunks) as c:
                    shared_up(pe, c)
                    shared_down(pe, c)

        @block.scalar
        def _(act):
            for c in range(n_chunks):
                act.wait_ge(logs_in, c + 1)
                if c >= 2:
                    act.wait_ge(turned, c - 1)
                act.activation(logT[:, c % 2, :], pl[0:E, :], ACT.Copy).then_inc(log_ok, 1)
            if shared is not None:
                shared_act(act, 0)
            act.wait_ge(low_ok, 1)
            act.activation(s[:, :, :], s[:, :, :], ACT.Exp).then_inc(exp_ok, 1)
            if shared is not None:
                with act.Fori(1, n_chunks) as c:
                    shared_act(act, c)

        @block.vector
        def _(dve):
            link = Chain(dve, chain).step
            if shared is not None:
                dve.sem_inc(hid_ok, 2)
            if gate_is_rows:
                dve.wait_ge(gw_turned, 1)
                dve.tensor_copy(gw[:, :, :], pl[:, 0:KD * E].rearrange("p (k e) -> p k e", k=KD)).then_inc(gw_ok, 1)
            dve.wait_ge(turned, n_chunks)
            link(dve.tensor_reduce(col[:, :], pt[:, :, :], AX.X, ALU.max))
            dve.tensor_tensor(s[:, :, :], pt[:, :, :], spread(col[:, :], E), ALU.subtract).then_inc(low_ok, 1)
            if shared is not None:
                shared_mul(dve, 0)
            dve.wait_ge(exp_ok, 1)
            link(dve.tensor_reduce(col[:, :], s[:, :, :], AX.X, ALU.add))
            link(dve.reciprocal(col[:, :], col[:, :]))
            link(dve.tensor_tensor(s[:, :, :], s[:, :, :], spread(col[:, :], E), ALU.mult))
            dve.wait_ge(made, 3)

            def pick(best, hot):
                link(dve.tensor_reduce(best[:, :], s[:, :, :], AX.X, ALU.max))
                link(dve.tensor_tensor(work[:, :, :], s[:, :, :], spread(best[:, :], E), ALU.is_ge))
                link(dve.tensor_tensor(work[:, :, :], work[:, :, :], rank[:, :, :], ALU.mult))
                link(dve.tensor_reduce(col[:, :], work[:, :, :], AX.X, ALU.max))
                link(dve.tensor_tensor(hot[:, :, :], work[:, :, :], spread(col[:, :], E), ALU.is_equal))

            pick(m1, one)
            link(dve.scalar_tensor_tensor(out=s[:, :, :], in0=one[:, :, :], scalar=-2.0, in1=s[:, :, :],
                                          op0=ALU.mult, op1=ALU.add))
            pick(m2, two)
            dve.tensor_tensor(mask[:, :, :], one[:, :, :], two[:, :, :], ALU.add).then_inc(mask_ok, 1)
            dve.wait_ge(counted, 1)
            whole = pc[:, 1, :].rearrange("p (t e) -> p t e", e=E)
            link(dve.tensor_copy(work[:, :, :], whole))
            a, b2 = work, s
            step = 1
            while step < T:
                dve.tensor_copy(b2[:, 0:step, :], a[:, 0:step, :])
                link(dve.tensor_tensor(b2[:, step:T, :], a[:, step:T, :], a[:, 0:T - step, :], ALU.add))
                a, b2 = b2, a
                step *= 2
            link(dve.tensor_copy(count[:, :], a[:, T - 1, :]))
            link(dve.tensor_tensor(offs[:, :, :], a[:, :, :], whole, ALU.subtract))
            link(dve.tensor_tensor(offs[:, :, :], offs[:, :, :], pc[:, 0, :].rearrange("p (t e) -> p t e", e=E),
                                   ALU.add))
            if capacity is None:
                link(dve.tensor_tensor(cmp[:, :, :], spread(count[:, :], T), edge[:, :, :], ALU.is_gt))
                link(dve.tensor_reduce(blocks[:, :], cmp[:, :, :], AX.X, ALU.add))
                a2, b3 = end, end2
                link(dve.tensor_copy(a2[:, :], blocks[:, :]))
                step = 1
                while step < E:
                    dve.tensor_copy(b3[:, 0:step], a2[:, 0:step])
                    link(dve.tensor_tensor(b3[:, step:E], a2[:, step:E], a2[:, 0:E - step], ALU.add))
                    a2, b3 = b3, a2
                    step *= 2
                link(dve.tensor_tensor(base[:, :], a2[:, :], blocks[:, :], ALU.subtract))
                link(dve.tensor_scalar(base[:, :], base[:, :], float(P), None, ALU.mult))
                link(dve.tensor_tensor(cmp2[:, :, :], slot_no[:, :, :],
                                       a2[:, :].unsqueeze(1).broadcast_to([P, BLOCKS0, E]), ALU.is_ge))
                link(dve.tensor_reduce(expert_f[:, :], cmp2[:, :, :], AX.X, ALU.add))
                dve.tensor_scalar(r["expert"][:, :], expert_f[:, :], float(E - 1), None, ALU.min)
            hots = ((one, m1, 0), (two, m2, 1))
            if capacity is not None:
                for hot, best, i in hots:
                    link(dve.tensor_tensor(work[:, :, :], offs[:, :, :], hot[:, :, :], ALU.mult))
                    link(dve.tensor_reduce(keep[:, :], work[:, :, :], AX.X, ALU.add))
                    link(dve.tensor_scalar(keep[:, :], keep[:, :], float(capacity), None, ALU.is_lt))
                    link(dve.tensor_tensor(r["weight"][i][:, :], best[:, :], keep[:, :], ALU.mult))
                    link(dve.tensor_tensor(work[:, :, :], offs[:, :, :],
                                           base[:, :].unsqueeze(1).broadcast_to([P, T, E]), ALU.add))
                    link(dve.tensor_tensor(work[:, :, :], work[:, :, :], hot[:, :, :], ALU.mult))
                    link(dve.tensor_reduce(col[:, :], work[:, :, :], AX.X, ALU.add))
                    link(dve.tensor_tensor(col[:, :], col[:, :], keep[:, :], ALU.mult))
                    dve.tensor_copy(r["take"][i][:, :], col[:, :])
                    link(dve.tensor_scalar(keep[:, :], keep[:, :], -float(FAR), float(FAR), ALU.mult, ALU.add))
                    dve.tensor_tensor(r["put"][i][:, :], col[:, :], keep[:, :], ALU.add).then_inc(slots_ok, 1)
                    dve.wait_ge(slots_ok, i + 1)
            else:
                link(dve.tensor_tensor(offs[:, :, :], offs[:, :, :],
                                       base[:, :].unsqueeze(1).broadcast_to([P, T, E]), ALU.add))
                for hot, best, i in hots:
                    link(dve.tensor_tensor(work[:, :, :], offs[:, :, :], hot[:, :, :], ALU.mult))
                    link(dve.tensor_reduce(col[:, :], work[:, :, :], AX.X, ALU.add))
                    dve.tensor_copy(r["take"][i][:, :], col[:, :])
                    dve.tensor_copy(r["put"][i][:, :], col[:, :]).then_inc(slots_ok, 1)
                    dve.wait_ge(slots_ok, i + 1)
            if capacity is None:
                link(dve.tensor_tensor(col[:, :], m1[:, :], m2[:, :], ALU.add))
                link(dve.tensor_scalar(col[:, :], col[:, :], 1e-20, None, ALU.add))
                link(dve.reciprocal(col[:, :], col[:, :]))
                link(dve.tensor_scalar(col[:, :], col[:, :], ROUTE_SCALE, None, ALU.mult))
                for best, i in ((m1, 0), (m2, 1)):
                    dve.tensor_tensor(r["weight"][i][:, :], best[:, :], col[:, :], ALU.mult)
            if shared is not None:
                with dve.Fori(1, n_chunks) as c:
                    shared_mul(dve, c)

        @block.gpsimd
        def _(pool):
            if shared is not None:
                pool.memset(wg[:, :, FS:FT * P], 0.0)
                pool.memset(wu[:, :, FS:FT * P], 0.0)
                pool.memset(wd[:, FT - 1, :], 0.0).then_inc(padded, 1)
            pool.iota(rank[:, :, :], pattern=[[0, T], [-1, E]], base=E, channel_multiplier=0,
                      allow_small_or_imprecise_dtypes=True)
            pool.iota(edge[:, :, :], pattern=[[0, E], [P, T]], base=0, channel_multiplier=0,
                      allow_small_or_imprecise_dtypes=True)
            pool.iota(slot_no[:, :, :], pattern=[[1, BLOCKS0], [0, E]], base=0, channel_multiplier=0,
                      allow_small_or_imprecise_dtypes=True)
            if capacity is not None:
                pool.iota(base[:, :], pattern=[[capacity, E]], base=0, channel_multiplier=0,
                          allow_small_or_imprecise_dtypes=True)
            pool.memset(ones[:, :], 1.0)
            pool.memset(before[:, :], 1.0).then_inc(made, 2)
            pool.wait_ge(made, 2)
            pool.affine_select(out=before[:, :], in_=before[:, :], compare_op=ALU.is_gt, fill=0.0, base=0,
                               pattern=[[1, P]], channel_multiplier=-1).then_inc(made, 1)
            for i in range(2):
                pool.wait_ge(slots_ok, i + 1)
                for t in range(T):
                    pool.indirect_dma_start(rows[:, :], bass.IndirectOffsetOnAxis(ap=r["put"][i][:, t:t + 1], axis=0),
                                            xn[:, t, :], None, bounds_check=rows.shape[0] - 1, oob_is_err=False)\
                        .then_inc(r["scattered"], 16)
            pool.wait_ge(r["scattered"], 16 * 2 * T)


def layer0_experts(nc, w, r, rows, outs, ident):
    FT = (F0 + P - 1) // P
    R = 4
    GROUPS = BLOCKS0 // R
    with ExitStack() as ctx:
        def sb(name, shape, dt=F32):
            return ctx.enter_context(nc.sbuf_tensor(f"e0_{name}", shape, dt))

        def ps(name, shape):
            return ctx.enter_context(nc.psum_tensor(f"e0_{name}", shape, F32))

        def sem(name):
            return ctx.enter_context(nc.semaphore(f"e0_{name}"))

        wg, wu = (sb(n, [P, KD, E * F0]) for n in ("wg", "wu"))
        wd = sb("wd", [P, FT, E * D])
        xg = sb("xg", [P, R, D])
        xgT = sb("xgT", [P, 2, KD, P])
        sg = sb("sg", [P, 2, F0])
        h = sb("h", [P, 2, F0])
        hT = sb("hT", [P, 2, FT, P])
        yo = sb("yo", [P, 2, D])
        px = ps("px", [P, KD, P])
        pg = [ps(f"pg{i}", [P, 512]) for i in range(2)]
        pu = [ps(f"pu{i}", [P, 512]) for i in range(2)]
        ph = ps("ph", [P, FT, P])
        py = ps("py", [P, D])
        w_in, x_turned, xT_ok, up_ok, silu_ok, h_ok, h_turned, hT_ok, y_done, y_ok = (
            sem(n) for n in ("w_in", "x_turned", "xT_ok", "up_ok", "silu_ok", "h_ok", "h_turned", "hT_ok",
                             "y_done", "y_ok"))
        x_in = [sem(f"x_in{i}") for i in range(R)]
        stored = [sem(f"stored{i}") for i in range(2)]
        block = ctx.enter_context(nc.Block())

        def width(f):
            return min(P, F0 - f * P)

        def walk(engine, step):
            for u in range(R):
                step(u, u, 0, u >= 1, R + 1)
            with engine.Fori(1, GROUPS - 1) as g:
                for u in range(R):
                    step(g * R + u, u, g, True, R + 1)
            for u in range(R):
                step((GROUPS - 1) * R + u, u, GROUPS - 1, True, R - u)
            step(GROUPS * R, 0, GROUPS, True, 0)

        @block.sync
        def _(sp):
            x_rows = rows.rearrange("(j p) d -> j p d", p=P)
            y_rows = outs.rearrange("(j p) d -> j p d", p=P)

            def load(j, slot):
                sp.dma_start(xg[:, slot, :], x_rows[bass.ds(j, 1), :, :].rearrange("o p d -> p (o d)"))\
                  .then_inc(x_in[slot], 16)

            def store(j, slot):
                sp.wait_ge(y_ok, j + 1)
                sp.dma_start(y_rows[bass.ds(j, 1), :, :].rearrange("o p d -> p (o d)"), yo[:, slot, :])\
                  .then_inc(stored[slot], 16)

            for j in range(R - 1):
                load(j, j)
            for dst, name, width_all in ((wg, "L0_ffn_w_gate", D), (wu, "L0_ffn_w_up", D), (wd, "L0_ffn_w_down", F0)):
                for k in range((width_all + P - 1) // P):
                    n = min(P, width_all - k * P)
                    sp.dma_start(dst[0:n, k, :].rearrange("p (e n) -> p e n", e=E),
                                 w[name][:, k * P:k * P + n, :].rearrange("e p n -> p e n")).then_inc(w_in, 16)

            def step(j, u, g, prev, left):
                if left >= R:
                    sp.wait_ge(x_turned, j)
                    load(j + R - 1, (u + R - 1) % R)
                if prev:
                    store(j - 1, (u - 1) % 2)
            for q in stored:
                sp.sem_inc(q, 16)
            walk(sp, step)
            for q in stored:
                sp.wait_ge(q, 16 * (BLOCKS0 // 2 + 1))

        @block.tensor
        def _(pe):
            def turn_x(j, u, g):
                pe.wait_ge(x_in[u], 16 * (g + 1))
                pe.wait_ge(xT_ok, j)
                for k in range(KD):
                    m = pe.transpose(px[:, k, :], xg[:, u, k * P:(k + 1) * P], ident[:, :])
                m.then_inc(x_turned, 1)

            def up(j, slot, wt, pp):
                e = pe.value_load(r["expert"][0:1, bass.ds(j, 1)], min_val=0, max_val=E - 1)
                for k in range(KD):
                    m = pe.matmul(pp[slot][:, 0:F0], xgT[:, slot, k, :], wt[:, k, bass.ds(e * F0, F0)],
                                  start=(k == 0), stop=(k == KD - 1))
                return m

            def turn_h(j, slot):
                pe.wait_ge(h_ok, j + 3)
                for f in range(FT):
                    n = width(f)
                    m = pe.transpose(ph[0:n, f, :], h[:, slot, f * P:f * P + n], ident[:, :])
                m.then_inc(h_turned, 1)

            def down(j, slot):
                e = pe.value_load(r["expert"][0:1, bass.ds(j, 1)], min_val=0, max_val=E - 1)
                pe.wait_ge(hT_ok, j + 1)
                pe.wait_ge(y_ok, j)
                for f in range(FT):
                    n = width(f)
                    m = pe.matmul(py[:, :], hT[0:n, slot, f, :], wd[0:n, f, bass.ds(e * D, D)],
                                  start=(f == 0), stop=(f == FT - 1))
                m.then_inc(y_done, 1)

            def step(j, u, g, prev, left):
                if left >= 2:
                    turn_x(j + 1, (u + 1) % R, g + (u + 1) // R)
                if left >= 1:
                    pe.wait_ge(xT_ok, j + 1)
                    pe.wait_ge(h_ok, j + 1)
                    up(j, u % 2, wg, pg)
                if prev:
                    turn_h(j - 1, (u - 1) % 2)
                if left >= 1:
                    up(j, u % 2, wu, pu).then_inc(up_ok, 1)
                if prev:
                    down(j - 1, (u - 1) % 2)

            turn_x(0, 0, 0)
            pe.wait_ge(w_in, 16 * (2 * KD + FT))
            walk(pe, step)

        @block.scalar
        def _(act):
            def xT(j, slot):
                act.wait_ge(x_turned, j + 1)
                act.activation(xgT[:, slot, :, :], px[:, :, :], ACT.Copy).then_inc(xT_ok, 1)

            def silu(j, slot):
                act.wait_ge(up_ok, j + 1)
                act.activation(sg[:, slot, :], pg[slot][:, 0:F0], ACT.Silu).then_inc(silu_ok, 1)

            def y(j, slot, n):
                act.wait_ge(y_done, j + 1)
                act.wait_ge(stored[slot], 16 * (n + 1))
                act.activation(yo[:, slot, :], py[:, :], ACT.Copy).then_inc(y_ok, 1)

            def step(j, u, g, prev, left):
                if left >= 2:
                    xT(j + 1, (u + 1) % 2)
                if left >= 1:
                    silu(j, u % 2)
                if prev:
                    y(j - 1, (u - 1) % 2, g * 2 + (u - 1) // 2)
            xT(0, 0)
            walk(act, step)

        @block.vector
        def _(dve):
            dve.sem_inc(h_ok, 2)

            def hidden(j, slot):
                dve.wait_ge(silu_ok, j + 1)
                dve.tensor_tensor(h[:, slot, :], sg[:, slot, :], pu[slot][:, 0:F0], ALU.mult).then_inc(h_ok, 1)

            def hiddenT(j, slot):
                dve.wait_ge(h_turned, j + 1)
                full = F0 // P
                dve.tensor_copy(hT[:, slot, 0:full, :], ph[:, 0:full, :])
                dve.tensor_copy(hT[0:width(full), slot, full, :], ph[0:width(full), full, :]).then_inc(hT_ok, 1)

            def step(j, u, g, prev, left):
                if prev:
                    hiddenT(j - 1, (u - 1) % 2)
                if left >= 1:
                    hidden(j, u % 2)
            walk(dve, step)


def combine_phase(nc, tag, r, outs, y, y_stats, x=None, x_load=None):
    R, fetched = FETCHES, r["fetched"]
    with ExitStack() as ctx:
        got = ctx.enter_context(nc.sbuf_tensor(f"{tag}_got", [P, R, 2, D], F32))
        added = ctx.enter_context(nc.semaphore(f"{tag}_added"))
        seen = ctx.enter_context(nc.semaphore(f"{tag}_seen"))
        x_in = ctx.enter_context(nc.semaphore(f"{tag}_x_in"))
        block = ctx.enter_context(nc.Block())

        @block.sync
        def _(sp):
            if x_load is not None:
                sp.dma_start(x[:, :, :], tiles_of(x_load)).then_inc(x_in, 16)
                sp.wait_ge(x_in, 16)

        @block.gpsimd
        def _(pool):
            for t in range(T):
                if t >= R:
                    pool.wait_ge(added, 2 * (t - R + 1))
                for i in range(2):
                    pool.indirect_dma_start(got[:, t % R, i, :], None, outs[:, :],
                                            bass.IndirectOffsetOnAxis(ap=r["take"][i][:, t:t + 1], axis=0))\
                        .then_inc(fetched[t % R][i], 16)

        @block.vector
        def _(dve):
            with dve.Fori(0, T // R) as g:
                for u in range(R):
                    t = g * R + u
                    for i in range(2):
                        dve.wait_ge(fetched[u][i], 16 * (g + 1))
                        dve.scalar_tensor_tensor(out=y[:, t, 0:D], in0=got[:, u, i, :],
                                                 scalar=r["weight"][i][:, bass.ds(t, 1)], in1=y[:, t, 0:D],
                                                 op0=ALU.mult, op1=ALU.add).then_inc(added, 1)
                        dve.wait_ge(added, 2 * t + i + 1)
                        dve.sem_inc(seen, 1)
                    dve.bn_stats(y_stats[:, t, :], y[:, t, 0:D])


SPAN = 512
MAX_UNITS = [(q, a, min(a + SPAN, (q + 1) * P)) for q in range(TB) for a in range(0, (q + 1) * P, SPAN)]
SCORE_UNITS = [(k, max(k * P, h * SPAN), (h + 1) * SPAN) for k in range(TB) for h in range(L // SPAN)
               if k * P < (h + 1) * SPAN]
BANKS = 3
PT_AT = [sum(L - P * j for j in range(k)) for k in range(TB + 1)]
MASKED = -1e30


def attention_order(wide, cur, prev, prev2, nxt, bank):
    n_max = len(MAX_UNITS)
    beside = {(c, k): [] for c in range(2) for k in range(TB)}
    if cur:
        beside[0, 0].append(("turn", 1, 0))
    if prev and wide:
        beside[0, 3].append(("invert", 0, 0))
        beside[1, 1].append(("scale", 0, 0))
        beside[1, 3].append(("invert", 1, 0))
        beside[1, 6].append(("scale", 1, 0))
    if prev2 and wide:
        for u in range(4):
            beside[0, 4 + u].append(("out", 0, u))
    if nxt:
        for u in range(4):
            beside[0, u if wide else u // 2].append(("prep", 0, u))
        if wide:
            places = [(0, k) for k in (4, 5, 6, 7)]
            places += [(1, k) for k, n in enumerate((3, 3, 3, 3, 2, 2, 2, 2)) for _ in range(n)]
            for h in range(2):
                beside[1, h].append(("v", 0, h))
        else:
            places = [(0, k) for k in range(2, TB) for _ in range(2)]
            places += [(1, k) for k, n in enumerate((2, 1, 2, 2, 2, 1, 1, 1)) for _ in range(n)]
        for m, at in enumerate(places):
            beside[at].append(("max", m // n_max, m % n_max))
        beside[1, 3 if wide else 1].append(("turn", 0, 0))
    order = []
    for c in range(2):
        for k in range(TB):
            main = []
            if cur:
                main.append(("score", c, k))
            if c == 0 and prev or c == 1 and cur:
                main.append(("weigh", 1 - c, k))
            extra = beside[c, k]
            mixed = []
            for m in main:
                mixed += extra[:1] + [m]
                extra = extra[1:]
            for name, a, n in mixed + extra:
                if name in ("score", "weigh", "invert", "scale"):
                    order.append((name, a, n, None))
                else:
                    order.append((name, a, n, bank))
                    bank = (bank + 1) % BANKS
    return order, bank


def attention_phase(nc, tag, wide, ident, q_src=None, oT_dram=None, w=None, xT_dram=None, y=None):
    dh = DK if wide else HD
    pairs = (HA if wide else H1) // 2
    n_pairs = B * pairs
    scale = dh ** -0.5
    n_prep = 4
    n_v = 2 if wide else 0
    n_po = P if wide else 4 * dh
    heads = 2 if wide else 1
    n_out = 4 if wide else 0
    n_max = len(MAX_UNITS)
    n_units = len(SCORE_UNITS)
    NARROW = 64
    with ExitStack() as ctx:
        def sb(name, shape, dt=F32):
            return ctx.enter_context(nc.sbuf_tensor(f"{tag}_{name}", shape, dt))

        def sem(name):
            return ctx.enter_context(nc.semaphore(f"{tag}_{name}"))

        if wide:
            xb = sb("xb", [P, 2, KD, L])
            wqk = sb("wqk", [P, 2, 3, KD, P])
            wo = sb("wo", [P, pairs, D])
            q1, q2, k1, k2 = ([[sb(f"{n}_{s}{c}", [P, L], F32R) for c in range(2)] for s in range(2)]
                              for n in ("q1", "q2", "k1", "k2"))
            oT = sb("oT", [P, L])
        else:
            qT, kT = ([sb(f"{n}_{s}", [P, L], F32R) for s in range(2)] for n in ("qT", "kT"))
            qc, kc = (sb(n, [P, TB, 2, NARROW]) for n in ("qc", "kc"))
            hi = sb("hi", [P, 2, TB, 2 * dh], F32R)
            stored = [sem(f"stored{s}") for s in range(2)]
        v = [sb(f"v{s}", [P, TB, 2, n_po]) for s in range(2)]
        half = n_po // 2
        v_at = (slice(0, dh), slice(dh, 2 * dh))
        one_at = (slice(dh, 2 * dh), slice(0, dh)) if wide else (slice(2 * dh, 3 * dh), slice(3 * dh, 4 * dh))
        raw = [sb(f"raw{c}", [P, L]) for c in range(heads)]
        if wide:
            sums = [sb(f"sums{c}", [P, TB]) for c in range(2)]
            inverse = [sb(f"inverse{c}", [P, TB]) for c in range(2)]
            factor = sb("factor", [P, L])
            sums_dram, inverse_dram = ([nc.dram_tensor(f"{tag}_{n}_dram{c}", (L,), F32).ap() for c in range(2)]
                                       for n in ("sums", "inverse"))
            sums_out, sums_in, inverse_out, inverse_in = ([sem(f"{n}{c}") for c in range(2)] for n in (
                "sums_out", "sums_in", "inverse_out", "inverse_in"))
        pt = [sb(f"pt{c}", [P, PT_AT[TB]]) for c in range(2)]
        parts = [sb(f"parts{c}", [P, TB, 2]) for c in range(2)]
        neg = sb("neg", [P, TB])
        mm = sb("mm", [P, 2, 2, TB], F32R)
        mt = sb("mt", [2 * TB, 2, P], F32R)
        ident16 = sb("ident16", [P, P], BF16)
        late = sb("late", [P, P], BF16)
        lateT = sb("lateT", [P, P], BF16)
        g = [ctx.enter_context(nc.psum_tensor(f"{tag}_g{i}", [P, SPAN], F32)) for i in range(BANKS)]
        stp = [ctx.enter_context(nc.psum_tensor(f"{tag}_st{i}", [P, SPAN], F32)) for i in range(BANKS)]
        po = [ctx.enter_context(nc.psum_tensor(f"{tag}_po{i}", [P, SPAN], F32)) for i in range(2)]
        (consts, prep, hi_ok, prep_ok, dup_ok, v_mm, v_ok, mx, max_ok, m_ok, mt_mm, mt_ok, st, pt_ok, pv, raw_ok,
         inverse_ok, scaled, out_mm, out_ok, chain, low_ok) = (sem(n) for n in (
             "consts", "prep", "hi_ok", "prep_ok", "dup_ok", "v_mm", "v_ok", "mx", "max_ok", "m_ok", "mt_mm", "mt_ok",
             "st", "pt_ok", "pv", "raw_ok", "inverse_ok", "scaled", "out_mm", "out_ok", "chain", "low_ok"))
        passed, chain_pool, passed_act = sem("passed"), sem("chain_pool"), sem("passed_act")
        wo_in = sem("wo_in")
        loaded = [sem(f"loaded{s}") for s in range(2)]
        rows_out = [sem(f"rows_out{c}") for c in range(2)]
        rows_in = [sem(f"rows_in{c}") for c in range(2)]
        m_dram = [nc.dram_tensor(f"{tag}_m{c}", (2, L), F32).ap() for c in range(2)]
        block = ctx.enter_context(nc.Block())

        def walk(engine, step):
            bank = 0

            def one(i, s, cur, prev, prev2, nxt, nxt2):
                nonlocal bank
                order, bank = attention_order(wide, cur, prev, prev2, nxt, bank)
                step(i, s, order, nxt, nxt2)

            one(-1, 1, False, False, False, True, True)
            one(0, 0, True, False, False, True, True)
            one(1, 1, True, True, False, True, True)
            with engine.Fori(0, (n_pairs - 4) // 2) as j:
                one(j * 2 + 2, 0, True, True, True, True, True)
                one(j * 2 + 3, 1, True, True, True, True, True)
            one(n_pairs - 2, 0, True, True, True, True, False)
            one(n_pairs - 1, 1, True, True, True, False, False)
            one(n_pairs, 0, False, True, True, False, False)
            if wide:
                one(n_pairs + 1, 1, False, False, True, False, False)

        def head_rows(c, n):
            return slice(NARROW * c, NARROW * c + n)

        def max_operands(s, c):
            if wide:
                return q1[s][c], k1[s][c], slice(c * dh, (c + 1) * dh)
            return qT[s], kT[s], head_rows(c, dh)

        def score_passes(s, c):
            if wide:
                return [(k1[s][c], q1[s][c], slice(0, P)), (k2[s][c], q2[s][c], slice(0, dh + 2))]
            return [(kT[s], qT[s], head_rows(c, 3 * dh + 2))]

        @block.sync
        def _(sp):
            def load(i, s):
                b, p = i // pairs, i % pairs
                sp.dma_start(xb[:, s, :, :], xT_dram[:, :, bass.ds(b * L, L)]).then_inc(loaded[s], 16)
                for n, name in enumerate(("L1_attn_Wq", "L1_attn_Wk", "L1_attn_Wv")):
                    sp.dma_start(wqk[:, s, n, :, :],
                                 w[name].rearrange("(k p) n -> p k n", p=P)[:, :, bass.ds(p * P, P)])\
                      .then_inc(loaded[s], 16)

            def store(i, s):
                b, p = (i - 1) // pairs, (i - 1) % pairs
                sp.wait_ge(raw_ok, 2 * i)
                first = (1 - s) * n_po
                sp.dma_start(oT_dram[0][bass.ds(p * 2 * dh, 2 * dh), bass.ds(b * L, L)],
                             raw[0][first:first + 2 * dh, :]).then_inc(stored[1 - s], 16)
                for c in range(2):
                    at = first + one_at[c].start
                    sp.dma_start(oT_dram[1][bass.ds(p * 2 + c, 1), bass.ds(b * L, L)], raw[0][at:at + 1, :])\
                      .then_inc(stored[1 - s], 16)

            def spread_sums(i, c):
                sp.wait_ge(raw_ok, (2 * i + c + 1) * 2)
                at = one_at[c].start
                sp.dma_start(sums_dram[c].rearrange("(o n) -> o n", o=1), raw[c][at:at + 1, :]).then_inc(sums_out[c], 16)
                sp.wait_ge(sums_out[c], 16 * (i + 1))
                sp.dma_start(sums[c][:, :], sums_dram[c].rearrange("(p t) -> p t", p=P)).then_inc(sums_in[c], 16)

            def spread_inverse(i, c):
                sp.wait_ge(inverse_ok, 2 * i + c + 1)
                sp.dma_start(inverse_dram[c].rearrange("(p t) -> p t", p=P), inverse[c][:, :])\
                  .then_inc(inverse_out[c], 16)
                sp.wait_ge(inverse_out[c], 16 * (i + 1))
                sp.dma_start(factor[v_at[c], :], inverse_dram[c].rearrange("(o n) -> o n", o=1).broadcast_to([dh, L]))\
                  .then_inc(inverse_in[c], 16)

            def spread_max(i, s, c):
                sp.wait_ge(mt_ok, 2 * i + c + 1)
                dst = q2[s][c][dh:dh + 2, :] if wide else qT[s][NARROW * c + 3 * dh:NARROW * c + 3 * dh + 2, :]
                sp.dma_start(m_dram[c].rearrange("h (t q) -> (h t) q", q=P), mt[:, c, :].bitcast(F32))\
                  .then_inc(rows_out[c], 16)
                sp.wait_ge(rows_out[c], 16 * (i + 1))
                sp.dma_start(dst.bitcast(F32), m_dram[c]).then_inc(rows_in[c], 16)

            def step(i, s, cur, prev, nxt, more):
                if prev and wide:
                    spread_sums(i - 1, 0)
                if cur:
                    spread_max(i, s, 1)
                if prev and wide:
                    spread_inverse(i - 1, 0)
                    spread_sums(i - 1, 1)
                if prev and not wide:
                    store(i, s)
                if wide and more:
                    sp.wait_ge(v_mm, n_v * (i + 1))
                    load(i + 2, s)
                if prev and wide:
                    spread_inverse(i - 1, 1)
                if nxt:
                    spread_max(i + 1, 1 - s, 0)

            if wide:
                load(0, 0)
                load(1, 1)
                sp.dma_start(wo[:, :, :], w["L1_attn_Wo"].rearrange("(c p) n -> p c n", p=P)).then_inc(wo_in, 16)
            if not wide:
                for q in stored:
                    sp.sem_inc(q, 48)
            step(-1, 1, False, False, True, False)
            step(0, 0, True, False, True, True)
            with sp.Fori(0, (n_pairs - 4) // 2) as j:
                step(j * 2 + 1, 1, True, True, True, True)
                step(j * 2 + 2, 0, True, True, True, True)
            step(n_pairs - 3, 1, True, True, True, True)
            step(n_pairs - 2, 0, True, True, True, False)
            step(n_pairs - 1, 1, True, True, False, False)
            step(n_pairs, 0, False, True, False, False)
            if not wide:
                for q in stored:
                    sp.wait_ge(q, 48 + 48 * (n_pairs // 2))

        @block.tensor
        def _(pe):
            fills = []

            def fill(i, i_of, reader, per_pair, index):
                n = len(fills)
                if n >= BANKS:
                    sem_, per, off, at = fills[-BANKS]
                    pe.wait_ge(sem_, (i + off) * per + at + 1)
                fills.append((reader, per_pair, i_of, index))
                return g[n % BANKS]

            def shift():
                fills[:] = [(a, b_, off - 1, d) for a, b_, off, d in fills]

            def project(i, s, u):
                n, h = u // 2, u % 2
                if u == 0:
                    if wide:
                        pe.wait_ge(loaded[s], 64 * ((i + 1) // 2 + 1))
                    else:
                        pe.wait_ge(low_ok, 4 * (i + 2))
                        pe.wait_ge(dup_ok, 4 * (i + 2))
                bank = fill(i, 1, prep_ok, n_prep, u)
                if wide:
                    for k in range(KD):
                        m = pe.matmul(bank[:, :], wqk[:, s, n, k, :], xb[:, s, k, h * SPAN:(h + 1) * SPAN],
                                      start=(k == 0), stop=(k == KD - 1))
                else:
                    for t in range(4):
                        m = pe.transpose(bank[:, t * P:(t + 1) * P],
                                         (qc, kc)[n][:, h * 4 + t, :, :].rearrange("p c n -> p (c n)"), ident[:, :])
                m.then_inc(prep, 1)

            def project_v(i, s, h):
                bank = fill(i, 1, v_ok, n_v, h)
                for t in range(4):
                    for k in range(KD):
                        m = pe.matmul(bank[:, t * P:(t + 1) * P],
                                      xb[:, s, k, (h * 4 + t) * P:(h * 4 + t + 1) * P], wqk[:, s, 2, k, :],
                                      start=(k == 0), stop=(k == KD - 1))
                m.then_inc(v_mm, 1)

            def max_unit(i, s, c, u):
                if u == 0 and c == 0:
                    pe.wait_ge(hi_ok if wide else prep_ok, n_prep * (i + 2))
                tile, a, z = MAX_UNITS[u]
                bank = fill(i, 1, max_ok, 2 * n_max, c * n_max + u)
                q_, k_, rows = max_operands(s, c)
                diagonal = z == (tile + 1) * P
                m = pe.matmul(bank[:, 0:z - a], q_[rows, tile * P:(tile + 1) * P], k_[rows, a:z],
                              start=True, stop=not diagonal)
                if diagonal:
                    m = pe.matmul(bank[:, z - a - P:z - a], ident16[:, :], late[:, :], start=False, stop=True)
                m.then_inc(mx, 1)

            def turn_max(i, c):
                pe.wait_ge(m_ok, 2 * (i + 1 - c) + c + 1)
                bank = fill(i, 1 - c, mt_ok, 2, c)
                pe.transpose(bank[0:2 * TB, 0:P], mm[:, c, :, :].rearrange("p h t -> p (h t)").bitcast(F32),
                             ident[:, :]).then_inc(mt_mm, 1)

            def score(i, s, c, k):
                if k == 0:
                    pe.wait_ge(rows_in[c], 16 * (i + 1))
                    if wide and c == 0:
                        pe.wait_ge(dup_ok, 4 * (i + 1))
                        pe.wait_ge(prep_ok, n_prep * (i + 1))
                for u, (tile, a, z) in enumerate(SCORE_UNITS):
                    if tile != k:
                        continue
                    pe.wait_ge(pt_ok, (2 * i + c) * n_units + u + 1)
                    bank = stp[u % BANKS]
                    passes = score_passes(s, c)
                    for n, (k_, q_, rows) in enumerate(passes):
                        m = pe.matmul(bank[:, 0:z - a], k_[rows, k * P:(k + 1) * P], q_[rows, a:z],
                                      start=(n == 0), stop=(n == len(passes) - 1 and a != k * P))
                    if a == k * P:
                        m = pe.matmul(bank[:, 0:P], ident16[:, :], lateT[:, :], start=False, stop=True)
                    m.then_inc(st, 1)

            def weigh(i, s, c, k):
                if k == 0 and c < heads:
                    pe.wait_ge(raw_ok, (heads * i + c) * 2)
                if k == 0 and c == 0:
                    pe.wait_ge(v_ok, 2 * (i + 1))
                for h in range(k // 4, 2):
                    a = max(k * P - h * SPAN, 0)
                    unit = SCORE_UNITS.index((k, h * SPAN + a, (h + 1) * SPAN))
                    pe.wait_ge(pt_ok, (2 * i + c) * n_units + unit + 1 + BANKS)
                    at = PT_AT[k] + h * SPAN + a - k * P
                    m = pe.matmul(po[h][0:n_po, a:SPAN], v[s][:, k, c, :], pt[c][:, at:at + SPAN - a],
                                  start=(k == 0 and c < heads), stop=(k == h * 4 + 3 and c >= heads - 1),
                                  skip_group_check=True)
                    if k == h * 4 + 3 and (wide or c == 1):
                        m.then_inc(pv, 1)

            def project_o(i, u):
                if u == 0:
                    pe.wait_ge(scaled, 2 * i - 1)
                bank = fill(i, -2, out_ok, n_out, u)
                for h in range(2):
                    t = u * 2 + h
                    m = pe.matmul(bank[:, h * D:(h + 1) * D], oT[:, t * P:(t + 1) * P], wo[:, (i - 2) % pairs, :],
                                  start=True, stop=True)
                m.then_inc(out_mm, 1)

            def step(i, s, order, nxt, nxt2):
                for name, c, n, _ in order:
                    if name == "score":
                        score(i, s, c, n)
                    elif name == "weigh":
                        weigh(i - c, s if c == 0 else 1 - s, c, n)
                    elif name == "prep":
                        project(i, 1 - s, n)
                    elif name == "v":
                        project_v(i, 1 - s, n)
                    elif name == "max":
                        max_unit(i, 1 - s, c, n)
                    elif name == "turn":
                        turn_max(i, c)
                    elif name == "out":
                        project_o(i, n)
                shift()

            pe.wait_ge(consts, 2)
            if wide:
                pe.wait_ge(wo_in, 16)
            walk(pe, step)

        @block.scalar
        def _(act):
            act.sem_inc(pt_ok, BANKS)

            def high(i, s, u, bank):
                n, h = u // 2, u % 2
                at = slice(h * SPAN, (h + 1) * SPAN)
                act.wait_ge(prep, n_prep * (i + 1) + u + 1)
                if wide:
                    for c in range(2):
                        rows = slice(c * dh, (c + 1) * dh)
                        m = act.activation((q1, k1)[n][s][c][rows, at], bank[rows, :], ACT.Copy,
                                           scale=scale if n == 0 else 1.0)
                    m.then_inc(hi_ok, 1)
                else:
                    act.activation((qT, kT)[n][s][:, at], bank[:, :], ACT.Copy).then_inc(prep_ok, 1)

            def values(i, s, h, bank):
                act.wait_ge(v_mm, n_v * (i + 1) + h + 1)
                for c in range(2):
                    m = act.activation(v[s][:, h * 4:h * 4 + 4, c, v_at[c]],
                                       bank[:, :].rearrange("p (t c n) -> p t c n", t=4, c=2)[:, :, c, :], ACT.Copy)
                m.then_inc(v_ok, 1)

            def exp(i, c, k):
                for u, (tile, a, z) in enumerate(SCORE_UNITS):
                    if tile == k:
                        act.wait_ge(st, (2 * i + c) * n_units + u + 1)
                        at = PT_AT[k] + a - k * P
                        act.activation(pt[c][:, at:at + z - a], stp[u % BANKS][:, 0:z - a], ACT.Exp).then_inc(pt_ok, 1)

            def drain(i, s, c):
                if wide:
                    act.wait_ge(scaled, 2 * i + c)
                else:
                    act.wait_ge(stored[s], 48 * ((i + 2) // 2))
                act.sem_inc(passed_act, 1)
                for h in range(2):
                    act.wait_ge(pv, (heads * i + (c if wide else 0)) * 2 + h + 1)
                    dst = raw[c] if wide else raw[0][s * half * 2:s * half * 2 + n_po, :]
                    act.activation(dst[:, h * SPAN:(h + 1) * SPAN], po[h][0:n_po, :], ACT.Copy).then_inc(raw_ok, 1)

            def step(i, s, order, nxt, nxt2):
                for name, c, n, bank in order:
                    if name == "prep":
                        high(i, 1 - s, n, g[bank])
                    elif name == "score":
                        exp(i, c, n)
                    elif name == "v":
                        values(i, 1 - s, n, g[bank])
                    elif name == "weigh" and n == TB - 1 and (wide or c == 1):
                        drain(i - c, s if c == 0 else 1 - s, c)
            walk(act, step)

        @block.vector
        def _(dve):
            def low(i, s, u, bank):
                n, h = u // 2, u % 2
                at = slice(h * SPAN, (h + 1) * SPAN)
                dve.wait_ge(hi_ok, n_prep * (i + 1) + u + 1)
                for c in range(2):
                    rows = slice(c * dh, (c + 1) * dh)
                    if n == 0:
                        dst = q1[s][c][(1 - c) * dh:(2 - c) * dh, at]
                    else:
                        dst = k2[s][c][0:dh, at]
                    m = dve.scalar_tensor_tensor(out=dst, in0=bank[rows, :], scalar=scale if n == 0 else 1.0,
                                                 in1=(q1, k1)[n][s][c][rows, at].bitcast(F32),
                                                 op0=ALU.mult, op1=ALU.subtract)
                m.then_inc(prep_ok, 1)

            def stack(i):
                b, p = (i + 1) // pairs, (i + 1) % pairs
                dve.wait_ge(prep, n_prep * (i + 1))
                for n in range(2):
                    src = q_src[:, bass.ds(b * TB, TB), bass.ds(n * D + p * 2 * dh, 2 * dh)]
                    dve.tensor_scalar(hi[:, n, :, :], src, scale if n == 0 else 1.0, None, ALU.mult).then_inc(hi_ok, 1)
                dve.wait_ge(hi_ok, 2 * (i + 2))
                for n in range(2):
                    for c in range(2):
                        src = q_src[:, bass.ds(b * TB, TB), bass.ds(n * D + p * 2 * dh + c * dh, dh)]
                        dst = (qc[:, :, c, dh:2 * dh], kc[:, :, c, 2 * dh:3 * dh])[n]
                        dve.scalar_tensor_tensor(out=dst, in0=src, scalar=scale if n == 0 else 1.0,
                                                 in1=hi[:, n, :, c * dh:(c + 1) * dh].bitcast(F32),
                                                 op0=ALU.mult, op1=ALU.subtract).then_inc(low_ok, 1)

            def max_unit(i, c, u, bank):
                tile, a, z = MAX_UNITS[u]
                dve.wait_ge(mx, 2 * n_max * (i + 1) + c * n_max + u + 1)
                dve.tensor_reduce(parts[c][:, tile, a // SPAN:a // SPAN + 1], bank[:, 0:z - a], AX.X, ALU.max)\
                   .then_inc(max_ok, 1)

            def minus_max(i, c):
                dve.wait_ge(max_ok, 2 * n_max * (i + 1) + (c + 1) * n_max)
                dve.tensor_reduce(neg[:, :], parts[c][:, :, :], AX.X, ALU.max, negate=True).then_inc(chain, 1)
                dve.wait_ge(chain, 2 * (2 * (i + 1) + c) + 1)
                dve.tensor_copy(mm[:, c, 0, :], neg[:, :]).then_inc(chain, 1)
                dve.wait_ge(chain, 2 * (2 * (i + 1) + c) + 2)
                dve.tensor_tensor(mm[:, c, 1, :], neg[:, :], mm[:, c, 0, :].bitcast(F32), ALU.subtract)\
                   .then_inc(m_ok, 1)

            def max_rows(i, c, bank):
                dve.wait_ge(mt_mm, 2 * (i + 1 - c) + c + 1)
                dve.tensor_copy(mt[:, c, :], bank[0:2 * TB, 0:P]).then_inc(mt_ok, 1)

            def invert(i, c):
                dve.wait_ge(sums_in[c], 16 * (i + 1))
                dve.reciprocal(inverse[c][:, :], sums[c][:, :]).then_inc(inverse_ok, 1)

            def scale_o(i, c):
                dve.wait_ge(inverse_in[c], 16 * (i + 1))
                rows = v_at[c]
                dve.tensor_tensor(oT[rows, :], raw[c][rows, :], factor[rows, :], ALU.mult).then_inc(scaled, 1)

            def add_out(i, u, bank):
                dve.wait_ge(out_mm, n_out * (i - 2) + u + 1)
                b = (i - 2) // pairs
                rows = y[:, bass.ds(b * TB + u * 2, 2), :]
                dve.tensor_tensor(rows, bank[:, :].rearrange("p (t d) -> p t d", t=2), rows, ALU.add)\
                   .then_inc(out_ok, 1)

            def step(i, s, order, nxt, nxt2):
                for name, c, n, bank in order:
                    if name == "prep" and wide:
                        low(i, 1 - s, n, g[bank])
                    elif name == "max":
                        max_unit(i, c, n, g[bank])
                        if n == n_max - 1:
                            minus_max(i, c)
                        if n == 2 and c == 0 and nxt2 and not wide:
                            stack(i + 1)
                    elif name == "turn":
                        max_rows(i, c, g[bank])
                    elif name == "out":
                        add_out(i, n, g[bank])
                    elif name == "invert":
                        invert(i - 1, c)
                    elif name == "scale":
                        scale_o(i - 1, c)
            dve.sem_inc(scaled, 1)
            dve.wait_ge(consts, 2)
            if not wide:
                stack(-1)
            walk(dve, step)

        @block.gpsimd
        def _(pool):
            link = Chain(pool, chain_pool).step
            for c in range(2):
                link(pool.memset(parts[c][:, :, 1:2], MASKED))
            for s in range(2):
                if wide:
                    for c in range(2):
                        link(pool.memset(k2[s][c][dh:dh + 2, :].bitcast(F32), 1.0))
                if not wide:
                    link(pool.memset(v[s][:, :, :, :], 0.0))
                for c in range(2):
                    link(pool.memset(v[s][:, :, c, one_at[c]], 1.0))
            if not wide:
                link(pool.memset(qc[:, :, :, :], 0.0))
                link(pool.memset(kc[:, :, :, :], 0.0))
                link(pool.memset(kc[:, :, :, 3 * dh:3 * dh + 2], 1.0))
            link(pool.tensor_copy(ident16[:, :], ident[:, :]))
            link(pool.memset(late[:, :], 0.0))
            link(pool.memset(lateT[:, :], 0.0))
            pool.affine_select(out=late[:, :], in_=late[:, :], compare_op=ALU.is_ge, fill=MASKED, base=0,
                               pattern=[[-1, P]], channel_multiplier=1).then_inc(consts, 1)
            pool.affine_select(out=lateT[:, :], in_=lateT[:, :], compare_op=ALU.is_ge, fill=MASKED, base=0,
                               pattern=[[1, P]], channel_multiplier=-1).then_inc(consts, 1)
            pool.wait_ge(consts, 2)

            def copies(i, s):
                for n in range(2):
                    pool.wait_ge(hi_ok, n_prep * (i + 1) + 2 * n + 2)
                    pool.sem_inc(passed, 1)
                    for c in range(2):
                        rows, other = slice(c * dh, (c + 1) * dh), slice((1 - c) * dh, (2 - c) * dh)
                        if n == 0:
                            m = pool.tensor_copy(q2[s][c][0:dh, :], q1[s][c][rows, :].bitcast(F32))
                        else:
                            m = pool.tensor_copy(k1[s][c][other, :], k1[s][c][rows, :].bitcast(F32))
                        m.then_inc(dup_ok, 1)
                        pool.wait_ge(dup_ok, 4 * (i + 1) + 2 * n + c + 1)
                        pool.sem_inc(passed, 1)

            def stack_high(i):
                pool.wait_ge(hi_ok, 2 * (i + 2))
                pool.sem_inc(passed, 1)
                for n, places in ((0, (0, 2)), (1, (0, 1))):
                    for at in places:
                        pool.tensor_copy((qc, kc)[n][:, :, :, at * dh:(at + 1) * dh],
                                         hi[:, n, :, :].bitcast(F32).rearrange("p t (c n) -> p t c n", c=2))\
                            .then_inc(dup_ok, 1)

            def copy_v(i, s):
                b, p = (i + 1) // pairs, (i + 1) % pairs
                pool.wait_ge(pv, 2 * i if not isinstance(i, int) or i >= 0 else 0)
                pool.sem_inc(passed, 1)
                for c in range(2):
                    pool.tensor_copy(v[s][:, :, c, v_at[c]],
                                     q_src[:, bass.ds(b * TB, TB), bass.ds(2 * D + p * 2 * dh + c * dh, dh)])\
                        .then_inc(v_ok, 1)

            def step(i, s, order, nxt, nxt2):
                if wide and nxt:
                    copies(i, 1 - s)
                if not wide and nxt2:
                    stack_high(i + 1)
                if not wide and nxt:
                    copy_v(i, 1 - s)
            if not wide:
                stack_high(-1)
            walk(pool, step)


def qkv_phase(nc, w, tables, hT, qkv):
    G = 3 * D
    with ExitStack() as ctx:
        def sb(name, shape, dt=F32):
            return ctx.enter_context(nc.sbuf_tensor(f"qkv_{name}", shape, dt))

        def sem(name):
            return ctx.enter_context(nc.semaphore(f"qkv_{name}"))

        half = HD // 2
        heads = 2 * H1
        raw = sb("raw", [P, KD, G])
        wt = sb("wt", [P, KD, G])
        cos, sin = (sb(n, [P, TB, half]) for n in ("cos", "sin"))
        stage = sb("stage", [P, 2, KD, P])
        prods = [[sb(f"prod{i}_{u}", [P, heads, half]) for i in range(4)] for u in range(2)]
        pa = [ctx.enter_context(nc.psum_tensor(f"qkv_pa{i}", [P, 2 * D], F32)) for i in range(2)]
        pb = [ctx.enter_context(nc.psum_tensor(f"qkv_pb{i}", [P, D], F32)) for i in range(2)]
        w_in, w_ok, staged, done, rotated, v_ok, prod_ok, seen = (
            sem(n) for n in ("w_in", "w_ok", "staged", "done", "rotated", "v_ok", "prod_ok", "seen"))
        block = ctx.enter_context(nc.Block())

        @block.sync
        def _(sp):
            sp.dma_start(raw[:, :, :], w["L1_ffn_Wqkv"].rearrange("(k p) n -> p k n", p=P)).then_inc(w_in, 16)
            for dst, src in ((cos, tables[0]), (sin, tables[1])):
                sp.dma_start(dst[:, :, :], tiles_of(src)).then_inc(w_in, 16)

        @block.gpsimd
        def _(pool):
            pool.wait_ge(w_in, 48)
            for kind in range(3):
                for k in range(KD):
                    pool.tensor_copy(wt[:, k, kind * D:(kind + 1) * D].rearrange("p (h n) -> p h n", n=HD),
                                     raw[:, k, :].rearrange("p (h c n) -> p h c n", c=3, n=HD)[:, :, kind, :])\
                        .then_inc(w_ok, 1)

        @block.scalar
        def _(act):
            act.sem_inc(v_ok, 2)

            def copy_in(t, u):
                act.wait_ge(done, t + 1)
                act.activation(stage[:, u % 2, :, :], hT[:, :, bass.ds(t * P, P)], ACT.Copy).then_inc(staged, 1)

            def copies(b, more):
                for u in range(TB):
                    t = b * TB + u
                    if more or u < TB - 1:
                        copy_in(t + 1, u + 1)
                    act.wait_ge(done, t + 3)
                    act.activation(qkv[:, t, 2 * D:G], pb[u % 2][:, :], ACT.Copy).then_inc(v_ok, 1)

            copy_in(0, 0)
            with act.Fori(0, T // TB - 1) as b:
                copies(b, True)
            copies(T // TB - 1, False)

        @block.tensor
        def _(pe):
            pe.sem_inc(done, 2)
            pe.wait_ge(w_ok, 6)
            with pe.Fori(0, T // TB) as b:
                for u in range(TB):
                    t = b * TB + u
                    pe.wait_ge(staged, t + 1)
                    pe.wait_ge(v_ok, t + 1)
                    pe.wait_ge(rotated, t + 1)
                    for out, a, z in ((pa, 0, 2 * D), (pb, 2 * D, G)):
                        for k in range(KD):
                            m = pe.matmul(out[u % 2][:, :], stage[:, u % 2, k, :], wt[:, k, a:z],
                                          start=(k == 0), stop=(k == KD - 1))
                    m.then_inc(done, 1)

        @block.vector
        def _(dve):
            dve.sem_inc(rotated, 2)
            with dve.Fori(0, T // TB) as b:
                for u in range(TB):
                    t = b * TB + u
                    dve.wait_ge(done, t + 3)
                    dve.sem_inc(seen, 1)
                    dve.wait_ge(rotated, t + 1)
                    prod = prods[u % 2]
                    x = pa[u % 2][:, :].rearrange("p (h c n) -> p h c n", c=2, n=half)
                    for n, (part, table) in enumerate(((0, cos), (1, sin), (0, sin), (1, cos))):
                        dve.tensor_tensor(prod[n][:, :, :], x[:, :, part, :],
                                          table[:, u, :].unsqueeze(1).broadcast_to([P, heads, half]), ALU.mult)\
                           .then_inc(prod_ok, 1)
                    dve.wait_ge(prod_ok, 4 * (t + 1))
                    y = qkv[:, t, 0:2 * D].rearrange("p (h c n) -> p h c n", c=2, n=half)
                    dve.tensor_tensor(y[:, :, 0, :], prod[0][:, :, :], prod[1][:, :, :], ALU.subtract)
                    dve.tensor_tensor(y[:, :, 1, :], prod[2][:, :, :], prod[3][:, :, :], ALU.add).then_inc(rotated, 1)


def output_phase(nc, w, oT_dram, y):
    R = 4
    PARTS = 8
    with ExitStack() as ctx:
        def sb(name, shape):
            return ctx.enter_context(nc.sbuf_tensor(f"op_{name}", shape, F32))

        def sem(name):
            return ctx.enter_context(nc.semaphore(f"op_{name}"))

        wp = sb("w", [P, KD, D])
        sums = sb("sums", [P, H1 * N // P])
        raw, factor = (sb(n, [P, KD, N]) for n in ("raw", "factor"))
        oT = sb("oT", [P, R, KD, 2 * P])
        py = [ctx.enter_context(nc.psum_tensor(f"op_py{i}", [P, 2, D], F32)) for i in range(2)]
        inverse_dram = nc.dram_tensor("op_inverse", (H1, N), F32).ap()
        w_in, sums_in, inverse_ok, inverse_out, oT_ok, done, added = (
            sem(n) for n in ("w_in", "sums_in", "inverse_ok", "inverse_out", "oT_ok", "done", "added"))
        loaded = [sem(f"loaded{c}") for c in range(PARTS)]
        block = ctx.enter_context(nc.Block())

        def across(ap):
            return ap.rearrange("h (c n) -> (h c) n", n=H1 * N // P)

        @block.sync
        def _(sp):
            heads = P // HD

            def part(c):
                return slice(c * (N // PARTS), (c + 1) * (N // PARTS))

            def load_raw(c):
                sp.dma_start(raw[:, :, part(c)], oT_dram[0].rearrange("(k p) n -> p k n", p=P)[:, :, part(c)])\
                  .then_inc(loaded[c], 16)

            sp.dma_start(sums[:, :], across(oT_dram[1])).then_inc(sums_in, 16)
            sp.dma_start(wp[:, :, :], w["L1_ffn_Wproj"].rearrange("(k p) n -> p k n", p=P)).then_inc(w_in, 16)
            load_raw(0)
            sp.wait_ge(inverse_ok, 1)
            sp.dma_start(across(inverse_dram), sums[:, :]).then_inc(inverse_out, 16)
            sp.wait_ge(inverse_out, 16)
            for c in range(PARTS):
                for k in range(KD):
                    src = inverse_dram[k * heads:(k + 1) * heads, part(c)]
                    sp.dma_start(factor[:, k, part(c)], src.unsqueeze(1).broadcast_to([heads, HD, N // PARTS]))\
                      .then_inc(loaded[c], 16)
                if c + 1 < PARTS:
                    load_raw(c + 1)

        @block.tensor
        def _(pe):
            pe.wait_ge(w_in, 16)
            with pe.Fori(0, T // 2 // R) as i:
                for u in range(R):
                    s = i * R + u
                    pe.wait_ge(oT_ok, s + 1)
                    pe.wait_ge(added, s + 1)
                    for v in range(2):
                        for k in range(KD):
                            m = pe.matmul(py[u % 2][:, v, :], oT[:, u, k, v * P:(v + 1) * P], wp[:, k, :],
                                          start=(k == 0), stop=(k == KD - 1))
                    m.then_inc(done, 1)

        @block.vector
        def _(dve):
            dve.sem_inc(added, 2)
            dve.wait_ge(sums_in, 16)
            dve.reciprocal(sums[:, :], sums[:, :]).then_inc(inverse_ok, 1)

            def divide(s, u):
                at = bass.ds(s * 2 * P, 2 * P)
                dve.tensor_tensor(oT[:, u, :, :], raw[:, :, at], factor[:, :, at], ALU.mult).then_inc(oT_ok, 1)

            def add(s, u):
                dve.wait_ge(done, s + 1)
                out = y[:, bass.ds(s * 2, 2), :]
                dve.tensor_tensor(out, py[u % 2][:, :, :], out, ALU.add).then_inc(added, 1)

            steps_per_part = T // 2 // PARTS
            for s in range(T // 2):
                if s % steps_per_part == 0:
                    dve.wait_ge(loaded[s // steps_per_part], 16 * (1 + KD))
                divide(s, s % R)
                if s >= 2:
                    add(s - 2, s % R)
            for s in range(T // 2 - 2, T // 2):
                add(s, s % R)


def layer1_experts(nc, w, gain, rows, outs, ident):
    FT = F1 // P
    STEPS = ROWS1 // SPAN
    PER = CAP // SPAN
    with ExitStack() as ctx:
        def sb(name, shape, dt=F32):
            return ctx.enter_context(nc.sbuf_tensor(f"e1_{name}", shape, dt))

        def ps(name, shape):
            return ctx.enter_context(nc.psum_tensor(f"e1_{name}", shape, F32))

        def sem(name):
            return ctx.enter_context(nc.semaphore(f"e1_{name}"))

        raw = [sb("raw1", [P, KD, F1]), sb("raw2", [P, FT, D])]
        cut = [[[sb(f"w{n + 1}_{s}{c}", shape, F32R) for c in range(2)] for s in range(2)]
               for n, shape in enumerate(([P, KD, F1], [P, FT, D]))]
        b1_rows = sb("b1_rows", [E * FT, P])
        b1 = sb("b1", [P, E, FT])
        b2 = sb("b2", [P, E * D])
        xg = sb("xg", [P, 2, SPAN // P, D])
        xf = sb("xf", [P, KD, SPAN])
        xT = [[sb(f"xT{s}{c}", [P, KD, SPAN], F32R) for c in range(2)] for s in range(2)]
        hf = sb("hf", [P, 2, SPAN])
        hid = [sb(f"hid{c}", [P, FT, SPAN], F32R) for c in range(2)]
        yo = sb("yo", [P, 2, 2, D])
        px = [ps(f"px{k}", [P, SPAN]) for k in range(KD)]
        ph = [ps(f"ph{i}", [P, SPAN]) for i in range(2)]
        py = [ps(f"py{i}", [P, 2, D]) for i in range(2)]
        pb = ps("pb", [P, E * FT])
        (b_in, b2_in, b_turned, b_ok, x_turned, x_high, xT_ok, up_ok, h_high, hid_ok, y_done, y_ok, seen) = (
            sem(n) for n in ("b_in", "b2_in", "b_turned", "b_ok", "x_turned", "x_high", "xT_ok", "up_ok", "h_high",
                             "hid_ok", "y_done", "y_ok", "seen"))
        w_in, w_high, w_ok, x_in, stored = ([sem(f"{n}{i}") for i in range(2)] for n in (
            "w_in", "w_high", "w_ok", "x_in", "stored"))
        block = ctx.enter_context(nc.Block())

        PARTS = ((0, 0), (0, 1), (1, 0))
        x_rows = tiles_of(rows)
        y_rows = tiles_of(outs)

        def walk(engine, step):
            with engine.Fori(0, STEPS // 4 - 1) as j:
                for v in range(4):
                    step(j * 4 + v, v, j, True)
            for v in range(4):
                step(STEPS - 4 + v, v, STEPS // 4 - 1, False)

        @block.sync
        def _(sp):
            def load_w(e, n):
                src = w[("L1_ffn_W1", "L1_ffn_W2")[n]][bass.ds(e, 1), :, :]
                sp.dma_start(raw[n][:, :, :], src.rearrange("o (k p) n -> p (o k) n", p=P)).then_inc(w_in[n], 16)

            def load_x(q, s):
                sp.dma_start(xg[:, s, :, :], x_rows[:, bass.ds(q * (SPAN // P), SPAN // P), :]).then_inc(x_in[s], 16)

            sp.dma_start(b1_rows[:, :], w["L1_ffn_b1"].rearrange("e (f p) -> (e f) p", p=P)).then_inc(b_in, 16)
            load_x(0, 0)
            load_w(0, 0)
            load_w(0, 1)
            sp.dma_start(b2[:, :], w["L1_ffn_b2"].rearrange("(o e) d -> o (e d)", o=1).broadcast_to([P, E * D]))\
              .then_inc(b2_in, 16)
            load_x(1, 1)
            for n in range(2):
                sp.wait_ge(w_ok[n], 1)
                load_w(1, n)
            for s in stored:
                sp.sem_inc(s, 16)

            def step(q, v, j, later):
                e = j * 2 + v // PER
                if later or v < 2:
                    sp.wait_ge(x_turned, q + 1)
                    load_x(q + 2, v % 2)
                for h in range(2):
                    sp.wait_ge(y_ok, 2 * q + h + 3)
                    sp.dma_start(y_rows[:, bass.ds(q * 4 + h * 2, 2), :], yo[:, h, :, :]).then_inc(stored[h], 16)
                if later:
                    sp.wait_ge(w_ok[v % 2], e + 2)
                    load_w(e + 2, v % 2)
            walk(sp, step)
            for s in stored:
                sp.wait_ge(s, 16 * (STEPS + 1))

        @block.tensor
        def _(pe):
            def turn_x(q, s, n):
                pe.wait_ge(x_in[s], 16 * (n + 1))
                pe.wait_ge(xT_ok, q)
                for k in range(KD):
                    for t in range(SPAN // P):
                        m = pe.transpose(px[k][:, t * P:(t + 1) * P], xg[:, s, t, k * P:(k + 1) * P], ident[:, :])
                m.then_inc(x_turned, 1)

            def up(q, s, ws):
                pe.wait_ge(xT_ok, q + 1)
                for f in range(FT):
                    pe.wait_ge(h_high, q * FT + f + 1)
                    for i, (a, b) in enumerate(PARTS):
                        for k in range(KD):
                            m = pe.matmul(ph[f % 2][:, :], cut[0][ws][a][:, k, f * P:(f + 1) * P], xT[s][b][:, k, :],
                                          start=(i == 0 and k == 0), stop=(i == len(PARTS) - 1 and k == KD - 1))
                    m.then_inc(up_ok, 1)

            def down(q, ws):
                for h in range(2):
                    pe.wait_ge(y_ok, 2 * q + h + 1)
                    for v in range(2):
                        t = h * 2 + v
                        for f in range(FT):
                            if t == 0:
                                pe.wait_ge(hid_ok, q * FT + f + 3)
                            for i, (a, b) in enumerate(PARTS):
                                m = pe.matmul(py[h][:, v, :], hid[b][:, f, t * P:(t + 1) * P], cut[1][ws][a][:, f, :],
                                              start=(i == 0 and f == 0), stop=(i == len(PARTS) - 1 and f == FT - 1))
                    m.then_inc(y_done, 1)

            def step(q, v, j, later):
                ws = v // PER
                if v % PER == 0:
                    for ok in w_ok:
                        pe.wait_ge(ok, j * 2 + ws + 1)
                up(q, v % 2, ws)
                if later or v < 3:
                    turn_x(q + 1, (v + 1) % 2, j * 2 + (v + 1) // 2)
                down(q, ws)

            pe.wait_ge(b_in, 16)
            pe.transpose(pb[:, :], b1_rows[:, :], ident[0:E * FT, 0:E * FT]).then_inc(b_turned, 1)
            turn_x(0, 0, 0)
            walk(pe, step)

        @block.scalar
        def _(act):
            act.sem_inc(h_high, 2)

            def scale_x(q, s):
                act.wait_ge(x_turned, q + 1)
                act.wait_ge(xT_ok, q)
                for dst in (xT[s][0], xf):
                    for k in range(KD):
                        m = act.activation(dst[:, k, :], px[k][:, :], ACT.Identity, scale=gain[0][:, k:k + 1],
                                           bias=gain[1][:, k:k + 1])
                m.then_inc(x_high, 1)

            def weight_high(e, n, s):
                act.wait_ge(w_in[n], 16 * (e + 1))
                act.activation(cut[n][s][0][:, :, :], raw[n][:, :, :], ACT.Copy).then_inc(w_high[n], 1)

            def step(q, v, j, later):
                e = j * 2 + v // PER
                bias = b1[:, bass.ds(e, 1), :]
                for f in range(FT):
                    act.wait_ge(up_ok, q * FT + f + 1)
                    act.sem_inc(seen, 1)
                    act.wait_ge(hid_ok, q * FT + f + 1)
                    act.sem_inc(seen, 1)
                    for dst in (hid[0][:, f, :], hf[:, f % 2, :]):
                        m = act.activation(dst, ph[f % 2][:, :], ACT.Gelu,
                                           bias=bias[:, :, f:f + 1].rearrange("p o f -> p (o f)"))
                    m.then_inc(h_high, 1)
                if later or v < 3:
                    scale_x(q + 1, (v + 1) % 2)
                if later or v < 2:
                    weight_high(e + 1, v % 2, 1 - v // PER)

            for n in range(2):
                weight_high(0, n, 0)
            act.wait_ge(b_ok, 1)
            scale_x(0, 0)
            walk(act, step)

        @block.vector
        def _(dve):
            def low(dst, src, high):
                return dve.tensor_tensor(dst, src, high.bitcast(F32), ALU.subtract)

            def weight_low(e, n, s):
                dve.wait_ge(w_high[n], e + 1)
                low(cut[n][s][1][:, :, :], raw[n][:, :, :], cut[n][s][0][:, :, :]).then_inc(w_ok[n], 1)

            def x_low(q, s):
                dve.wait_ge(x_high, q + 1)
                low(xT[s][1][:, :, :], xf[:, :, :], xT[s][0][:, :, :]).then_inc(xT_ok, 1)

            dve.wait_ge(b_turned, 1)
            dve.tensor_copy(b1[:, :, :], pb[:, :].rearrange("p (e f) -> p e f", e=E)).then_inc(b_ok, 1)
            dve.sem_inc(y_ok, 2)
            dve.sem_inc(hid_ok, 2)
            for n in range(2):
                weight_low(0, n, 0)
            x_low(0, 0)
            dve.wait_ge(b2_in, 16)

            def step(q, v, j, later):
                e = j * 2 + v // PER
                for f in range(FT):
                    dve.wait_ge(h_high, q * FT + f + 3)
                    low(hid[1][:, f, :], hf[:, f % 2, :], hid[0][:, f, :]).then_inc(hid_ok, 1)
                if later or v < 3:
                    x_low(q + 1, (v + 1) % 2)
                if later or v < 2:
                    weight_low(e + 1, v % 2, 1 - v // PER)
                shift = b2[:, bass.ds(e * D, D)].unsqueeze(1).broadcast_to([P, 2, D])
                for h in range(2):
                    dve.wait_ge(y_done, 2 * q + h + 1)
                    dve.wait_ge(stored[h], 16 * (q + 1))
                    dve.tensor_tensor(yo[:, h, :, :], py[h][:, :, :], shift, ALU.add).then_inc(y_ok, 1)
            walk(dve, step)


def load_gains(nc, ctx, w, ident):
    names = ("ln1_g", "ln1_b", "ln2_g", "ln2_b")
    cols = ctx.enter_context(nc.sbuf_tensor("gain_cols", [P, len(names) * KD], F32))
    with ExitStack() as inner:
        rows = inner.enter_context(nc.sbuf_tensor("gain_rows", [len(names) * KD, P], F32))
        turned = inner.enter_context(nc.psum_tensor("gain_turned", [P, len(names) * KD], F32))
        loaded, turned_ok = (inner.enter_context(nc.semaphore(f"gain_{n}")) for n in ("loaded", "turned_ok"))
        block = inner.enter_context(nc.Block())

        @block.sync
        def _(sp):
            for i, name in enumerate(names):
                sp.dma_start(rows[i * KD:(i + 1) * KD, :], w["L1_ffn_" + name].rearrange("(k p) -> k p", p=P))\
                  .then_inc(loaded, 16)

        @block.tensor
        def _(pe):
            pe.wait_ge(loaded, 16 * len(names))
            pe.transpose(turned[:, :], rows[:, :], ident[0:len(names) * KD, 0:len(names) * KD]).then_inc(turned_ok, 1)

        @block.vector
        def _(dve):
            dve.wait_ge(turned_ok, 1)
            dve.tensor_copy(cols[:, :], turned[:, :])
    cols = [cols[:, i * KD:(i + 1) * KD] for i in range(len(names))]
    return [(cols[0], cols[1]), (cols[2], cols[3])]


def build(nc, w, tables, out):
    with ExitStack() as ctx:
        def sb(name, shape, dt=F32):
            return ctx.enter_context(nc.sbuf_tensor(name, shape, dt))
        ident, zeros = sb("ident", [P, P]), sb("zeros", [P, D])
        flat = w["L0_attn_x"].rearrange("b l d -> (b l) d")
        result = out.rearrange("b l d -> (b l) d")
        rows = nc.dram_tensor("sorted_rows", (ROWS0, D), F32).ap()
        outs = nc.dram_tensor("expert_rows", (ROWS0, D), F32).ap()
        rows1 = nc.dram_tensor("sorted_rows1", (ROWS1, D), F32).ap()
        outs1 = nc.dram_tensor("expert_rows1", (ROWS1, D), F32).ap()
        x_kept2 = nc.dram_tensor("x_kept2", (N, D), F32).ap()
        oT_dram = nc.dram_tensor("oT", (D, N), F32).ap(), nc.dram_tensor("o_sums", (H1, N), F32).ap()
        x_kept = nc.dram_tensor("x_kept", (N, D), F32).ap()
        xT_dram = nc.dram_tensor("xT", (P, KD, N), F32).ap()
        setup_phase(nc, ident, zeros)
        with ExitStack() as s0:
            xn_a = s0.enter_context(nc.sbuf_tensor("xn_a", [P, T, D], F32))
            with ExitStack() as s1:
                x = s1.enter_context(nc.sbuf_tensor("x", [P, T, D], F32))
                y = s1.enter_context(nc.sbuf_tensor("y0", [P, T, D + 1], F32))
                r = make_router(nc, s1, ctx, "r0")
                with ExitStack() as s2:
                    xT = s2.enter_context(nc.sbuf_tensor("xT0", [P, KD, N], F32))
                    norm_phase(nc, "n0", x, ident, x_src=flat, xn=xn_a, xT_sb=xT, zero=(zeros, rows))
                    layer0_attention(nc, w, xn_a, xT, y, ident)
                    norm_phase(nc, "n1", x, ident, y=y, ysum=y[:, :, D], xn=xn_a, xT_sb=xT)
                    route_phase(nc, "r0", w["L0_ffn_gate_w"], True, xT, xn_a, ident, r, rows, None, shared=(w, y))
                layer0_experts(nc, w, r, rows, outs, ident)
                y_stats = s1.enter_context(nc.sbuf_tensor("y_stats0", [P, T, 6], F32))
                combine_phase(nc, "c0", r, outs, y, y_stats)
                norm_phase(nc, "n2", x, ident, y=y, y_stats=y_stats, xn=xn_a, xT_dram=xT_dram, x_save=x_kept)
            clear_phase(nc)
            attention_phase(nc, "a1", True, ident, w=w, xT_dram=xT_dram, y=xn_a)
            gains = load_gains(nc, s0, w, ident)
            with ExitStack() as s1:
                qkv = s1.enter_context(nc.sbuf_tensor("qkv", [P, T, 3 * D], F32))
                with ExitStack() as s2:
                    hT = s2.enter_context(nc.sbuf_tensor("hT", [P, KD, N], F32))
                    with ExitStack() as s3:
                        x = s3.enter_context(nc.sbuf_tensor("x1", [P, T, D], F32))
                        norm_phase(nc, "n3", x, ident, y=xn_a, xn=xn_a, xT_sb=hT, twice=True, gain=gains[0],
                                   x_load=x_kept, x_save=x_kept2)
                    qkv_phase(nc, w, tables, hT, qkv)
                attention_phase(nc, "a2", False, ident, q_src=qkv, oT_dram=oT_dram)
            output_phase(nc, w, oT_dram, xn_a)
            clear_phase(nc)
            with ExitStack() as s1:
                r = make_router(nc, s1, ctx, "r1")
                with ExitStack() as s2:
                    xT = s2.enter_context(nc.sbuf_tensor("xT1", [P, KD, N], F32))
                    h_raw = s2.enter_context(nc.sbuf_tensor("h_raw", [P, T, D], F32))
                    norm_phase(nc, "n4", None, ident, y=xn_a, residual=False, xn=h_raw, xT_sb=xT, gain=gains[1],
                               zero=(zeros, rows1))
                    route_phase(nc, "r1", w["L1_ffn_Wgate"], False, xT, h_raw, ident, r, rows1, CAP)
                layer1_experts(nc, w, gains[1], rows1, outs1, ident)
                x = s1.enter_context(nc.sbuf_tensor("x2", [P, T, D], F32))
                y_stats = s1.enter_context(nc.sbuf_tensor("y_stats1", [P, T, 6], F32))
                combine_phase(nc, "c1", r, outs1, xn_a, y_stats, x=x, x_load=x_kept2)
                norm_phase(nc, "n5", x, ident, y=xn_a, y_stats=y_stats, out_dst=result)


_SHAPES = {
    "L0_attn_x": (B, L, D), "L0_attn_Wq": (D, D), "L0_attn_Wk": (D, D), "L0_attn_Wv": (D, D),
    "L0_attn_proj": (D, PROJ), "L0_ffn_gate_w": (E, D), "L0_ffn_w_gate": (E, D, F0), "L0_ffn_w_up": (E, D, F0),
    "L0_ffn_w_down": (E, F0, D), "L0_ffn_sw_gate": (D, FS), "L0_ffn_sw_up": (D, FS), "L0_ffn_sw_down": (FS, D),
    "L1_attn_Wq": (D, HA * DK), "L1_attn_Wk": (D, HA * DK), "L1_attn_Wv": (D, HA * DK), "L1_attn_Wo": (HA * DK, D),
    "L1_ffn_ln1_g": (D,), "L1_ffn_ln1_b": (D,), "L1_ffn_Wqkv": (D, 3 * D), "L1_ffn_Wproj": (D, D),
    "L1_ffn_ln2_g": (D,), "L1_ffn_ln2_b": (D,), "L1_ffn_Wgate": (D, E), "L1_ffn_W1": (E, D, F1),
    "L1_ffn_b1": (E, F1), "L1_ffn_W2": (E, F1, D), "L1_ffn_b2": (E, D),
}


def kernel(**inputs):
    import concourse.bacc as bacc
    from concourse.bass_utils import run_bass_kernel_spmd

    nc = bacc.Bacc("TRN2", target_bir_lowering=False, num_devices=1)
    arrays = {f"in_{name}": np.ascontiguousarray(inputs[name]) for name in _SHAPES}
    w = {name: nc.dram_tensor(f"in_{name}", shape, F32, kind="ExternalInput").ap() for name, shape in _SHAPES.items()}
    out = nc.dram_tensor("out", (B, L, D), F32, kind="ExternalOutput").ap()
    inv_freq = np.float32(1.0) / np.float32(10000.0) ** (np.arange(0, HD, 2, dtype=np.float32) / np.float32(HD))
    angle = np.arange(L, dtype=np.float32)[:, None] * inv_freq
    arrays["cos"], arrays["sin"] = np.cos(angle), np.sin(angle)
    tables = [nc.dram_tensor(name, (L, HD // 2), F32, kind="ExternalInput").ap() for name in ("cos", "sin")]
    build(nc, w, tables, out)
    return run_bass_kernel_spmd(nc, [arrays], core_ids=[0]).results[0]["out"]
```
